# Optimizing a Trainium2 kernel written in Bass

```python
import numpy as np
import jax
import jax.numpy as jnp

def _softmax(x, axis=-1):
    return jax.nn.softmax(x, axis=axis)

def _gelu(x):
    return jax.nn.gelu(x, approximate=True)

def _silu(x):
    return jax.nn.silu(x)

def _sigmoid(x):
    return jax.nn.sigmoid(x)

def _layernorm(x, axis=-1, eps=1e-05):
    m = jnp.mean(x, axis=axis, keepdims=True)
    v = jnp.var(x, axis=axis, keepdims=True)
    return (x - m) / jnp.sqrt(v + eps)

def _scatter_add(tgt, idx, src, axis=0):
    return tgt.at[idx].add(src)

def _segment_sum(src, seg, n):
    return jax.ops.segment_sum(src, seg, n)
kernel_name = 'mk_gnn_ffn_d1_gnn_r8_351ed9'

def setup_inputs(seed: int=0):
    np.random.seed(seed)
    _w = jnp.asarray

    def _rec_inputs():
        import jax
        import jax.numpy as jnp
        _gk = jax.random.key(seed)
        x = -0.0003713 + 1 * jax.random.normal(jax.random.fold_in(_gk, 1), (6250, 256), jnp.float32)
        _s = jax.random.randint(jax.random.fold_in(_gk, 2), (100000,), 0, 6250, jnp.int32)
        _d = jax.random.randint(jax.random.fold_in(_gk, 3), (100000,), 0, 6250, jnp.int32)
        _loop = jnp.arange(6250, dtype=jnp.int32)
        src = jnp.concatenate([_s, _d, _loop])
        dst = jnp.concatenate([_d, _s, _loop])
        _o = jnp.argsort(dst, stable=True)
        src = src[_o]
        dst = dst[_o]
        return (x, src, dst)
    x, src, dst = _rec_inputs()

    def _L0_gnn_setup():
        import jax, jax.numpy as jnp
        import numpy as np
        N, DEG = (6250, 16)
        E = N * DEG
        IN_DIM, OUT_DIM, HEADS = (256, 64, 4)
        SLOPE = 0.01
        key = jax.random.key(seed)
        k1, k2, k3, k4, k5 = jax.random.split(key, 5)
        h = jax.random.normal(k1, (N, IN_DIM), dtype=jnp.float32)
        W = jax.random.normal(k2, (HEADS, IN_DIM, OUT_DIM), dtype=jnp.float32) * 0.05
        a_src = jax.random.normal(k3, (HEADS, OUT_DIM), dtype=jnp.float32) * 0.05
        a_dst = jax.random.normal(k4, (HEADS, OUT_DIM), dtype=jnp.float32) * 0.05
        src = jax.random.randint(k5, (E,), 0, N, dtype=jnp.int32)
        dst = jnp.repeat(jnp.arange(N, dtype=jnp.int32), DEG)
        return {'h': h, 'W': W, 'a_src': a_src, 'a_dst': a_dst, 'src': src, 'dst': dst}
    _L0_gnn_all = _L0_gnn_setup()
    _L0_gnn_in = {k: v for k, v in _L0_gnn_all.items() if k in ('W', 'a_src', 'a_dst')}
    del _L0_gnn_all

    def _L0_ffn_setup():
        import jax, jax.numpy as jnp
        import numpy as np
        B, S, H, F, E, K = (8, 512, 256, 512, 16, 2)
        EPS = 1e-05
        key = jax.random.key(seed)
        ks = jax.random.split(key, 9)
        sc = 0.02
        return {'x': jax.random.normal(ks[0], (B, S, H), dtype=jnp.float32), 'gate_w': jax.random.normal(ks[1], (H, E), dtype=jnp.float32) * sc, 'gate_b': jnp.zeros((E,), dtype=jnp.float32), 'w1': jax.random.normal(ks[2], (E, H, F), dtype=jnp.float32) * sc, 'b1': jnp.zeros((E, F), dtype=jnp.float32), 'w2': jax.random.normal(ks[3], (E, F, H), dtype=jnp.float32) * sc, 'b2': jnp.zeros((E, H), dtype=jnp.float32), 'gamma': jnp.ones((H,), dtype=jnp.float32), 'beta': jnp.zeros((H,), dtype=jnp.float32)}
    _L0_ffn_all = _L0_ffn_setup()
    _L0_ffn_in = {k: v for k, v in _L0_ffn_all.items() if k in ('gate_w', 'gate_b', 'w1', 'b1', 'w2', 'b2', 'gamma', 'beta')}
    del _L0_ffn_all
    return {'x': x, 'src': src, 'dst': dst, 'L0_gnn_W': _L0_gnn_in['W'], 'L0_gnn_a_src': _L0_gnn_in['a_src'], 'L0_gnn_a_dst': _L0_gnn_in['a_dst'], 'L0_ffn_gate_w': _L0_ffn_in['gate_w'], 'L0_ffn_gate_b': _L0_ffn_in['gate_b'], 'L0_ffn_w1': _L0_ffn_in['w1'], 'L0_ffn_b1': _L0_ffn_in['b1'], 'L0_ffn_w2': _L0_ffn_in['w2'], 'L0_ffn_b2': _L0_ffn_in['b2'], 'L0_ffn_gamma': _L0_ffn_in['gamma'], 'L0_ffn_beta': _L0_ffn_in['beta']}

def reference(x, src, dst, L0_gnn_W, L0_gnn_a_src, L0_gnn_a_dst, L0_ffn_gate_w, L0_ffn_gate_b, L0_ffn_w1, L0_ffn_b1, L0_ffn_w2, L0_ffn_b2, L0_ffn_gamma, L0_ffn_beta):
    import jax
    import jax.numpy as jnp

    def _L0_gnn_ref(h, W, a_src, a_dst, src, dst):
        import jax, jax.numpy as jnp
        import numpy as np
        N, DEG = (6250, 16)
        E = N * DEG
        IN_DIM, OUT_DIM, HEADS = (256, 64, 4)
        SLOPE = 0.01
        z = jnp.einsum('ni,hid->nhd', h, W)
        es = jnp.einsum('nhd,hd->nh', z, a_src)
        ed = jnp.einsum('nhd,hd->nh', z, a_dst)
        e = es[src] + ed[dst]
        e = jnp.where(e >= 0, e, SLOPE * e)
        m = jax.ops.segment_max(e, dst, num_segments=N)
        ex = jnp.exp(e - m[dst])
        denom = jax.ops.segment_sum(ex, dst, num_segments=N)
        alpha = ex / denom[dst]
        msg = alpha[:, :, None] * z[src]
        out = jax.ops.segment_sum(msg, dst, num_segments=N)
        return out.reshape(N, HEADS * OUT_DIM)

    def _L0_ffn_ref(x, gate_w, gate_b, w1, b1, w2, b2, gamma, beta):
        import jax, jax.numpy as jnp
        import numpy as np
        B, S, H, F, E, K = (8, 512, 256, 512, 16, 2)
        EPS = 1e-05
        gate_logits = x @ gate_w + gate_b
        topk_vals, topk_idx = jax.lax.top_k(gate_logits, K)
        topk_w = jax.nn.softmax(topk_vals, axis=-1)
        h = jax.nn.relu(jnp.einsum('bsh,ehf->bsef', x, w1) + b1)
        expert_out = jnp.einsum('bsef,efh->bseh', h, w2) + b2
        sel = jnp.take_along_axis(expert_out, topk_idx[:, :, :, None], axis=2)
        moe = jnp.sum(topk_w[..., None] * sel, axis=2)
        y = x + moe
        mu = jnp.mean(y, axis=-1, keepdims=True)
        var = jnp.var(y, axis=-1, keepdims=True)
        return (y - mu) / jnp.sqrt(var + EPS) * gamma + beta
    x = x + _L0_gnn_ref(_layernorm(x, axis=-1), L0_gnn_W, L0_gnn_a_src, L0_gnn_a_dst, src, dst)
    x = x + _L0_ffn_ref(_layernorm(x, axis=-1)[None], L0_ffn_gate_w, L0_ffn_gate_b, L0_ffn_w1, L0_ffn_b1, L0_ffn_w2, L0_ffn_b2, L0_ffn_gamma, L0_ffn_beta)[0]
    return x

_drawn_inputs = setup_inputs


def setup_inputs(seed=0):
    import zlib

    import numpy as np

    out = dict(_drawn_inputs(seed))
    spreads = {'L0_ffn_gate_b': (0.0, 0.1),
     'L0_ffn_b1': (0.0, 0.709),
     'L0_ffn_b2': (0.0, 0.1),
     'L0_ffn_gamma': (1.0, 0.2),
     'L0_ffn_beta': (0.0, 0.1)}
    factors = {'L0_gnn_a_dst': 3.234}
    for name, (base, spread) in spreads.items():
        noise = np.random.default_rng([zlib.crc32(name.encode()), seed]).standard_normal(out[name].shape)
        drawn = base * np.exp(spread * noise) if base else spread * noise
        out[name] = jnp.asarray(drawn.astype(out[name].dtype))
    for name, factor in factors.items():
        out[name] = (out[name] * factor).astype(out[name].dtype)
    return out
```

```python
from contextlib import ExitStack

import concourse.bass as bass
from concourse import mybir

F32 = mybir.dt.float32
I32 = mybir.dt.int32
ALU = mybir.AluOpType
ACT = mybir.ActivationFunctionType
AX = mybir.AxisListType
RMAX = bass.bass_isa.ReduceOp.max

P = 128
G = 4
RING = 8
SLOPE = 0.01
EPS = 1e-5
LEVEL = 64.0
DECIDED = 1e-28
PASSES_MAX = 4096
FAR = 1e30
TINY = 1e-30
PAD_DST = 1 << 20


def pipeline(eng, count, unroll, head, stages):
    last = max(lag for _, lag in stages)
    head = -(-head // unroll) * unroll
    rounds = (count - head) // unroll

    def peeled(i):
        for stage, lag in stages:
            if 0 <= i - lag < count:
                stage(i - lag, (i - lag) % unroll, (i - lag) // unroll)

    for i in range(head):
        peeled(i)
    with eng.Fori(0, rounds) as r:
        for u in range(unroll):
            for stage, lag in stages:
                at = head + u - lag
                stage(r * unroll + at, at % unroll, r + at // unroll)
    for i in range(head + rounds * unroll, count + last):
        peeled(i)


def early(item, depth):
    return isinstance(item, int) and item < depth


def gnn_moe_kernel(nc, x, src, dst, W, a_src, a_dst, gate_w, gate_b, w1, b1, w2, b2, gamma, beta, out):
    N, D = x.shape
    E = src.shape[0]
    HEADS, _, DH = W.shape
    EXPERTS, _, F = w1.shape
    TOP = 2
    NT = -(-N // P)
    REST = N - (NT - 1) * P
    KD = D // P
    FC = F // P
    ROW = D + HEADS
    CHUNKS = -(-E // P)
    GROUPS = -(-CHUNKS // G)
    assert GROUPS * G * P > E
    FULL = E // (G * P)
    VISITS = FULL + NT
    BLOCKS = -(-CHUNKS // P)
    FULL_CHUNKS = E // P
    TILES = (N * TOP + EXPERTS * (P - 1)) // P
    NE = NT * EXPERTS

    z_table = nc.dram_tensor("z_table", [NT * P, ROW], F32).ap()
    slot_rows = nc.dram_tensor("slot_rows", [TILES * P, D], F32).ap()
    expert_rows = nc.dram_tensor("expert_rows", [TILES * P, D], F32).ap()

    whole = ExitStack()

    def sem(name):
        return whole.enter_context(nc.semaphore(name))

    def sb(ctx, name, shape, dt=F32):
        return ctx.enter_context(nc.sbuf_tensor(name, shape, dt))

    def ps(ctx, name, shape=(P, 512)):
        return ctx.enter_context(nc.psum_tensor(name, list(shape), F32))

    def over(ap, shape):
        return ap.to_broadcast(shape)

    with whole:
        xs = sb(whole, "xs", [P, NT, D])
        acc = sb(whole, "acc", [P, NT, ROW])
        ident = sb(whole, "ident", [P, P])
        ones = sb(whole, "ones", [P, P])
        iota_p = sb(whole, "iota_p", [P, 1])
        iota_f = sb(whole, "iota_f", [P, 512])
        rows_bc = sb(whole, "rows_bc", [P, 4 * D + EXPERTS])
        stats = sb(whole, "stats", [P, NT, 6])
        mean = sb(whole, "mean", [P, NT])
        rstd = sb(whole, "rstd", [P, NT])
        ln_tmp = sb(whole, "ln_tmp", [P, 2, NT])
        eps_col = sb(whole, "eps_col", [P, 1])
        src_idx = sb(whole, "src_idx", [P, BLOCKS * P], I32)
        dst_col = sb(whole, "dst_col", [P, BLOCKS * P])
        esed = sb(whole, "esed", [P, NT, 2 * HEADS])
        visit_base = sb(whole, "visit_base", [P, VISITS])
        visit_tile = sb(whole, "visit_tile", [1, VISITS], I32)
        visit_group = sb(whole, "visit_group", [1, VISITS], I32)
        visit_slot = sb(whole, "visit_slot", [1, VISITS], I32)
        group_free = sb(whole, "group_free", [1, GROUPS], I32)

        def bulk_rstd(step, ready):
            a, b = ln_tmp[:, 0, :], ln_tmp[:, 1, :]
            step(nc.vector.tensor_tensor(mean[:, :], stats[:, :, 1], stats[:, :, 4], ALU.add))
            step(nc.vector.tensor_scalar(mean[:, :], mean[:, :], 0.5, None, ALU.mult))
            step(nc.vector.tensor_tensor(a, stats[:, :, 1], mean[:, :], ALU.subtract))
            step(nc.vector.tensor_tensor(a, a, a, ALU.mult))
            step(nc.vector.tensor_tensor(b, stats[:, :, 2], stats[:, :, 5], ALU.add))
            nc.vector.scalar_tensor_tensor(out=a, in0=b, scalar=1.0 / D, in1=a, op0=ALU.mult, op1=ALU.add).then_inc(ready, 1)

        def stepper(eng, semaphore):
            count = [0]

            def step(instruction):
                count[0] += 1
                instruction.then_inc(semaphore, 1)
                eng.wait_ge(semaphore, count[0])
            return step

        a_const = sem("a_const"); a_identz = sem("a_identz"); a_padded = sem("a_padded")
        a_x = [sem(f"a_x{i}") for i in range(2)]
        a_edges = sem("a_edges"); a_w = sem("a_w"); a_rows = sem("a_rows"); a_last = sem("a_last")
        a_vstep = sem("a_vstep"); a_rows_ps = sem("a_rows_ps"); a_rows_sb = sem("a_rows_sb")
        a_edge_f = sem("a_edge_f"); a_edge_ps = sem("a_edge_ps"); a_edge_sb = sem("a_edge_sb")
        a_last_f = sem("a_last_f"); a_last_ps = sem("a_last_ps"); a_ge = sem("a_ge"); a_cnt = sem("a_cnt")
        a_stats = sem("a_stats"); a_var = sem("a_var"); a_root = sem("a_root"); a_waug = sem("a_waug")
        a_xn = sem("a_xn"); a_xT_ps = sem("a_xT_ps"); a_xT = sem("a_xT"); a_z_ps = sem("a_z_ps")
        a_z = sem("a_z"); a_store = [sem(f"a_store{i}") for i in range(2)]
        with ExitStack() as ctx:
            src_raw = sb(ctx, "src_raw", [P, BLOCKS, P], I32)
            dst_raw = sb(ctx, "dst_raw", [P, BLOCKS, P], I32)
            edge_f = sb(ctx, "edge_f", [P, 2, BLOCKS, P])
            wcat = sb(ctx, "wcat", [P, KD, D + 2 * HEADS])
            wprod = sb(ctx, "wprod", [P, D])
            rows = sb(ctx, "rows", [1, 4 * D + EXPERTS])
            last_i = sb(ctx, "last_i", [1, FULL], I32)
            last_f = sb(ctx, "last_f", [1, FULL])
            iota_i = sb(ctx, "iota_i", [P, 512], I32)
            iota_pi = sb(ctx, "iota_pi", [P, 1], I32)
            below = sb(ctx, "below", [P, 3, 512])
            thr = sb(ctx, "thr", [P, 4])
            xn = sb(ctx, "xn", [P, 2, D])
            xnT = sb(ctx, "xnT", [P, 2, D])
            z_out = sb(ctx, "z_out", [P, 2, ROW])
            psA = [ps(ctx, f"psA{i}") for i in range(4)]
            psT = [ps(ctx, f"psTa{i}") for i in range(2)]
            psZ = [ps(ctx, f"psZa{i}") for i in range(2)]
            block = ctx.enter_context(nc.Block())
            EB = [(k, b) for k in range(2) for b in range(0, BLOCKS, 4)]

            @block.sync
            def _(sp):
                half = (NT - 1) // 2
                sp.dma_start(xs[:, 0:half, :], x[0:half * P].rearrange("(t p) c -> p t c", p=P)).then_inc(a_x[0], 16)
                sp.dma_start(xs[:, half:NT - 1, :], x[half * P:(NT - 1) * P].rearrange("(t p) c -> p t c", p=P)).then_inc(a_x[0], 16)
                for c in range(KD):
                    sp.dma_start(wcat[:, c, 0:D].rearrange("p (h d) -> p h d", h=HEADS),
                                 W[:, c * P:(c + 1) * P, :].rearrange("h p d -> p h d")).then_inc(a_w, 16)
                sp.wait_ge(a_padded, 1)
                sp.dma_start(xs[0:REST, NT - 1, :], x[(NT - 1) * P:N]).then_inc(a_x[1], 16)

                def store(t, s, r):
                    sp.wait_ge(a_z, t + 1)
                    sp.dma_start(z_table[bass.ds(t * P, P), :], z_out[:, s, :]).then_inc(a_store[s], 16)
                pipeline(sp, NT, 2, 2, [(store, 0)])
                for s in range(2):
                    sp.wait_ge(a_store[s], 16 * len(range(s, NT, 2)))

            @block.scalar
            def _(act):
                for i, r in enumerate((a_src, a_dst)):
                    act.dma_start(rows[0:1, i * D:(i + 1) * D], r.rearrange("h d -> (h d)").unsqueeze(0)).then_inc(a_rows, 16)
                for i, r in enumerate((gamma, beta)):
                    act.dma_start(rows[0:1, (2 + i) * D:(3 + i) * D], r.unsqueeze(0)).then_inc(a_rows, 16)
                act.dma_start(rows[0:1, 4 * D:], gate_b.unsqueeze(0)).then_inc(a_rows, 16)
                act.wait_ge(a_padded, 3)
                tail = BLOCKS - 1
                for raw, e in ((src_raw, src), (dst_raw, dst)):
                    act.dma_start(raw[:, 0:tail, :], e[0:tail * P * P].rearrange("(b p f) -> p b f", p=P, f=P)).then_inc(a_edges, 16)
                    n = FULL_CHUNKS - tail * P
                    act.dma_start(raw[0:n, tail, :], e[tail * P * P:FULL_CHUNKS * P].rearrange("(p f) -> p f", f=P)).then_inc(a_edges, 16)
                    if E > FULL_CHUNKS * P:
                        act.dma_start(raw[n:n + 1, tail, 0:E - FULL_CHUNKS * P],
                                      e[FULL_CHUNKS * P:E].unsqueeze(0)).then_inc(a_edges, 16)
                with nc.allow_non_contiguous_dma("the last destination of each group"):
                    act.dma_start(last_i[:, :], dst[0:FULL * G * P].rearrange("(g f) -> g f", f=G * P)[:, G * P - 1:G * P]
                                  .rearrange("g o -> o g")).then_inc(a_last, 16)
                act.wait_ge(a_var, 1)
                nc.scalar.activation(rstd[:, :], ln_tmp[:, 0, :], ACT.Sqrt, bias=eps_col[:, 0:1]).then_inc(a_root, 1)

                def copy_xT(t, s, r):
                    act.wait_ge(a_xT_ps, t + 1)
                    if not early(t, 2):
                        act.wait_ge(a_z_ps, t - 1)
                    nc.scalar.copy(xnT[:, s, :], psT[s][:, 0:D]).then_inc(a_xT, 1)

                def copy_z(t, s, r):
                    act.wait_ge(a_z_ps, t + 1)
                    if not early(t, 2):
                        act.wait_ge(a_store[s], 16 * r)
                    nc.scalar.copy(z_out[:, s, :], psZ[s][:, 0:ROW])
                    nc.scalar.copy(esed[:, bass.ds(t, 1), :].rearrange("p o c -> p (o c)"),
                                   psZ[s][:, D:D + 2 * HEADS]).then_inc(a_z, 1)
                pipeline(act, NT, 2, 3, [(copy_xT, 0), (copy_z, 1)])

            @block.gpsimd
            def _(pool):
                nc.gpsimd.memset(xs[:, NT - 1, :], 0.0).then_inc(a_padded, 1)
                nc.gpsimd.memset(src_raw[:, BLOCKS - 1, :], 0).then_inc(a_padded, 1)
                nc.gpsimd.memset(dst_raw[:, BLOCKS - 1, :], PAD_DST).then_inc(a_padded, 1)
                nc.gpsimd.memset(ident[:, :], 0.0).then_inc(a_identz, 1)
                nc.gpsimd.memset(ones[:, :], 1.0).then_inc(a_const, 1)
                nc.gpsimd.memset(eps_col[:, :], EPS).then_inc(a_const, 1)
                nc.gpsimd.iota(iota_i[:, :], [[1, 512]], base=0, channel_multiplier=0).then_inc(a_const, 1)
                nc.gpsimd.iota(iota_pi[:, :], [[1, 1]], base=0, channel_multiplier=1).then_inc(a_const, 1)
                pool.wait_ge(a_identz, 1)
                nc.gpsimd.affine_select(out=ident[:, :], in_=ident[:, :], compare_op=ALU.not_equal, fill=1.0,
                                        base=0, pattern=[[-1, P]], channel_multiplier=1).then_inc(a_const, 1)

            @block.vector
            def _(dve):
                step = stepper(dve, a_vstep)
                dve.wait_ge(a_const, 5)
                step(nc.vector.tensor_copy(iota_f[:, :], iota_i[:, :]))
                step(nc.vector.tensor_copy(iota_p[:, :], iota_pi[:, :]))
                dve.wait_ge(a_rows_ps, 3)
                for i, (lo, hi) in enumerate(((0, 2 * D), (2 * D, 4 * D), (4 * D, 4 * D + EXPERTS))):
                    nc.vector.tensor_copy(rows_bc[:, lo:hi], psA[i][:, 0:hi - lo]).then_inc(a_rows_sb, 1)
                dve.wait_ge(a_w, 16 * KD)
                dve.wait_ge(a_rows_sb, 3)
                for c in range(KD):
                    for k in range(2):
                        step(nc.vector.tensor_tensor(wprod[:, :], wcat[:, c, 0:D], rows_bc[:, k * D:(k + 1) * D], ALU.mult))
                        step(nc.vector.tensor_reduce(wcat[:, c, D + k * HEADS:D + (k + 1) * HEADS],
                                                     wprod[:, :].rearrange("p (h d) -> p h d", h=HEADS), AX.X, ALU.add))
                dve.wait_ge(a_x[0], 32)
                dve.wait_ge(a_x[1], 16)

                def tile_stats(t, s, r):
                    nc.vector.bn_stats(stats[:, bass.ds(t, 1), :].rearrange("p o s -> p (o s)"),
                                       xs[:, bass.ds(t, 1), :].rearrange("p o c -> p (o c)")).then_inc(a_stats, 1)
                pipeline(dve, NT, 8, 1, [(tile_stats, 0)])
                dve.wait_ge(a_stats, NT)
                bulk_rstd(step, a_var)
                dve.wait_ge(a_root, 1)
                step(nc.vector.reciprocal(rstd[:, :], rstd[:, :]))

                def norm(t, s, r):
                    if not early(t, 2):
                        dve.wait_ge(a_xT_ps, t - 1)
                    nc.vector.tensor_scalar(xn[:, s, :], xs[:, bass.ds(t, 1), :].rearrange("p o c -> p (o c)"),
                                            mean[:, bass.ds(t, 1)], rstd[:, bass.ds(t, 1)],
                                            ALU.subtract, ALU.mult).then_inc(a_xn, 1)
                pipeline(dve, NT, 2, 2, [(norm, 0)])

                dve.wait_ge(a_edges, 16 * (6 if E > FULL_CHUNKS * P else 4))
                for k, raw in enumerate((src_raw, dst_raw)):
                    nc.vector.tensor_copy(edge_f[:, k, :, :], raw[:, :, :]).then_inc(a_edge_f, 1)
                for n, (k, b) in enumerate(EB):
                    m = min(4, BLOCKS - b)
                    dve.wait_ge(a_edge_ps, n + 1)
                    to = (src_idx, dst_col)[k]
                    nc.vector.tensor_copy(to[:, b * P:(b + m) * P], psA[n % 4][:, 0:m * P]).then_inc(a_edge_sb, 1)
                dve.wait_ge(a_last, 16)
                nc.vector.tensor_copy(last_f[:, :], last_i[:, :]).then_inc(a_last_f, 1)
                step(nc.vector.tensor_scalar(thr[:, 0:1], iota_p[:, :], float(P), float(P), ALU.mult, ALU.add))
                dve.wait_ge(a_last_ps, 1)
                step(nc.vector.tensor_scalar(below[:, 2, 0:FULL], psT[0][:, 0:FULL], thr[:, 0:1], None, ALU.is_lt))
                step(nc.vector.tensor_reduce(thr[:, 1:2], below[:, 2, 0:FULL], AX.X, ALU.add))
                step(nc.vector.scalar_tensor_tensor(out=thr[:, 2:3], in0=iota_p[:, :], scalar=1.0, in1=thr[:, 1:2], op0=ALU.add, op1=ALU.add))
                nc.vector.tensor_scalar(below[:, 0, 0:VISITS], iota_f[:, 0:VISITS], thr[:, 2:3], None, ALU.is_ge).then_inc(a_ge, 1)
                nc.vector.tensor_scalar(below[:, 1, 0:GROUPS], iota_f[:, 0:GROUPS], thr[:, 1:2], None, ALU.is_gt).then_inc(a_ge, 1)
                dve.wait_ge(a_cnt, 2)
                step(nc.vector.tensor_scalar(visit_base[:, :], psT[0][:, 0:VISITS], float(P), None, ALU.mult))
                step(nc.vector.tensor_copy(visit_tile[:, :], psT[0][0:1, 0:VISITS]))
                step(nc.vector.scalar_tensor_tensor(out=visit_group[:, :], in0=psT[0][0:1, 0:VISITS], scalar=-1.0,
                                                    in1=iota_f[0:1, 0:VISITS], op0=ALU.mult, op1=ALU.add))
                step(nc.vector.tensor_scalar(visit_slot[:, :], visit_group[:, :], RING - 1, None, ALU.bitwise_and))
                step(nc.vector.memset(group_free[:, 0:RING], 0))
                step(nc.vector.tensor_tensor(group_free[:, RING - 1:GROUPS], psT[1][0:1, 0:GROUPS - RING + 1],
                                             iota_f[0:1, 0:GROUPS - RING + 1], ALU.add))

            @block.tensor
            def _(pe):
                pe.wait_ge(a_const, 5)
                pe.wait_ge(a_rows, 16 * 5)
                for i, (lo, hi) in enumerate(((0, 2 * D), (2 * D, 4 * D), (4 * D, 4 * D + EXPERTS))):
                    nc.tensor.matmul(psA[i][:, 0:hi - lo], ones[0:1, :], rows[0:1, lo:hi], start=True, stop=True).then_inc(a_rows_ps, 1)

                def transpose(t, s, r):
                    pe.wait_ge(a_xn, t + 1)
                    if not early(t, 2):
                        pe.wait_ge(a_xT, t - 1)
                    for c in range(KD):
                        last = nc.tensor.transpose(psT[s][:, c * P:(c + 1) * P], xn[:, s, c * P:(c + 1) * P], ident[:, :])
                    last.then_inc(a_xT_ps, 1)

                def project(t, s, r):
                    pe.wait_ge(a_xT, t + 1)
                    if not early(t, 2):
                        pe.wait_ge(a_z, t - 1)
                    for c in range(KD):
                        last = nc.tensor.matmul(psZ[s][:, 0:D + 2 * HEADS], xnT[:, s, c * P:(c + 1) * P], wcat[:, c, :],
                                                start=c == 0, stop=c == KD - 1)
                    last.then_inc(a_z_ps, 1)
                pipeline(pe, NT, 2, 3, [(transpose, 0), (project, 1)])
                pe.wait_ge(a_edge_f, 2)
                pe.wait_ge(a_rows_sb, 3)
                for n, (k, b) in enumerate(EB):
                    if n >= 4:
                        pe.wait_ge(a_edge_sb, n - 3)
                    for j in range(min(4, BLOCKS - b)):
                        last = nc.tensor.transpose(psA[n % 4][:, j * P:(j + 1) * P], edge_f[:, k, b + j, :], ident[:, :])
                    last.then_inc(a_edge_ps, 1)
                pe.wait_ge(a_last_f, 1)
                pe.wait_ge(a_xT, NT)
                nc.tensor.matmul(psT[0][:, 0:FULL], ones[0:1, :], last_f[0:1, :], start=True, stop=True).then_inc(a_last_ps, 1)
                pe.wait_ge(a_ge, 2)
                nc.tensor.matmul(psT[0][:, 0:VISITS], ones[0:NT, :], below[0:NT, 0, 0:VISITS], start=True, stop=True).then_inc(a_cnt, 1)
                nc.tensor.matmul(psT[1][:, 0:GROUPS], ones[0:NT, :], below[0:NT, 1, 0:GROUPS], start=True, stop=True).then_inc(a_cnt, 1)

        b_zero = sem("b_zero"); b_fill = sem("b_fill"); b_vstep = sem("b_vstep")
        b_spread = sem("b_spread"); b_all = sem("b_all"); b_passes = sem("b_passes")
        b_pstep = sem("b_pstep"); b_nodes = sem("b_nodes")
        b_idx = sem("b_idx"); b_landed = [sem(f"b_landed{i}") for i in range(RING)]
        b_group = sem("b_group"); b_apart = sem("b_apart")
        b_loc = sem("b_loc"); b_S = sem("b_S"); b_ST_ps = sem("b_ST_ps"); b_ST = sem("b_ST")
        b_dest = sem("b_dest"); b_estep = sem("b_estep"); b_arg = sem("b_arg"); b_p = sem("b_p")
        b_msg = sem("b_msg"); b_sum = sem("b_sum"); b_acc = sem("b_acc")
        SH = 2 * HEADS
        SR = 8
        with ExitStack() as ctx:
            nodes = sb(ctx, "nodes", [P, NT, SH])
            level = sb(ctx, "level", [P, HEADS])
            spread = sb(ctx, "spread", [P, 2 * SH])
            spread_all = sb(ctx, "spread_all", [P, SH])
            npass_f = sb(ctx, "npass_f", [P, 2])
            npass_i = sb(ctx, "npass_i", [P, 1], I32)
            decided = sb(ctx, "decided", [P, NT, HEADS])
            pass_tmp = sb(ctx, "pass_tmp", [P, NT, HEADS])
            zeros = sb(ctx, "zeros", [P, D])
            idx_ring = sb(ctx, "idx_ring", [P, RING, G], I32)
            ring = sb(ctx, "ring", [P, RING, G, ROW])
            loc = sb(ctx, "loc", [P, SR, G])
            S = sb(ctx, "S", [P, SR, G, P])
            ST = sb(ctx, "ST", [P, 2, G * P])
            earg = sb(ctx, "earg", [P, 4, 3, G * HEADS])
            msg = sb(ctx, "msg", [P, 4, G, ROW])
            psT = [ps(ctx, f"psTb{i}") for i in range(2)]
            psE = [ps(ctx, f"psEb{i}") for i in range(2)]
            psM = [ps(ctx, f"psMb{i}") for i in range(2)]
            block = ctx.enter_context(nc.Block())

            @block.sync
            def _(sp):
                sp.wait_ge(b_zero, 1)
                sp.dma_start(slot_rows.rearrange("(j p) c -> p j c", p=P),
                             over(zeros[:, :].unsqueeze(1), [P, TILES, D])).then_inc(b_fill, 16)
                sp.wait_ge(b_passes, 1)
                npass = sp.value_load(npass_i[0:1, 0:1], min_val=1, max_val=PASSES_MAX)
                with sp.Fori(0, npass) as k:
                    def relay(g, s, r):
                        sp.wait_ge(b_landed[s], 16 * G * (k * len(range(s, GROUPS, RING)) + r + 1))
                        sp.nop().then_inc(b_group, 1)
                    pipeline(sp, GROUPS, RING, 0, [(relay, 0)])
                sp.wait_ge(b_fill, 16)

            @block.gpsimd
            def _(pool):
                nc.gpsimd.memset(zeros[:, :], 0.0).then_inc(b_zero, 1)
                pool.wait_ge(b_spread, 1)
                nc.gpsimd.partition_all_reduce(spread_all[:, :], spread[:, 0:SH], P, RMAX).then_inc(b_all, 1)
                pool.wait_ge(b_passes, 1)
                npass = pool.value_load(npass_i[0:1, 0:1], min_val=1, max_val=PASSES_MAX)
                with pool.Fori(0, npass) as k:
                    def fetch_idx(g, s, r):
                        done = pool.value_load(group_free[0:1, bass.ds(g, 1)], min_val=0, max_val=VISITS)
                        pool.wait_ge(b_msg, k * VISITS + done + 1)
                        pool.sem_inc(b_apart, 1)
                        nc.gpsimd.tensor_copy(idx_ring[:, s, :], src_idx[:, bass.ds(g * G, G)]).then_inc(b_idx, 1)

                    def gather(g, s, r):
                        pool.wait_ge(b_idx, k * GROUPS + g + 1)
                        pool.sem_inc(b_apart, 1)
                        for c in range(G):
                            nc.gpsimd.indirect_dma_start(ring[:, s, c, :], None, z_table,
                                                         bass.IndirectOffsetOnAxis(ap=idx_ring[:, s, c:c + 1], axis=0)
                                                         ).then_inc(b_landed[s], 16)
                    pipeline(pool, GROUPS, RING, 1, [(fetch_idx, 0), (gather, 1)])

            @block.vector
            def _(dve):
                step = stepper(dve, b_vstep)
                step(nc.vector.tensor_reduce(spread[:, 0:HEADS], esed[:, :, 0:HEADS].rearrange("p t h -> p h t"), AX.X, ALU.max))
                step(nc.vector.tensor_reduce(spread[:, SH:SH + HEADS], esed[:, :, 0:HEADS].rearrange("p t h -> p h t"), AX.X, ALU.min))
                nc.vector.tensor_scalar(spread[:, HEADS:SH], spread[:, SH:SH + HEADS], -1.0, None, ALU.mult).then_inc(b_spread, 1)
                nc.vector.memset(acc[:, :, :], 0.0).then_inc(b_msg, 1)
                step(nc.vector.tensor_copy(nodes[:, :, 0:HEADS], esed[:, :, HEADS:SH]))
                dve.wait_ge(b_all, 1)
                step(nc.vector.tensor_copy(level[:, :], spread_all[:, 0:HEADS]))
                step(nc.vector.tensor_tensor(spread[:, SH + HEADS:2 * SH], spread_all[:, 0:HEADS], spread_all[:, HEADS:SH], ALU.add))
                step(nc.vector.tensor_reduce(npass_f[:, 0:1], spread[:, SH + HEADS:2 * SH], AX.X, ALU.max))
                step(nc.vector.tensor_scalar(npass_f[:, 1:2], npass_f[:, 0:1], 1.0 / LEVEL, 1.0, ALU.mult, ALU.add))
                nc.vector.tensor_scalar(npass_i[:, :], npass_f[:, 1:2], float(PASSES_MAX), None, ALU.min).then_inc(b_passes, 1)
                dve.wait_ge(b_passes, 1)
                npass = dve.value_load(npass_i[0:1, 0:1], min_val=1, max_val=PASSES_MAX)
                with dve.Fori(0, npass) as k:
                    PASS_STEPS = 5
                    made = [0]

                    def pass_step(instruction):
                        made[0] += 1
                        instruction.then_inc(b_pstep, 1)
                        dve.wait_ge(b_pstep, k * PASS_STEPS + made[0])
                    den = acc[:, :, D:ROW]
                    pass_step(nc.vector.tensor_scalar(decided[:, :, :], den, DECIDED, None, ALU.is_ge))
                    pass_step(nc.vector.tensor_tensor(pass_tmp[:, :, :], esed[:, :, HEADS:SH],
                                                      over(level[:, :].unsqueeze(1), [P, NT, HEADS]), ALU.add))
                    pass_step(nc.vector.scalar_tensor_tensor(out=pass_tmp[:, :, :], in0=pass_tmp[:, :, :], scalar=SLOPE,
                                                             in1=pass_tmp[:, :, :], op0=ALU.mult, op1=ALU.max))
                    pass_step(nc.vector.scalar_tensor_tensor(out=nodes[:, :, HEADS:SH], in0=decided[:, :, :], scalar=FAR,
                                                             in1=pass_tmp[:, :, :], op0=ALU.mult, op1=ALU.add))
                    pass_step(nc.vector.tensor_scalar(level[:, :], level[:, :], LEVEL, None, ALU.subtract))
                    for h in range(HEADS):
                        nc.vector.tensor_tensor(acc[:, :, h * DH:(h + 1) * DH], acc[:, :, h * DH:(h + 1) * DH],
                                                       over(decided[:, :, h:h + 1], [P, NT, DH]), ALU.mult)
                    assert made[0] == PASS_STEPS
                    nc.vector.tensor_tensor(den, den, decided[:, :, :], ALU.mult).then_inc(b_nodes, 1)
                    dve.wait_ge(b_nodes, k + 1)
                    dve.sem_inc(b_apart, 1)
                    base = k * VISITS

                    def locate(v, s, r):
                        group = dve.value_load(visit_group[0:1, bass.ds(v, 1)], min_val=0, max_val=GROUPS - 1)
                        nc.vector.tensor_scalar(loc[:, s, :], dst_col[:, bass.ds(group * G, G)],
                                                visit_base[:, bass.ds(v, 1)], None, ALU.subtract).then_inc(b_loc, 1)

                    def one_hot(v, s, r):
                        dve.wait_ge(b_loc, base + v + 1)
                        if not early(v, SR):
                            dve.wait_ge(b_sum, base + v - SR + 1)
                        nc.vector.tensor_tensor(S[:, s, :, :], over(iota_f[:, 0:P].unsqueeze(1), [P, G, P]),
                                                over(loc[:, s, :].unsqueeze(2), [P, G, P]), ALU.is_equal).then_inc(b_S, 1)

                    def e_add(v, s, r):
                        group = dve.value_load(visit_group[0:1, bass.ds(v, 1)], min_val=0, max_val=GROUPS - 1)
                        slot = dve.value_load(visit_slot[0:1, bass.ds(v, 1)], min_val=0, max_val=RING - 1)
                        dve.wait_ge(b_dest, base + v + 1)
                        dve.wait_ge(b_group, k * GROUPS + group + 1)
                        dest = psE[s % 2][:, 0:G * SH].rearrange("p (g c) -> p g c", g=G)
                        nc.vector.tensor_tensor(earg[:, s % 4, 0, :].rearrange("p (g h) -> p g h", g=G),
                                                ring[:, bass.ds(slot, 1), :, D:ROW].rearrange("p o g h -> p (o g) h"),
                                                dest[:, :, 0:HEADS], ALU.add).then_inc(b_estep, 1)

                    def e_lrelu(v, s, r):
                        dve.wait_ge(b_estep, 3 * base + 3 * v + 1)
                        nc.vector.scalar_tensor_tensor(out=earg[:, s % 4, 1, :], in0=earg[:, s % 4, 0, :], scalar=SLOPE,
                                                       in1=earg[:, s % 4, 0, :], op0=ALU.mult, op1=ALU.max).then_inc(b_estep, 1)

                    def e_shift(v, s, r):
                        dve.wait_ge(b_estep, 3 * base + 3 * v + 2)
                        dest = psE[s % 2][:, 0:G * SH].rearrange("p (g c) -> p g c", g=G)
                        nc.vector.tensor_tensor(earg[:, s % 4, 2, :].rearrange("p (g h) -> p g h", g=G),
                                                earg[:, s % 4, 1, :].rearrange("p (g h) -> p g h", g=G),
                                                dest[:, :, HEADS:SH], ALU.subtract).then_inc(b_estep, 1)

                    def e_clamp(v, s, r):
                        dve.wait_ge(b_estep, 3 * base + 3 * v + 3)
                        nc.vector.tensor_scalar(earg[:, s % 4, 0, :], earg[:, s % 4, 2, :], 0.0, None, ALU.min).then_inc(b_arg, 1)

                    def message(v, s, r):
                        slot = dve.value_load(visit_slot[0:1, bass.ds(v, 1)], min_val=0, max_val=RING - 1)
                        dve.wait_ge(b_p, base + v + 1)
                        nc.vector.tensor_tensor(msg[:, s % 4, :, 0:D].rearrange("p g (h d) -> p g h d", h=HEADS),
                                                ring[:, bass.ds(slot, 1), :, 0:D].rearrange("p o g (h d) -> p (o g) h d", h=HEADS),
                                                over(msg[:, s % 4, :, D:ROW].unsqueeze(3), [P, G, HEADS, DH]), ALU.mult).then_inc(b_msg, 1)

                    def accumulate(v, s, r):
                        tile = dve.value_load(visit_tile[0:1, bass.ds(v, 1)], min_val=0, max_val=NT - 1)
                        dve.wait_ge(b_sum, base + v + 1)
                        if not early(v, 1):
                            dve.wait_ge(b_acc, base + v)
                        at = acc[:, bass.ds(tile, 1), :].rearrange("p o c -> p (o c)")
                        nc.vector.tensor_tensor(at, at, psM[s % 2][:, 0:ROW], ALU.add).then_inc(b_acc, 1)
                    pipeline(dve, VISITS, SR, SR, [(locate, 0), (e_add, 2), (one_hot, 0), (e_lrelu, 2), (accumulate, 5),
                                                   (e_shift, 2), (message, 3), (e_clamp, 2)])
                    dve.wait_ge(b_acc, base + VISITS)

            @block.scalar
            def _(act):
                act.wait_ge(b_passes, 1)
                npass = act.value_load(npass_i[0:1, 0:1], min_val=1, max_val=PASSES_MAX)
                with act.Fori(0, npass) as k:
                    base = k * VISITS

                    def copy_ST(v, s, r):
                        act.wait_ge(b_ST_ps, base + v + 1)
                        if not early(v, 2):
                            act.wait_ge(b_dest, base + v - 1)
                        nc.scalar.copy(ST[:, s % 2, :], psT[s % 2][:, 0:G * P]).then_inc(b_ST, 1)

                    def exponent(v, s, r):
                        act.wait_ge(b_arg, base + v + 1)
                        if not early(v, 4):
                            act.wait_ge(b_sum, base + v - 3)
                        nc.scalar.activation(msg[:, s % 4, :, D:ROW], earg[:, s % 4, 0, :].rearrange("p (g h) -> p g h", g=G),
                                             ACT.Exp).then_inc(b_p, 1)
                    pipeline(act, VISITS, SR, 5, [(copy_ST, 0), (exponent, 2)])

            @block.tensor
            def _(pe):
                pe.wait_ge(b_passes, 1)
                npass = pe.value_load(npass_i[0:1, 0:1], min_val=1, max_val=PASSES_MAX)
                with pe.Fori(0, npass) as k:
                    base = k * VISITS
                    pe.wait_ge(b_nodes, k + 1)

                    def transpose(v, s, r):
                        pe.wait_ge(b_S, base + v + 1)
                        if not early(v, 2):
                            pe.wait_ge(b_ST, base + v - 1)
                        for c in range(G):
                            last = nc.tensor.transpose(psT[s % 2][:, c * P:(c + 1) * P], S[:, s, c, :], ident[:, :])
                        last.then_inc(b_ST_ps, 1)

                    def destination(v, s, r):
                        tile = pe.value_load(visit_tile[0:1, bass.ds(v, 1)], min_val=0, max_val=NT - 1)
                        pe.wait_ge(b_ST, base + v + 1)
                        if not early(v, 2):
                            pe.wait_ge(b_arg, base + v - 1)
                        for c in range(G):
                            last = nc.tensor.matmul(psE[s % 2][:, c * SH:(c + 1) * SH], ST[:, s % 2, c * P:(c + 1) * P],
                                                    nodes[:, bass.ds(tile, 1), :].rearrange("p o c -> p (o c)"),
                                                    start=True, stop=True)
                        last.then_inc(b_dest, 1)

                    def weigh(v, s, r):
                        pe.wait_ge(b_msg, base + v + 2)
                        if not early(v, 2):
                            pe.wait_ge(b_acc, base + v - 1)
                        for c in range(G):
                            last = nc.tensor.matmul(psM[s % 2][:, 0:ROW], S[:, s, c, :], msg[:, s % 4, c, :],
                                                    start=c == 0, stop=c == G - 1)
                        last.then_inc(b_sum, 1)
                    pipeline(pe, VISITS, SR, 5, [(transpose, 0), (destination, 1), (weigh, 3)])

        c_vstep = sem("c_vstep"); c_lstep = sem("c_lstep"); c_stats = sem("c_stats"); c_var = sem("c_var")
        c_root = sem("c_root"); c_gate = sem("c_gate"); c_xn = sem("c_xn"); c_xT_ps = sem("c_xT_ps")
        c_xT = sem("c_xT"); c_log_ps = sem("c_log_ps"); c_log = sem("c_log"); c_gap = sem("c_gap")
        c_exp = sem("c_exp"); c_strict = sem("c_strict"); c_taken = sem("c_taken"); c_rank = sem("c_rank")
        c_slots = sem("c_slots"); c_sent = sem("c_sent"); c_b1 = sem("c_b1"); c_b1_ps = sem("c_b1_ps")
        c_iota = sem("c_iota"); c_b2 = sem("c_b2"); c_valid = sem("c_valid")
        slot_of = sb(whole, "slot_of", [P, TOP, NT], I32)
        share = sb(whole, "share", [P, TOP, NT])
        dense = sb(whole, "dense", [P, NT, EXPERTS])
        tile_expert = sb(whole, "tile_expert", [1, TILES], I32)
        b1T = sb(whole, "b1T", [P, EXPERTS, FC])
        b2_sb = sb(whole, "b2_sb", [EXPERTS, D])
        with ExitStack() as ctx:
            rden = sb(ctx, "rden", [P, NT, HEADS])
            attn = sb(ctx, "attn", [P, 2, D])
            gate = sb(ctx, "gate", [P, KD, EXPERTS])
            xnT = sb(ctx, "xnTc", [P, 2, D])
            logits = sb(ctx, "logits", [P, NT, EXPERTS])
            work = sb(ctx, "work", [P, NT, EXPERTS])
            hot = sb(ctx, "hot", [P, TOP, NT, EXPERTS])
            taken = sb(ctx, "taken", [P, NT, EXPERTS])
            top = sb(ctx, "top", [P, TOP, NT])
            best = sb(ctx, "best", [P, NT])
            gap = sb(ctx, "gap", [P, 2, NT])
            strict = sb(ctx, "strict", [P, P])
            total = sb(ctx, "total", [P, EXPERTS, NT])
            upto = sb(ctx, "upto", [P, EXPERTS, NT])
            resets = sb(ctx, "resets", [P, EXPERTS, NT])
            reverse_i = sb(ctx, "reverse_i", [P, EXPERTS], I32)
            reverse = sb(ctx, "reverse", [P, EXPERTS])
            tiles_i = sb(ctx, "tiles_i", [P, 2, EXPERTS], I32)
            tiles_f = sb(ctx, "tiles_f", [P, 4, EXPERTS])
            past = sb(ctx, "past", [1, TILES, EXPERTS])
            past_sum = sb(ctx, "past_sum", [1, TILES])
            slot_f = sb(ctx, "slot_f", [P, NT])
            valid = sb(ctx, "valid", [P, NT])
            b1_sb = sb(ctx, "b1_sb", [EXPERTS * FC, P])
            psT = [ps(ctx, f"psTc{i}") for i in range(2)]
            psL = [ps(ctx, f"psLc{i}") for i in range(2)]
            HALF = (NT + 1) // 2
            psR = [ps(ctx, f"psRc{i}") for i in range(2)]
            psN = [ps(ctx, f"psNc{i}") for i in range(2)]
            block = ctx.enter_context(nc.Block())

            @block.sync
            def _(sp):
                for c in range(KD):
                    sp.dma_start(gate[:, c, :], gate_w[c * P:(c + 1) * P, :]).then_inc(c_gate, 16)
                sp.dma_start(b1_sb[:, :], b1.rearrange("e (c f) -> (e c) f", f=P)).then_inc(c_b1, 16)
                sp.dma_start(b2_sb[:, :], b2).then_inc(c_b2, 16)
                sp.wait_ge(c_b2, 16)

            @block.gpsimd
            def _(pool):
                nc.gpsimd.iota(reverse_i[:, :], [[-1, EXPERTS]], base=EXPERTS, channel_multiplier=0).then_inc(c_iota, 1)
                nc.gpsimd.memset(valid[:, :], 1.0).then_inc(c_valid, 1)
                pool.wait_ge(c_valid, 1)
                nc.gpsimd.affine_select(out=valid[:, NT - 1:NT], in_=valid[:, NT - 1:NT], compare_op=ALU.is_ge, fill=0.0,
                                        base=REST - 1, pattern=[[0, 1]], channel_multiplier=-1).then_inc(c_iota, 1)
                nc.gpsimd.affine_select(out=strict[:, :], in_=ones[:, :], compare_op=ALU.is_gt, fill=0.0,
                                        base=0, pattern=[[1, P]], channel_multiplier=-1).then_inc(c_strict, 1)
                pool.wait_ge(c_slots, 1)
                for t in range(NT):
                    n = P if t < NT - 1 else REST
                    for k in range(TOP):
                        nc.gpsimd.indirect_dma_start(slot_rows, bass.IndirectOffsetOnAxis(ap=slot_of[0:n, k, t:t + 1], axis=0),
                                                     acc[0:n, t, 0:D], None).then_inc(c_sent, 16)
                pool.wait_ge(c_sent, 16 * TOP * NT)

            @block.scalar
            def _(act):
                act.wait_ge(c_var, 1)
                nc.scalar.activation(rstd[:, :], ln_tmp[:, 0, :], ACT.Sqrt, bias=eps_col[:, 0:1]).then_inc(c_root, 1)

                def copy_xT(t, s, r):
                    act.wait_ge(c_xT_ps, t + 1)
                    if not early(t, 2):
                        act.wait_ge(c_log_ps, t - 1)
                    nc.scalar.copy(xnT[:, s, :], psT[s][:, 0:D]).then_inc(c_xT, 1)
                pipeline(act, NT, 2, 2, [(copy_xT, 0)])
                act.wait_ge(c_gap, 1)
                nc.scalar.activation(gap[:, 1, :], gap[:, 0, :], ACT.Exp).then_inc(c_exp, 1)

            @block.tensor
            def _(pe):
                pe.wait_ge(c_gate, 16 * KD)

                def transpose(t, s, r):
                    pe.wait_ge(c_xn, t + 1)
                    if not early(t, 2):
                        pe.wait_ge(c_xT, t - 1)
                    for c in range(KD):
                        last = nc.tensor.transpose(psT[s][:, c * P:(c + 1) * P], attn[:, s, c * P:(c + 1) * P], ident[:, :])
                    last.then_inc(c_xT_ps, 1)

                def logit(t, s, r):
                    pe.wait_ge(c_xT, t + 1)
                    if not early(t, 2):
                        pe.wait_ge(c_log, t - 1)
                    for c in range(KD):
                        last = nc.tensor.matmul(psL[s][:, 0:EXPERTS], xnT[:, s, c * P:(c + 1) * P], gate[:, c, :],
                                                start=c == 0, stop=c == KD - 1)
                    last.then_inc(c_log_ps, 1)
                pipeline(pe, NT, 2, 3, [(transpose, 0), (logit, 1)])
                pe.wait_ge(c_b1, 16)
                pe.wait_ge(c_xT, NT)
                nc.tensor.transpose(psT[0][:, 0:EXPERTS * FC], b1_sb[:, :], ident[0:EXPERTS * FC, 0:EXPERTS * FC]).then_inc(c_b1_ps, 1)
                pe.wait_ge(c_strict, 1)
                pe.wait_ge(c_taken, 1)
                for i, (lo, hi) in enumerate(((0, HALF), (HALF, NT))):
                    rhs = taken[:, lo:hi, :].rearrange("p t e -> p (t e)")
                    nc.tensor.matmul(psR[i][:, 0:(hi - lo) * EXPERTS], strict[:, :], rhs, start=True, stop=True).then_inc(c_rank, 1)
                    nc.tensor.matmul(psN[i][:, 0:(hi - lo) * EXPERTS], ones[:, :], rhs, start=True, stop=True).then_inc(c_rank, 1)

            @block.vector
            def _(dve):
                step = stepper(dve, c_vstep)
                step(nc.vector.tensor_scalar(rden[:, :, :], acc[:, :, D:ROW], TINY, None, ALU.max))
                step(nc.vector.reciprocal(rden[:, :, :], rden[:, :, :]))

                def residual(t, s, r):
                    nc.vector.tensor_tensor(attn[:, s, :].rearrange("p (h d) -> p h d", h=HEADS),
                                            acc[:, bass.ds(t, 1), 0:D].rearrange("p o (h d) -> p (o h) d", h=HEADS),
                                            over(rden[:, bass.ds(t, 1), :].rearrange("p o h -> p (o h)").unsqueeze(2), [P, HEADS, DH]),
                                            ALU.mult).then_inc(c_lstep, 1)

                def add_x(t, s, r):
                    dve.wait_ge(c_lstep, 2 * t + 1)
                    at = xs[:, bass.ds(t, 1), :].rearrange("p o c -> p (o c)")
                    nc.vector.tensor_tensor(at, at, attn[:, s, :], ALU.add).then_inc(c_lstep, 1)

                def tile_stats(t, s, r):
                    dve.wait_ge(c_lstep, 2 * t + 2)
                    nc.vector.bn_stats(stats[:, bass.ds(t, 1), :].rearrange("p o s -> p (o s)"),
                                       xs[:, bass.ds(t, 1), :].rearrange("p o c -> p (o c)")).then_inc(c_stats, 1)
                pipeline(dve, NT, 2, 2, [(residual, 0), (add_x, 0), (tile_stats, 0)])
                dve.wait_ge(c_stats, NT)
                bulk_rstd(step, c_var)
                dve.wait_ge(c_root, 1)
                step(nc.vector.reciprocal(rstd[:, :], rstd[:, :]))

                def norm(t, s, r):
                    if not early(t, 2):
                        dve.wait_ge(c_xT_ps, t - 1)
                    x_t = xs[:, bass.ds(t, 1), :].rearrange("p o c -> p (o c)")
                    nc.vector.tensor_scalar(attn[:, s, :], x_t, mean[:, bass.ds(t, 1)], rstd[:, bass.ds(t, 1)],
                                            ALU.subtract, ALU.mult).then_inc(c_xn, 1)
                    nc.vector.tensor_scalar(acc[:, bass.ds(t, 1), 0:D].rearrange("p o c -> p (o c)"), x_t,
                                            mean[:, bass.ds(t, 1)], rstd[:, bass.ds(t, 1)],
                                            ALU.subtract, ALU.mult).then_inc(c_stats, 1)

                def keep_logit(t, s, r):
                    dve.wait_ge(c_log_ps, t + 1)
                    nc.vector.tensor_tensor(logits[:, bass.ds(t, 1), :].rearrange("p o e -> p (o e)"), psL[s][:, 0:EXPERTS],
                                            rows_bc[:, 4 * D:], ALU.add).then_inc(c_log, 1)
                pipeline(dve, NT, 2, 4, [(norm, 0), (keep_logit, 2)])
                dve.wait_ge(c_log, NT)
                dve.wait_ge(c_stats, 2 * NT)

                dve.wait_ge(c_iota, 2)
                step(nc.vector.tensor_copy(reverse[:, :], reverse_i[:, :]))
                rev = over(reverse[:, :].unsqueeze(1), [P, NT, EXPERTS])
                wide = [P, NT, EXPERTS]
                for k in range(TOP):
                    step(nc.vector.tensor_reduce(top[:, k, :], logits[:, :, :], AX.X, ALU.max))
                    step(nc.vector.tensor_tensor(work[:, :, :], logits[:, :, :], over(top[:, k, :].unsqueeze(2), wide), ALU.is_equal))
                    step(nc.vector.tensor_tensor(work[:, :, :], work[:, :, :], rev, ALU.mult))
                    step(nc.vector.tensor_reduce(best[:, :], work[:, :, :], AX.X, ALU.max))
                    step(nc.vector.tensor_tensor(hot[:, k, :, :], rev, over(best[:, :].unsqueeze(2), wide), ALU.is_equal))
                    if k < TOP - 1:
                        step(nc.vector.scalar_tensor_tensor(out=logits[:, :, :], in0=hot[:, k, :, :], scalar=-FAR,
                                                            in1=logits[:, :, :], op0=ALU.mult, op1=ALU.add))
                nc.vector.tensor_tensor(gap[:, 0, :], top[:, 1, :], top[:, 0, :], ALU.subtract).then_inc(c_gap, 1)
                step(nc.vector.tensor_tensor(taken[:, :, :], hot[:, 0, :, :], hot[:, 1, :, :], ALU.add))
                nc.vector.tensor_tensor(taken[:, :, :], taken[:, :, :], over(valid[:, :].unsqueeze(2), wide), ALU.mult).then_inc(c_taken, 1)
                dve.wait_ge(c_exp, 1)
                step(nc.vector.tensor_scalar(gap[:, 0, :], gap[:, 1, :], 1.0, None, ALU.add))
                step(nc.vector.reciprocal(share[:, 0, :], gap[:, 0, :]))
                step(nc.vector.tensor_tensor(share[:, 1, :], gap[:, 1, :], share[:, 0, :], ALU.mult))
                step(nc.vector.tensor_tensor(work[:, :, :], hot[:, 0, :, :], over(share[:, 0, :].unsqueeze(2), wide), ALU.mult))
                step(nc.vector.tensor_tensor(dense[:, :, :], hot[:, 1, :, :], over(share[:, 1, :].unsqueeze(2), wide), ALU.mult))
                step(nc.vector.tensor_tensor(dense[:, :, :], dense[:, :, :], work[:, :, :], ALU.add))
                dve.wait_ge(c_b1_ps, 1)
                step(nc.vector.tensor_copy(b1T[:, :, :].rearrange("p e c -> p (e c)"), psT[0][:, 0:EXPERTS * FC]))

                step(nc.vector.memset(resets[:, :, :], 1.0))
                step(nc.vector.memset(resets[:, :, 0:1], 0.0))
                dve.wait_ge(c_rank, 4)
                for i, (lo, hi) in enumerate(((0, HALF), (HALF, NT))):
                    step(nc.vector.tensor_copy(total[:, :, lo:hi],
                                               psN[i][:, 0:(hi - lo) * EXPERTS].rearrange("p (t e) -> p e t", e=EXPERTS)))
                flat = "p e t -> p (e t)"
                step(nc.vector.tensor_tensor_scan(upto[:, :, :].rearrange(flat), resets[:, :, :].rearrange(flat),
                                                  total[:, :, :].rearrange(flat), 0.0, ALU.mult, ALU.add))
                step(nc.vector.tensor_tensor(total[:, :, :], upto[:, :, :], total[:, :, :], ALU.subtract))
                shift = P.bit_length() - 1
                step(nc.vector.tensor_scalar(tiles_i[:, 0, :], upto[:, :, NT - 1], float(P - 1), None, ALU.add))
                step(nc.vector.tensor_scalar(tiles_i[:, 1, :], tiles_i[:, 0, :], shift, None, ALU.arith_shift_right))
                step(nc.vector.tensor_copy(tiles_f[:, 0, :], tiles_i[:, 1, :]))
                step(nc.vector.tensor_tensor_scan(tiles_f[:, 1, :], ones[:, 0:EXPERTS], tiles_f[:, 0, :], 0.0, ALU.mult, ALU.add))
                step(nc.vector.tensor_tensor(tiles_f[:, 2, :], tiles_f[:, 1, :], tiles_f[:, 0, :], ALU.subtract))
                step(nc.vector.tensor_scalar(tiles_f[:, 3, :], tiles_f[:, 2, :], float(P), None, ALU.mult))
                step(nc.vector.tensor_tensor(total[:, :, :], total[:, :, :], over(tiles_f[:, 3, :].unsqueeze(2), [P, EXPERTS, NT]), ALU.add))
                for i, (lo, hi) in enumerate(((0, HALF), (HALF, NT))):
                    step(nc.vector.tensor_tensor(work[:, lo:hi, :], total[:, :, lo:hi].rearrange("p e t -> p t e"),
                                                 psR[i][:, 0:(hi - lo) * EXPERTS].rearrange("p (t e) -> p t e", e=EXPERTS), ALU.add))
                for k in range(TOP):
                    step(nc.vector.tensor_tensor(logits[:, :, :], work[:, :, :], hot[:, k, :, :], ALU.mult))
                    step(nc.vector.tensor_reduce(slot_f[:, :], logits[:, :, :], AX.X, ALU.add))
                    step(nc.vector.tensor_copy(slot_of[:, k, :], slot_f[:, :]))
                long = [1, TILES, EXPERTS]
                step(nc.vector.tensor_tensor(past[:, :, :], over(iota_f[0:1, 0:TILES].unsqueeze(2), long),
                                             over(tiles_f[0:1, 1, :].unsqueeze(1), long), ALU.is_ge))
                step(nc.vector.tensor_reduce(past_sum[:, :], past[:, :, :], AX.X, ALU.add))
                nc.vector.tensor_scalar(tile_expert[:, :], past_sum[:, :], float(EXPERTS - 1), None, ALU.min).then_inc(c_slots, 1)

        WR = 3
        d_w = [sem(f"d_w{i}") for i in range(4)]; d_rows = [sem(f"d_rows{i}") for i in range(4)]
        d_stored = [sem(f"d_stored{i}") for i in range(4)]
        d_xT_ps = sem("d_xT_ps"); d_xT = sem("d_xT"); d_up = sem("d_up"); d_hid = sem("d_hid")
        d_down = sem("d_down"); d_y = sem("d_y")
        with ExitStack() as ctx:
            w1_sb = sb(ctx, "w1_sb", [P, 4, KD, F])
            w2_sb = sb(ctx, "w2_sb", [P, 4, FC, D])
            rows_sb = sb(ctx, "rows_sb", [P, 4, D])
            xT = sb(ctx, "xT", [P, 4, KD, P])
            hid = sb(ctx, "hid", [P, 4, FC, P])
            y_sb = sb(ctx, "y_sb", [P, 4, D])
            psX = [ps(ctx, f"psXd{i}") for i in range(2)]
            psH = [ps(ctx, f"psHd{i}") for i in range(2)]
            psY = [ps(ctx, f"psYd{i}") for i in range(2)]
            block = ctx.enter_context(nc.Block())
            w1_v = w1.rearrange("e (c p) f -> (e c p) f", p=P)
            w2_v = w2.rearrange("e (c p) f -> (e c p) f", p=P)

            @block.sync
            def _(sp):
                def load(j, s, r):
                    e = sp.value_load(tile_expert[0:1, bass.ds(j, 1)], min_val=0, max_val=EXPERTS - 1)
                    if not early(j, 4):
                        sp.wait_ge(d_down, j - 3)
                    sp.dma_start(rows_sb[:, s, :], slot_rows[bass.ds(j * P, P), :]).then_inc(d_rows[s], 16)
                    sp.dma_start(w1_sb[:, s, :, :], w1_v[bass.ds(e * D, D), :].rearrange("(c p) f -> p c f", p=P)).then_inc(d_w[s], 16)
                    sp.dma_start(w2_sb[:, s, :, :], w2_v[bass.ds(e * F, F), :].rearrange("(c p) f -> p c f", p=P)).then_inc(d_w[s], 16)
                pipeline(sp, TILES, 4, 4, [(load, 0)])

            @block.gpsimd
            def _(pool):
                def store(j, s, r):
                    pool.wait_ge(d_y, j + 1)
                    nc.gpsimd.dma_start(expert_rows[bass.ds(j * P, P), :], y_sb[:, s, :]).then_inc(d_stored[s], 16)
                pipeline(pool, TILES, 4, 0, [(store, 0)])
                for s in range(4):
                    pool.wait_ge(d_stored[s], 16 * len(range(s, TILES, 4)))

            @block.tensor
            def _(pe):
                def transpose(j, s, r):
                    pe.wait_ge(d_rows[s], 16 * (r + 1))
                    if not early(j, 2):
                        pe.wait_ge(d_xT, j - 1)
                    for c in range(KD):
                        last = nc.tensor.transpose(psX[s % 2][:, c * P:(c + 1) * P], rows_sb[:, s, c * P:(c + 1) * P], ident[:, :])
                    last.then_inc(d_xT_ps, 1)

                def up(j, s, r):
                    pe.wait_ge(d_w[s], 32 * (r + 1))
                    pe.wait_ge(d_xT, j + 1)
                    if not early(j, 2):
                        pe.wait_ge(d_hid, j - 1)
                    for f in range(FC):
                        for c in range(KD):
                            last = nc.tensor.matmul(psH[s % 2][:, f * P:(f + 1) * P], w1_sb[:, s, c, f * P:(f + 1) * P],
                                                    xT[:, s, c, :], start=c == 0, stop=c == KD - 1)
                    last.then_inc(d_up, 1)

                def down(j, s, r):
                    pe.wait_ge(d_hid, j + 1)
                    if not early(j, 2):
                        pe.wait_ge(d_y, j - 1)
                    for f in range(FC):
                        last = nc.tensor.matmul(psY[s % 2][:, 0:D], hid[:, s, f, :], w2_sb[:, s, f, :],
                                                start=f == 0, stop=f == FC - 1)
                    last.then_inc(d_down, 1)
                pipeline(pe, TILES, 4, 4, [(transpose, 0), (up, 1), (down, 2)])

            @block.scalar
            def _(act):
                def relu(j, s, r):
                    e = act.value_load(tile_expert[0:1, bass.ds(j, 1)], min_val=0, max_val=EXPERTS - 1)
                    act.wait_ge(d_up, j + 1)
                    if not early(j, 4):
                        act.wait_ge(d_down, j - 3)
                    for f in range(FC):
                        last = nc.scalar.activation(hid[:, s, f, :], psH[s % 2][:, f * P:(f + 1) * P], ACT.Relu,
                                                    bias=b1T[:, bass.ds(e, 1), f:f + 1].rearrange("p o f -> p (o f)"))
                    last.then_inc(d_hid, 1)
                pipeline(act, TILES, 4, 4, [(relu, 0)])

            @block.vector
            def _(dve):
                def copy_xT(j, s, r):
                    dve.wait_ge(d_xT_ps, j + 1)
                    if not early(j, 4):
                        dve.wait_ge(d_up, j - 3)
                    nc.vector.tensor_copy(xT[:, s, :, :].rearrange("p c t -> p (c t)"), psX[s % 2][:, 0:D]).then_inc(d_xT, 1)

                def copy_y(j, s, r):
                    dve.wait_ge(d_down, j + 1)
                    if not early(j, 4):
                        dve.wait_ge(d_stored[s], 16 * r)
                    nc.vector.tensor_copy(y_sb[:, s, :], psY[s % 2][:, 0:D]).then_inc(d_y, 1)
                pipeline(dve, TILES, 4, 7, [(copy_xT, 0), (copy_y, 3)])

        ER = 8
        e_got = [sem(f"e_got{i}") for i in range(ER)]
        e_dT_ps = sem("e_dT_ps"); e_dT = sem("e_dT"); e_bias = sem("e_bias"); e_sum = sem("e_sum"); e_fin = sem("e_fin")
        e_dv = sem("e_dv"); e_var = sem("e_var"); e_root = sem("e_root"); e_apart = sem("e_apart"); e_y = sem("e_y")
        e_out = [sem(f"e_out{i}") for i in range(ER)]
        with ExitStack() as ctx:
            got = sb(ctx, "got", [P, ER, TOP, D])
            denseT = sb(ctx, "denseT", [EXPERTS, 2, P])
            dcol = sb(ctx, "dcol", [P, 2, EXPERTS])
            y = sb(ctx, "y", [P, ER, D])
            mv = sb(ctx, "mv", [P, ER, 12])
            psD = [ps(ctx, f"psDe{i}") for i in range(2)]
            psB = [ps(ctx, f"psBe{i}") for i in range(2)]
            block = ctx.enter_context(nc.Block())

            @block.gpsimd
            def _(pool):
                for t in range(NT):
                    n = P if t < NT - 1 else REST
                    if t >= ER:
                        pool.wait_ge(e_sum, 4 * (t - ER) + 3)
                    for k in range(TOP):
                        nc.gpsimd.indirect_dma_start(got[0:n, t % ER, k, :], None, expert_rows,
                                                     bass.IndirectOffsetOnAxis(ap=slot_of[0:n, k, t:t + 1], axis=0)
                                                     ).then_inc(e_got[t % ER], 16)

            @block.tensor
            def _(pe):
                def transpose(t, s, r):
                    pe.wait_ge(e_dv, t + 1)
                    if not early(t, 2):
                        pe.wait_ge(e_dT, t - 1)
                    nc.tensor.transpose(psD[s][0:EXPERTS, 0:P], dcol[:, s, :], ident[:, :]).then_inc(e_dT_ps, 1)

                def bias(t, s, r):
                    pe.wait_ge(e_dT, t + 1)
                    if not early(t, 2):
                        pe.wait_ge(e_sum, 4 * t - 5)
                    nc.tensor.matmul(psB[s][:, 0:D], denseT[:, s, :], b2_sb[:, :], start=True, stop=True).then_inc(e_bias, 1)
                pipeline(pe, NT, 2, 3, [(transpose, 0), (bias, 1)])

            @block.scalar
            def _(act):
                def copy_dT(t, s, r):
                    act.wait_ge(e_dT_ps, t + 1)
                    if not early(t, 2):
                        act.wait_ge(e_bias, t - 1)
                    nc.scalar.copy(denseT[:, s % 2, :], psD[s % 2][0:EXPERTS, 0:P]).then_inc(e_dT, 1)

                def root(t, s, r):
                    act.wait_ge(e_var, t + 1)
                    nc.scalar.activation(mv[:, s, 8:9], mv[:, s, 7:8], ACT.Sqrt, bias=eps_col[:, 0:1]).then_inc(e_root, 1)
                pipeline(act, NT, ER, 10, [(copy_dT, 0), (root, 2)])

            @block.vector
            def _(dve):
                def column(t, s, r):
                    if not early(t, 2):
                        dve.wait_ge(e_dT_ps, t - 1)
                    nc.vector.tensor_copy(dcol[:, s % 2, :], dense[:, bass.ds(t, 1), :].rearrange("p o e -> p (o e)")).then_inc(e_dv, 1)

                def combine(t, s, r):
                    dve.wait_ge(e_got[s], 16 * TOP * (r + 1))
                    dve.wait_ge(e_bias, t + 1)
                    if not early(t, ER):
                        dve.wait_ge(e_out[s], 16 * r)
                    base_row = acc[:, bass.ds(t, 1), 0:D].rearrange("p o c -> p (o c)")
                    nc.vector.scalar_tensor_tensor(out=y[:, s, :], in0=got[:, s, 0, :], scalar=share[:, 0, bass.ds(t, 1)],
                                                   in1=base_row, op0=ALU.mult, op1=ALU.add).then_inc(e_sum, 1)
                    dve.wait_ge(e_sum, 4 * t + 1)
                    nc.vector.scalar_tensor_tensor(out=y[:, s, :], in0=got[:, s, 1, :], scalar=share[:, 1, bass.ds(t, 1)],
                                                   in1=y[:, s, :], op0=ALU.mult, op1=ALU.add).then_inc(e_sum, 1)
                    dve.wait_ge(e_sum, 4 * t + 2)
                    nc.vector.tensor_tensor(y[:, s, :], y[:, s, :], psB[s % 2][:, 0:D], ALU.add).then_inc(e_sum, 1)
                    dve.wait_ge(e_sum, 4 * t + 3)
                    nc.vector.bn_stats(mv[:, s, 0:6], y[:, s, :]).then_inc(e_sum, 1)
                    dve.wait_ge(e_sum, 4 * t + 4)
                    dve.sem_inc(e_apart, 1)
                    nc.vector.bn_aggr(mv[:, s, 6:8], mv[:, s, 0:6]).then_inc(e_var, 1)

                def finish(t, s, r):
                    dve.wait_ge(e_root, t + 1)
                    nc.vector.reciprocal(mv[:, s, 9:10], mv[:, s, 8:9]).then_inc(e_fin, 1)
                    dve.wait_ge(e_fin, 4 * t + 1)
                    nc.vector.tensor_scalar(y[:, s, :], y[:, s, :], mv[:, s, 6:7], mv[:, s, 9:10],
                                            ALU.subtract, ALU.mult).then_inc(e_fin, 1)
                    dve.wait_ge(e_fin, 4 * t + 2)
                    nc.vector.tensor_tensor(y[:, s, :], y[:, s, :], rows_bc[:, 2 * D:3 * D], ALU.mult).then_inc(e_fin, 1)
                    dve.wait_ge(e_fin, 4 * t + 3)
                    nc.vector.tensor_tensor(y[:, s, :], y[:, s, :], rows_bc[:, 3 * D:4 * D], ALU.add).then_inc(e_fin, 1)
                    dve.wait_ge(e_fin, 4 * t + 4)
                    nc.vector.tensor_tensor(y[:, s, :], y[:, s, :], xs[:, bass.ds(t, 1), :].rearrange("p o c -> p (o c)"),
                                            ALU.add).then_inc(e_y, 1)
                pipeline(dve, NT, ER, 10, [(column, 0), (combine, 1), (finish, 2)])

            @block.sync
            def _(sp):
                def store(t, s, r):
                    sp.wait_ge(e_y, t + 1)
                    if isinstance(t, int) and t == NT - 1:
                        sp.dma_start(out[(NT - 1) * P:N, :], y[0:REST, s, :]).then_inc(e_out[s], 16)
                    else:
                        sp.dma_start(out[bass.ds(t * P, P), :], y[:, s, :]).then_inc(e_out[s], 16)
                pipeline(sp, NT, ER, 0, [(store, 0)])
                for s in range(ER):
                    sp.wait_ge(e_out[s], 16 * len(range(s, NT, ER)))


_INS = ['x', 'src', 'dst', 'L0_gnn_W', 'L0_gnn_a_src', 'L0_gnn_a_dst', 'L0_ffn_gate_w', 'L0_ffn_gate_b',
        'L0_ffn_w1', 'L0_ffn_b1', 'L0_ffn_w2', 'L0_ffn_b2', 'L0_ffn_gamma', 'L0_ffn_beta']


def kernel(**inputs):
    import numpy as _np
    import concourse.bacc as _bacc
    from concourse import mybir as _mybir
    from concourse.bass_utils import run_bass_kernel_spmd as _run

    nc = _bacc.Bacc("TRN2", target_bir_lowering=False, num_devices=1)
    arrays, args = {}, []
    for name in _INS:
        a = _np.ascontiguousarray(inputs[name])
        arrays[f"in_{name}_dram"] = a
        args.append(nc.dram_tensor(f"in_{name}_dram", a.shape, _mybir.dt.from_np(a.dtype), kind="ExternalInput").ap())
    out = nc.dram_tensor("out_0_dram", inputs["x"].shape, _mybir.dt.float32, kind="ExternalOutput").ap()
    gnn_moe_kernel(nc, *args, out)
    r = _run(nc, [arrays], core_ids=[0])
    return r.results[0]["out_0_dram"]
```

```python
from contextlib import ExitStack

import concourse.bass as bass
from concourse import mybir

F32 = mybir.dt.float32
I32 = mybir.dt.int32
BF16 = mybir.dt.bfloat16
ALU = mybir.AluOpType
ACT = mybir.ActivationFunctionType
AX = mybir.AxisListType
RMAX = bass.bass_isa.ReduceOp.max

P = 128
G = 4
RING = 8
SLOPE = 0.01
EPS = 1e-5
LEVEL = 64.0
DECIDED = 1e-28
PASSES_MAX = 4096
FAR = 1e30
NOWHERE = 1 << 15
MSG_TO_ACC = 2
TINY = 1e-30
PAD_DST = 1 << 20


def pipeline(eng, count, unroll, head, stages):
    last = max(lag for _, lag in stages)
    head = -(-head // unroll) * unroll
    rounds = (count - head) // unroll

    def peeled(i):
        for stage, lag in stages:
            if 0 <= i - lag < count:
                stage(i - lag, (i - lag) % unroll, (i - lag) // unroll)

    for i in range(head):
        peeled(i)
    with eng.Fori(0, rounds) as r:
        for u in range(unroll):
            for stage, lag in stages:
                at = head + u - lag
                stage(r * unroll + at, at % unroll, r + at // unroll)
    for i in range(head + rounds * unroll, count + last):
        peeled(i)


def early(item, depth):
    return isinstance(item, int) and item < depth


def gnn_moe_kernel(nc, x, src, dst, W, a_src, a_dst, gate_w, gate_b, w1, b1, w2, b2, gamma, beta, out):
    N, D = x.shape
    E = src.shape[0]
    HEADS, _, DH = W.shape
    EXPERTS, _, F = w1.shape
    TOP = 2
    NT = -(-N // P)
    REST = N - (NT - 1) * P
    KD = D // P
    FC = F // P
    ROW = D + HEADS
    CHUNKS = -(-E // P)
    GROUPS = -(-CHUNKS // G)
    assert GROUPS * G * P > E
    FULL = E // (G * P)
    VISITS = FULL + NT
    BLOCKS = -(-CHUNKS // P)
    FULL_CHUNKS = E // P
    TILES = (N * TOP + EXPERTS * (P - 1)) // P
    NE = NT * EXPERTS

    z_table = nc.dram_tensor("z_table", [NT * P, ROW], F32).ap()
    norm_rows = nc.dram_tensor("norm_rows", [NT * P, D], F32).ap()
    pair_rows = nc.dram_tensor("pair_rows", [(TOP * NT + TILES) * P, D], F32).ap()

    whole = ExitStack()

    def sem(name):
        return whole.enter_context(nc.semaphore(name))

    def sb(ctx, name, shape, dt=F32):
        return ctx.enter_context(nc.sbuf_tensor(name, shape, dt))

    def ps(ctx, name, shape=(P, 512)):
        return ctx.enter_context(nc.psum_tensor(name, list(shape), F32))

    def over(ap, shape):
        return ap.to_broadcast(shape)

    with whole:
        xs = sb(whole, "xs", [P, NT, D])
        acc = sb(whole, "acc", [P, NT, ROW])
        ident = sb(whole, "ident", [P, P])
        ones = sb(whole, "ones", [P, P])
        iota_p = sb(whole, "iota_p", [P, 1])
        iota_f = sb(whole, "iota_f", [P, 512])
        rows_bc = sb(whole, "rows_bc", [P, 4 * D + EXPERTS])
        stats = sb(whole, "stats", [P, NT, 6])
        mean = sb(whole, "mean", [P, NT])
        rstd = sb(whole, "rstd", [P, NT])
        ln_tmp = sb(whole, "ln_tmp", [P, 2, NT])
        eps_col = sb(whole, "eps_col", [P, 1])
        esed = sb(whole, "esed", [P, NT, 2 * HEADS])
        graph = whole.enter_context(ExitStack())
        src_idx = sb(graph, "src_idx", [P, BLOCKS * P], I32)
        dst_col = sb(graph, "dst_col", [P, BLOCKS * P])
        visit_base = sb(graph, "visit_base", [P, VISITS])
        visit_tile = sb(graph, "visit_tile", [1, VISITS], I32)
        visit_group = sb(graph, "visit_group", [1, VISITS], I32)
        visit_slot = sb(graph, "visit_slot", [1, VISITS], I32)
        visit_word = sb(graph, "visit_word", [1, VISITS], I32)
        group_free = sb(graph, "group_free", [1, GROUPS], I32)

        def bulk_rstd(step, ready):
            a, b = ln_tmp[:, 0, :], ln_tmp[:, 1, :]
            step(nc.vector.tensor_tensor(mean[:, :], stats[:, :, 1], stats[:, :, 4], ALU.add))
            step(nc.vector.tensor_scalar(mean[:, :], mean[:, :], 0.5, None, ALU.mult))
            step(nc.vector.tensor_tensor(a, stats[:, :, 1], mean[:, :], ALU.subtract))
            step(nc.vector.tensor_tensor(a, a, a, ALU.mult))
            step(nc.vector.tensor_tensor(b, stats[:, :, 2], stats[:, :, 5], ALU.add))
            nc.vector.scalar_tensor_tensor(out=a, in0=b, scalar=1.0 / D, in1=a, op0=ALU.mult, op1=ALU.add).then_inc(ready, 1)

        def stepper(eng, semaphore):
            count = [0]

            def step(instruction):
                count[0] += 1
                instruction.then_inc(semaphore, 1)
                eng.wait_ge(semaphore, count[0])
            return step

        a_const = sem("a_const"); a_identz = sem("a_identz"); a_padded = sem("a_padded")
        a_x = [sem(f"a_x{i}") for i in range(2)]
        a_edges = sem("a_edges"); a_w = sem("a_w"); a_rows = sem("a_rows"); a_last = sem("a_last")
        a_vstep = sem("a_vstep"); a_rows_ps = sem("a_rows_ps"); a_rows_sb = sem("a_rows_sb")
        a_edge_f = sem("a_edge_f"); a_edge_ps = sem("a_edge_ps"); a_edge_sb = sem("a_edge_sb")
        a_last_f = sem("a_last_f"); a_last_ps = sem("a_last_ps"); a_ge = sem("a_ge"); a_cnt = sem("a_cnt")
        a_stats = sem("a_stats"); a_var = sem("a_var"); a_root = sem("a_root"); a_waug = sem("a_waug")
        a_xn = sem("a_xn"); a_xT_ps = sem("a_xT_ps"); a_xT = sem("a_xT"); a_z_ps = sem("a_z_ps")
        a_z = sem("a_z"); a_store = [sem(f"a_store{i}") for i in range(2)]
        with ExitStack() as ctx:
            src_raw = sb(ctx, "src_raw", [P, BLOCKS, P], I32)
            dst_raw = sb(ctx, "dst_raw", [P, BLOCKS, P], I32)
            edge_f = sb(ctx, "edge_f", [P, 2, BLOCKS, P])
            wcat = sb(ctx, "wcat", [P, KD, D + 2 * HEADS])
            wprod = sb(ctx, "wprod", [P, D])
            rows = sb(ctx, "rows", [1, 4 * D + EXPERTS])
            last_i = sb(ctx, "last_i", [1, FULL], I32)
            last_f = sb(ctx, "last_f", [1, FULL])
            iota_i = sb(ctx, "iota_i", [P, 512], I32)
            iota_pi = sb(ctx, "iota_pi", [P, 1], I32)
            below = sb(ctx, "below", [P, 3, 512])
            thr = sb(ctx, "thr", [P, 4])
            xn = sb(ctx, "xn", [P, 2, D])
            xnT = sb(ctx, "xnT", [P, 2, D])
            z_out = sb(ctx, "z_out", [P, 2, ROW])
            psA = [ps(ctx, f"psA{i}") for i in range(4)]
            psT = [ps(ctx, f"psTa{i}") for i in range(2)]
            psZ = [ps(ctx, f"psZa{i}") for i in range(2)]
            block = ctx.enter_context(nc.Block())
            EB = [(k, b) for k in range(2) for b in range(0, BLOCKS, 4)]

            @block.sync
            def _(sp):
                half = (NT - 1) // 2
                sp.dma_start(xs[:, 0:half, :], x[0:half * P].rearrange("(t p) c -> p t c", p=P)).then_inc(a_x[0], 16)
                sp.dma_start(xs[:, half:NT - 1, :], x[half * P:(NT - 1) * P].rearrange("(t p) c -> p t c", p=P)).then_inc(a_x[0], 16)
                for c in range(KD):
                    sp.dma_start(wcat[:, c, 0:D].rearrange("p (h d) -> p h d", h=HEADS),
                                 W[:, c * P:(c + 1) * P, :].rearrange("h p d -> p h d")).then_inc(a_w, 16)
                sp.wait_ge(a_padded, 1)
                sp.dma_start(xs[0:REST, NT - 1, :], x[(NT - 1) * P:N]).then_inc(a_x[1], 16)

                def store(t, s, r):
                    sp.wait_ge(a_z, t + 1)
                    sp.dma_start(z_table[bass.ds(t * P, P), :], z_out[:, s, :]).then_inc(a_store[s], 16)
                pipeline(sp, NT, 2, 2, [(store, 0)])
                for s in range(2):
                    sp.wait_ge(a_store[s], 16 * len(range(s, NT, 2)))

            @block.scalar
            def _(act):
                for i, r in enumerate((a_src, a_dst)):
                    act.dma_start(rows[0:1, i * D:(i + 1) * D], r.rearrange("h d -> (h d)").unsqueeze(0)).then_inc(a_rows, 16)
                for i, r in enumerate((gamma, beta)):
                    act.dma_start(rows[0:1, (2 + i) * D:(3 + i) * D], r.unsqueeze(0)).then_inc(a_rows, 16)
                act.dma_start(rows[0:1, 4 * D:], gate_b.unsqueeze(0)).then_inc(a_rows, 16)
                act.wait_ge(a_padded, 3)
                tail = BLOCKS - 1
                for raw, e in ((src_raw, src), (dst_raw, dst)):
                    act.dma_start(raw[:, 0:tail, :], e[0:tail * P * P].rearrange("(b p f) -> p b f", p=P, f=P)).then_inc(a_edges, 16)
                    n = FULL_CHUNKS - tail * P
                    act.dma_start(raw[0:n, tail, :], e[tail * P * P:FULL_CHUNKS * P].rearrange("(p f) -> p f", f=P)).then_inc(a_edges, 16)
                    if E > FULL_CHUNKS * P:
                        act.dma_start(raw[n:n + 1, tail, 0:E - FULL_CHUNKS * P],
                                      e[FULL_CHUNKS * P:E].unsqueeze(0)).then_inc(a_edges, 16)
                with nc.allow_non_contiguous_dma("the last destination of each group"):
                    act.dma_start(last_i[:, :], dst[0:FULL * G * P].rearrange("(g f) -> g f", f=G * P)[:, G * P - 1:G * P]
                                  .rearrange("g o -> o g")).then_inc(a_last, 16)
                act.wait_ge(a_var, 1)
                nc.scalar.activation(rstd[:, :], ln_tmp[:, 0, :], ACT.Sqrt, bias=eps_col[:, 0:1]).then_inc(a_root, 1)

                def copy_xT(t, s, r):
                    act.wait_ge(a_xT_ps, t + 1)
                    if not early(t, 2):
                        act.wait_ge(a_z_ps, t - 1)
                    nc.scalar.copy(xnT[:, s, :], psT[s][:, 0:D]).then_inc(a_xT, 1)

                def copy_z(t, s, r):
                    act.wait_ge(a_z_ps, t + 1)
                    if not early(t, 2):
                        act.wait_ge(a_store[s], 16 * r)
                    nc.scalar.copy(z_out[:, s, :], psZ[s][:, 0:ROW])
                    nc.scalar.copy(esed[:, bass.ds(t, 1), :].rearrange("p o c -> p (o c)"),
                                   psZ[s][:, D:D + 2 * HEADS]).then_inc(a_z, 1)
                pipeline(act, NT, 2, 3, [(copy_xT, 0), (copy_z, 1)])

            @block.gpsimd
            def _(pool):
                nc.gpsimd.memset(xs[:, NT - 1, :], 0.0).then_inc(a_padded, 1)
                nc.gpsimd.memset(src_raw[:, BLOCKS - 1, :], 0).then_inc(a_padded, 1)
                nc.gpsimd.memset(dst_raw[:, BLOCKS - 1, :], PAD_DST).then_inc(a_padded, 1)
                nc.gpsimd.memset(ident[:, :], 0.0).then_inc(a_identz, 1)
                nc.gpsimd.memset(ones[:, :], 1.0).then_inc(a_const, 1)
                nc.gpsimd.memset(eps_col[:, :], EPS).then_inc(a_const, 1)
                nc.gpsimd.iota(iota_i[:, :], [[1, 512]], base=0, channel_multiplier=0).then_inc(a_const, 1)
                nc.gpsimd.iota(iota_pi[:, :], [[1, 1]], base=0, channel_multiplier=1).then_inc(a_const, 1)
                pool.wait_ge(a_identz, 1)
                nc.gpsimd.affine_select(out=ident[:, :], in_=ident[:, :], compare_op=ALU.not_equal, fill=1.0,
                                        base=0, pattern=[[-1, P]], channel_multiplier=1).then_inc(a_const, 1)

            @block.vector
            def _(dve):
                step = stepper(dve, a_vstep)
                dve.wait_ge(a_const, 5)
                step(nc.vector.tensor_copy(iota_f[:, :], iota_i[:, :]))
                step(nc.vector.tensor_copy(iota_p[:, :], iota_pi[:, :]))
                dve.wait_ge(a_rows_ps, 3)
                for i, (lo, hi) in enumerate(((0, 2 * D), (2 * D, 4 * D), (4 * D, 4 * D + EXPERTS))):
                    nc.vector.tensor_copy(rows_bc[:, lo:hi], psA[i][:, 0:hi - lo]).then_inc(a_rows_sb, 1)
                dve.wait_ge(a_w, 16 * KD)
                dve.wait_ge(a_rows_sb, 3)
                for c in range(KD):
                    for k in range(2):
                        step(nc.vector.tensor_tensor(wprod[:, :], wcat[:, c, 0:D], rows_bc[:, k * D:(k + 1) * D], ALU.mult))
                        step(nc.vector.tensor_reduce(wcat[:, c, D + k * HEADS:D + (k + 1) * HEADS],
                                                     wprod[:, :].rearrange("p (h d) -> p h d", h=HEADS), AX.X, ALU.add))
                dve.wait_ge(a_x[0], 32)
                dve.wait_ge(a_x[1], 16)

                def tile_stats(t, s, r):
                    nc.vector.bn_stats(stats[:, bass.ds(t, 1), :].rearrange("p o s -> p (o s)"),
                                       xs[:, bass.ds(t, 1), :].rearrange("p o c -> p (o c)")).then_inc(a_stats, 1)
                pipeline(dve, NT, 8, 1, [(tile_stats, 0)])
                dve.wait_ge(a_stats, NT)
                bulk_rstd(step, a_var)
                dve.wait_ge(a_root, 1)
                step(nc.vector.reciprocal(rstd[:, :], rstd[:, :]))

                def norm(t, s, r):
                    if not early(t, 2):
                        dve.wait_ge(a_xT_ps, t - 1)
                    nc.vector.tensor_scalar(xn[:, s, :], xs[:, bass.ds(t, 1), :].rearrange("p o c -> p (o c)"),
                                            mean[:, bass.ds(t, 1)], rstd[:, bass.ds(t, 1)],
                                            ALU.subtract, ALU.mult).then_inc(a_xn, 1)
                pipeline(dve, NT, 2, 2, [(norm, 0)])

                dve.wait_ge(a_edges, 16 * (6 if E > FULL_CHUNKS * P else 4))
                for k, raw in enumerate((src_raw, dst_raw)):
                    nc.vector.tensor_copy(edge_f[:, k, :, :], raw[:, :, :]).then_inc(a_edge_f, 1)
                for n, (k, b) in enumerate(EB):
                    m = min(4, BLOCKS - b)
                    dve.wait_ge(a_edge_ps, n + 1)
                    to = (src_idx, dst_col)[k]
                    nc.vector.tensor_copy(to[:, b * P:(b + m) * P], psA[n % 4][:, 0:m * P]).then_inc(a_edge_sb, 1)
                dve.wait_ge(a_last, 16)
                nc.vector.tensor_copy(last_f[:, :], last_i[:, :]).then_inc(a_last_f, 1)
                step(nc.vector.tensor_scalar(thr[:, 0:1], iota_p[:, :], float(P), float(P), ALU.mult, ALU.add))
                dve.wait_ge(a_last_ps, 1)
                step(nc.vector.tensor_scalar(below[:, 2, 0:FULL], psT[0][:, 0:FULL], thr[:, 0:1], None, ALU.is_lt))
                step(nc.vector.tensor_reduce(thr[:, 1:2], below[:, 2, 0:FULL], AX.X, ALU.add))
                step(nc.vector.scalar_tensor_tensor(out=thr[:, 2:3], in0=iota_p[:, :], scalar=1.0, in1=thr[:, 1:2], op0=ALU.add, op1=ALU.add))
                nc.vector.tensor_scalar(below[:, 0, 0:VISITS], iota_f[:, 0:VISITS], thr[:, 2:3], None, ALU.is_ge).then_inc(a_ge, 1)
                nc.vector.tensor_scalar(below[:, 1, 0:GROUPS], iota_f[:, 0:GROUPS], thr[:, 1:2], None, ALU.is_gt).then_inc(a_ge, 1)
                dve.wait_ge(a_cnt, 2)
                step(nc.vector.tensor_scalar(visit_base[:, :], psT[0][:, 0:VISITS], -float(P), None, ALU.mult))
                step(nc.vector.tensor_copy(visit_tile[:, :], psT[0][0:1, 0:VISITS]))
                step(nc.vector.scalar_tensor_tensor(out=visit_group[:, :], in0=psT[0][0:1, 0:VISITS], scalar=-1.0,
                                                    in1=iota_f[0:1, 0:VISITS], op0=ALU.mult, op1=ALU.add))
                step(nc.vector.tensor_scalar(visit_slot[:, :], visit_group[:, :], RING - 1, None, ALU.bitwise_and))
                step(nc.vector.tensor_copy(visit_word[:, :], visit_slot[:, :]))
                step(nc.vector.scalar_tensor_tensor(out=visit_word[:, MSG_TO_ACC:VISITS], in0=visit_tile[:, 0:VISITS - MSG_TO_ACC],
                                                    scalar=float(RING), in1=visit_slot[:, MSG_TO_ACC:VISITS], op0=ALU.mult, op1=ALU.add))
                step(nc.vector.memset(group_free[:, 0:RING], 0))
                step(nc.vector.tensor_tensor(group_free[:, RING - 1:GROUPS], psT[1][0:1, 0:GROUPS - RING + 1],
                                             iota_f[0:1, 0:GROUPS - RING + 1], ALU.add))

            @block.tensor
            def _(pe):
                pe.wait_ge(a_const, 5)
                pe.wait_ge(a_rows, 16 * 5)
                for i, (lo, hi) in enumerate(((0, 2 * D), (2 * D, 4 * D), (4 * D, 4 * D + EXPERTS))):
                    nc.tensor.matmul(psA[i][:, 0:hi - lo], ones[0:1, :], rows[0:1, lo:hi], start=True, stop=True).then_inc(a_rows_ps, 1)

                def transpose(t, s, r):
                    pe.wait_ge(a_xn, t + 1)
                    if not early(t, 2):
                        pe.wait_ge(a_xT, t - 1)
                    for c in range(KD):
                        last = nc.tensor.transpose(psT[s][:, c * P:(c + 1) * P], xn[:, s, c * P:(c + 1) * P], ident[:, :])
                    last.then_inc(a_xT_ps, 1)

                def project(t, s, r):
                    pe.wait_ge(a_xT, t + 1)
                    if not early(t, 2):
                        pe.wait_ge(a_z, t - 1)
                    for c in range(KD):
                        last = nc.tensor.matmul(psZ[s][:, 0:D + 2 * HEADS], xnT[:, s, c * P:(c + 1) * P], wcat[:, c, :],
                                                start=c == 0, stop=c == KD - 1)
                    last.then_inc(a_z_ps, 1)
                pipeline(pe, NT, 2, 3, [(transpose, 0), (project, 1)])
                pe.wait_ge(a_edge_f, 2)
                pe.wait_ge(a_rows_sb, 3)
                for n, (k, b) in enumerate(EB):
                    if n >= 4:
                        pe.wait_ge(a_edge_sb, n - 3)
                    for j in range(min(4, BLOCKS - b)):
                        last = nc.tensor.transpose(psA[n % 4][:, j * P:(j + 1) * P], edge_f[:, k, b + j, :], ident[:, :])
                    last.then_inc(a_edge_ps, 1)
                pe.wait_ge(a_last_f, 1)
                pe.wait_ge(a_xT, NT)
                nc.tensor.matmul(psT[0][:, 0:FULL], ones[0:1, :], last_f[0:1, :], start=True, stop=True).then_inc(a_last_ps, 1)
                pe.wait_ge(a_ge, 2)
                nc.tensor.matmul(psT[0][:, 0:VISITS], ones[0:NT, :], below[0:NT, 0, 0:VISITS], start=True, stop=True).then_inc(a_cnt, 1)
                nc.tensor.matmul(psT[1][:, 0:GROUPS], ones[0:NT, :], below[0:NT, 1, 0:GROUPS], start=True, stop=True).then_inc(a_cnt, 1)

        b_vstep = sem("b_vstep")
        b_spread = sem("b_spread"); b_all = sem("b_all"); b_passes = sem("b_passes")
        b_pstep = sem("b_pstep"); b_nodes = sem("b_nodes")
        b_idx = [sem(f"b_idx{i}") for i in range(RING)]; b_landed = [sem(f"b_landed{i}") for i in range(RING)]
        b_group = sem("b_group"); b_apart = sem("b_apart")
        b_loc = sem("b_loc"); b_S = sem("b_S"); b_ST_ps = sem("b_ST_ps"); b_ST = sem("b_ST")
        b_dest = sem("b_dest"); b_estep = sem("b_estep"); b_arg = sem("b_arg"); b_p = sem("b_p")
        b_msg = sem("b_msg"); b_sum = sem("b_sum"); b_acc = sem("b_acc"); b_es = sem("b_es")
        SH = 2 * HEADS
        SR = 8
        with ExitStack() as ctx:
            nodes = sb(ctx, "nodes", [P, NT, SH])
            level = sb(ctx, "level", [P, HEADS])
            spread = sb(ctx, "spread", [P, 2 * SH])
            spread_all = sb(ctx, "spread_all", [P, SH])
            npass_f = sb(ctx, "npass_f", [P, 2])
            npass_i = sb(ctx, "npass_i", [P, 1], I32)
            decided = sb(ctx, "decided", [P, NT, HEADS])
            pass_tmp = sb(ctx, "pass_tmp", [P, NT, HEADS])
            idx_ring = sb(ctx, "idx_ring", [P, RING, G], I32)
            ring = sb(ctx, "ring", [P, RING, G, ROW])
            es_edge = sb(ctx, "es_edge", [P, 4, G, HEADS])
            loc = sb(ctx, "loc", [P, SR, G])
            S = sb(ctx, "S", [P, SR, G, P])
            ST = sb(ctx, "ST", [P, 2, G * P])
            earg = sb(ctx, "earg", [P, 4, 3, G * HEADS])
            msg = sb(ctx, "msg", [P, 4, G, ROW])
            psT = [ps(ctx, f"psTb{i}") for i in range(2)]
            psE = [ps(ctx, f"psEb{i}") for i in range(2)]
            psM = [ps(ctx, f"psMb{i}") for i in range(2)]
            block = ctx.enter_context(nc.Block())

            @block.sync
            def _(sp):
                sp.wait_ge(b_passes, 1)
                npass = sp.value_load(npass_i[0:1, 0:1], min_val=1, max_val=PASSES_MAX)
                with sp.Fori(0, npass) as k:
                    def uses(s):
                        return len(range(s, GROUPS, RING))

                    def fetch_idx(g, s, r):
                        sp.dma_start(idx_ring[:, s, :], src_idx[:, bass.ds(g * G, G)]).then_inc(b_idx[s], 16)

                    def relay(g, s, r):
                        sp.wait_ge(b_landed[s], 16 * G * (k * uses(s) + r + 1))
                        sp.nop().then_inc(b_group, 1)

                    for g in range(RING):
                        fetch_idx(g, g, 0)
                    rounds = GROUPS // RING - 1
                    with sp.Fori(0, rounds) as r:
                        for s in range(RING):
                            relay(r * RING + s, s, r)
                            fetch_idx((r + 1) * RING + s, s, r + 1)
                    for g in range(rounds * RING, GROUPS):
                        relay(g, g % RING, g // RING)
                        if g + RING < GROUPS:
                            fetch_idx(g + RING, g % RING, g // RING + 1)


            @block.gpsimd
            def _(pool):
                pool.wait_ge(b_spread, 1)
                nc.gpsimd.partition_all_reduce(spread_all[:, :], spread[:, 0:SH], P, RMAX).then_inc(b_all, 1)
                pool.wait_ge(b_passes, 1)
                npass = pool.value_load(npass_i[0:1, 0:1], min_val=1, max_val=PASSES_MAX)
                with pool.Fori(0, npass) as k:
                    def gather(g, s, r):
                        done = pool.value_load(group_free[0:1, bass.ds(g, 1)], min_val=0, max_val=VISITS)
                        pool.wait_ge(b_msg, k * VISITS + done + 1)
                        pool.wait_ge(b_idx[s], 16 * (k * len(range(s, GROUPS, RING)) + r + 1))
                        pool.sem_inc(b_apart, 1)
                        for c in range(G):
                            nc.gpsimd.indirect_dma_start(ring[:, s, c, :], None, z_table,
                                                         bass.IndirectOffsetOnAxis(ap=idx_ring[:, s, c:c + 1], axis=0)
                                                         ).then_inc(b_landed[s], 16)
                    pipeline(pool, GROUPS, RING, 0, [(gather, 0)])

            @block.vector
            def _(dve):
                step = stepper(dve, b_vstep)
                step(nc.vector.tensor_reduce(spread[:, 0:HEADS], esed[:, :, 0:HEADS].rearrange("p t h -> p h t"), AX.X, ALU.max))
                step(nc.vector.tensor_reduce(spread[:, SH:SH + HEADS], esed[:, :, 0:HEADS].rearrange("p t h -> p h t"), AX.X, ALU.min))
                nc.vector.tensor_scalar(spread[:, HEADS:SH], spread[:, SH:SH + HEADS], -1.0, None, ALU.mult).then_inc(b_spread, 1)
                nc.vector.memset(acc[:, :, :], 0.0).then_inc(b_msg, 1)
                step(nc.vector.tensor_copy(nodes[:, :, 0:HEADS], esed[:, :, HEADS:SH]))
                dve.wait_ge(b_all, 1)
                step(nc.vector.tensor_copy(level[:, :], spread_all[:, 0:HEADS]))
                step(nc.vector.tensor_tensor(spread[:, SH + HEADS:2 * SH], spread_all[:, 0:HEADS], spread_all[:, HEADS:SH], ALU.add))
                step(nc.vector.tensor_reduce(npass_f[:, 0:1], spread[:, SH + HEADS:2 * SH], AX.X, ALU.max))
                step(nc.vector.tensor_scalar(npass_f[:, 1:2], npass_f[:, 0:1], 1.0 / LEVEL, 1.0, ALU.mult, ALU.add))
                nc.vector.tensor_scalar(npass_i[:, :], npass_f[:, 1:2], float(PASSES_MAX), None, ALU.min).then_inc(b_passes, 1)
                dve.wait_ge(b_passes, 1)
                npass = dve.value_load(npass_i[0:1, 0:1], min_val=1, max_val=PASSES_MAX)
                with dve.Fori(0, npass) as k:
                    PASS_STEPS = 5
                    made = [0]

                    def pass_step(instruction):
                        made[0] += 1
                        instruction.then_inc(b_pstep, 1)
                        dve.wait_ge(b_pstep, k * PASS_STEPS + made[0])
                    den = acc[:, :, D:ROW]
                    pass_step(nc.vector.tensor_scalar(decided[:, :, :], den, DECIDED, None, ALU.is_ge))
                    pass_step(nc.vector.tensor_tensor(pass_tmp[:, :, :], esed[:, :, HEADS:SH],
                                                      over(level[:, :].unsqueeze(1), [P, NT, HEADS]), ALU.add))
                    pass_step(nc.vector.scalar_tensor_tensor(out=pass_tmp[:, :, :], in0=pass_tmp[:, :, :], scalar=SLOPE,
                                                             in1=pass_tmp[:, :, :], op0=ALU.mult, op1=ALU.max))
                    pass_step(nc.vector.scalar_tensor_tensor(out=nodes[:, :, HEADS:SH], in0=decided[:, :, :], scalar=FAR,
                                                             in1=pass_tmp[:, :, :], op0=ALU.mult, op1=ALU.add))
                    pass_step(nc.vector.tensor_scalar(level[:, :], level[:, :], LEVEL, None, ALU.subtract))
                    for h in range(HEADS):
                        nc.vector.tensor_tensor(acc[:, :, h * DH:(h + 1) * DH], acc[:, :, h * DH:(h + 1) * DH],
                                                       over(decided[:, :, h:h + 1], [P, NT, DH]), ALU.mult)
                    assert made[0] == PASS_STEPS
                    nc.vector.tensor_tensor(den, den, decided[:, :, :], ALU.mult).then_inc(b_nodes, 1)
                    dve.wait_ge(b_nodes, k + 1)
                    dve.sem_inc(b_apart, 1)
                    base = k * VISITS

                    def one_hot(v, s, r):
                        dve.wait_ge(b_loc, base + v + 1)
                        if not early(v, SR):
                            dve.wait_ge(b_sum, base + v - SR + 1)
                        nc.vector.tensor_tensor(S[:, s, :, :], over(iota_f[:, 0:P].unsqueeze(1), [P, G, P]),
                                                over(loc[:, s, :].unsqueeze(2), [P, G, P]), ALU.is_equal).then_inc(b_S, 1)

                    def e_add(v, s, r):
                        dve.wait_ge(b_es, base + v + 1)
                        dve.wait_ge(b_dest, base + v + 1)
                        dest = psE[s % 2][:, 0:G * SH].rearrange("p (g c) -> p g c", g=G)
                        nc.vector.tensor_tensor(earg[:, s % 4, 0, :].rearrange("p (g h) -> p g h", g=G),
                                                es_edge[:, s % 4, :, :], dest[:, :, 0:HEADS], ALU.add).then_inc(b_estep, 1)

                    def e_lrelu(v, s, r):
                        dve.wait_ge(b_estep, 3 * base + 3 * v + 1)
                        nc.vector.scalar_tensor_tensor(out=earg[:, s % 4, 1, :], in0=earg[:, s % 4, 0, :], scalar=SLOPE,
                                                       in1=earg[:, s % 4, 0, :], op0=ALU.mult, op1=ALU.max).then_inc(b_estep, 1)

                    def e_shift(v, s, r):
                        dve.wait_ge(b_estep, 3 * base + 3 * v + 2)
                        dest = psE[s % 2][:, 0:G * SH].rearrange("p (g c) -> p g c", g=G)
                        nc.vector.tensor_tensor(earg[:, s % 4, 2, :].rearrange("p (g h) -> p g h", g=G),
                                                earg[:, s % 4, 1, :].rearrange("p (g h) -> p g h", g=G),
                                                dest[:, :, HEADS:SH], ALU.subtract).then_inc(b_estep, 1)

                    def e_clamp(v, s, r):
                        dve.wait_ge(b_estep, 3 * base + 3 * v + 3)
                        nc.vector.tensor_scalar(earg[:, s % 4, 0, :], earg[:, s % 4, 2, :], 0.0, None, ALU.min).then_inc(b_arg, 1)

                    word = [None]

                    def look_up(v, s, r):
                        word[0] = dve.value_load(visit_word[0:1, bass.ds(v, 1)], min_val=0, max_val=RING * NT - 1)

                    def message(v, s, r):
                        slot = word[0] & (RING - 1)
                        dve.wait_ge(b_p, base + v + 1)
                        nc.vector.tensor_tensor(msg[:, s % 4, :, 0:D].rearrange("p g (h d) -> p g h d", h=HEADS),
                                                ring[:, bass.ds(slot, 1), :, 0:D].rearrange("p o g (h d) -> p (o g) h d", h=HEADS),
                                                over(msg[:, s % 4, :, D:ROW].unsqueeze(3), [P, G, HEADS, DH]), ALU.mult).then_inc(b_msg, 1)

                    def accumulate(v, s, r):
                        if isinstance(v, int) and v + MSG_TO_ACC >= VISITS:
                            tile = dve.value_load(visit_tile[0:1, bass.ds(v, 1)], min_val=0, max_val=NT - 1)
                        else:
                            tile = (word[0] >> (RING.bit_length() - 1)).with_bounds(min_val=0, max_val=NT - 1)
                        dve.wait_ge(b_sum, base + v + 1)
                        if not early(v, 1):
                            dve.wait_ge(b_acc, base + v)
                        at = acc[:, bass.ds(tile, 1), :].rearrange("p o c -> p (o c)")
                        nc.vector.tensor_tensor(at, at, psM[s % 2][:, 0:ROW], ALU.add).then_inc(b_acc, 1)
                    pipeline(dve, VISITS, SR, SR, [(look_up, 3), (e_add, 2), (one_hot, 0), (e_lrelu, 2), (accumulate, 3 + MSG_TO_ACC),
                                                   (e_shift, 2), (message, 3), (e_clamp, 2)])
                    dve.wait_ge(b_acc, base + VISITS)

            @block.scalar
            def _(act):
                act.wait_ge(b_passes, 1)
                npass = act.value_load(npass_i[0:1, 0:1], min_val=1, max_val=PASSES_MAX)
                with act.Fori(0, npass) as k:
                    base = k * VISITS

                    def locate(v, s, r):
                        group = act.value_load(visit_group[0:1, bass.ds(v, 1)], min_val=0, max_val=GROUPS - 1)
                        if not early(v, SR):
                            act.wait_ge(b_S, base + v - SR + 1)
                        nc.scalar.activation(loc[:, s, :], dst_col[:, bass.ds(group * G, G)], ACT.Identity,
                                             bias=visit_base[:, bass.ds(v, 1)]).then_inc(b_loc, 1)

                    def open_group(v, s, r):
                        group = act.value_load(visit_group[0:1, bass.ds(v, 1)], min_val=0, max_val=GROUPS - 1)
                        slot = group & (RING - 1)
                        act.wait_ge(b_group, k * GROUPS + group + 1)
                        if not early(v, 4):
                            act.wait_ge(b_arg, base + v - 3)
                        nc.scalar.copy(es_edge[:, s % 4, :, :],
                                       ring[:, bass.ds(slot, 1), :, D:ROW].rearrange("p o g h -> p (o g) h")).then_inc(b_es, 1)

                    def copy_ST(v, s, r):
                        act.wait_ge(b_ST_ps, base + v + 1)
                        if not early(v, 2):
                            act.wait_ge(b_dest, base + v - 1)
                        nc.scalar.copy(ST[:, s % 2, :], psT[s % 2][:, 0:G * P]).then_inc(b_ST, 1)

                    def exponent(v, s, r):
                        act.wait_ge(b_arg, base + v + 1)
                        if not early(v, 4):
                            act.wait_ge(b_sum, base + v - 3)
                        nc.scalar.activation(msg[:, s % 4, :, D:ROW], earg[:, s % 4, 0, :].rearrange("p (g h) -> p g h", g=G),
                                             ACT.Exp).then_inc(b_p, 1)
                    pipeline(act, VISITS, SR, 8, [(locate, 0), (copy_ST, 2), (open_group, 2), (exponent, 3)])

            @block.tensor
            def _(pe):
                pe.wait_ge(b_passes, 1)
                npass = pe.value_load(npass_i[0:1, 0:1], min_val=1, max_val=PASSES_MAX)
                with pe.Fori(0, npass) as k:
                    base = k * VISITS
                    pe.wait_ge(b_nodes, k + 1)

                    def transpose(v, s, r):
                        pe.wait_ge(b_S, base + v + 1)
                        if not early(v, 2):
                            pe.wait_ge(b_ST, base + v - 1)
                        for c in range(G):
                            last = nc.tensor.transpose(psT[s % 2][:, c * P:(c + 1) * P], S[:, s, c, :], ident[:, :])
                        last.then_inc(b_ST_ps, 1)

                    def destination(v, s, r):
                        tile = pe.value_load(visit_tile[0:1, bass.ds(v, 1)], min_val=0, max_val=NT - 1)
                        pe.wait_ge(b_ST, base + v + 1)
                        if not early(v, 2):
                            pe.wait_ge(b_arg, base + v - 1)
                        for c in range(G):
                            last = nc.tensor.matmul(psE[s % 2][:, c * SH:(c + 1) * SH], ST[:, s % 2, c * P:(c + 1) * P],
                                                    nodes[:, bass.ds(tile, 1), :].rearrange("p o c -> p (o c)"),
                                                    start=True, stop=True)
                        last.then_inc(b_dest, 1)

                    def weigh(v, s, r):
                        pe.wait_ge(b_msg, base + v + 2)
                        if not early(v, 2):
                            pe.wait_ge(b_acc, base + v - 1)
                        for c in range(G):
                            last = nc.tensor.matmul(psM[s % 2][:, 0:ROW], S[:, s, c, :], msg[:, s % 4, c, :],
                                                    start=c == 0, stop=c == G - 1)
                        last.then_inc(b_sum, 1)
                    pipeline(pe, VISITS, SR, 5, [(transpose, 0), (destination, 1), (weigh, 3)])

        graph.close()
        c_vstep = sem("c_vstep"); c_stats = sem("c_stats"); c_var = sem("c_var")
        c_root = sem("c_root"); c_gate = sem("c_gate"); c_xn = sem("c_xn"); c_xT_ps = sem("c_xT_ps")
        c_xT = sem("c_xT"); c_log_ps = sem("c_log_ps"); c_log = sem("c_log"); c_gap = sem("c_gap")
        c_exp = sem("c_exp"); c_strict = sem("c_strict"); c_taken = sem("c_taken"); c_rank = sem("c_rank")
        c_b1 = sem("c_b1"); c_b1_ps = sem("c_b1_ps"); c_iota = sem("c_iota"); c_b2 = sem("c_b2")
        c_valid = sem("c_valid"); c_kept = sem("c_kept"); c_saved = [sem(f"c_saved{i}") for i in range(4)]
        c_low = sem("c_low"); c_high = sem("c_high"); c_listed = sem("c_listed")
        share = sb(whole, "share", [P, TOP, NT])
        dense = sb(whole, "dense", [P, NT, EXPERTS])
        slot_ends = sb(whole, "slot_ends", [P, TILES, 2], I32)
        tile_expert = sb(whole, "tile_expert", [1, TILES], I32)
        b1T = sb(whole, "b1T", [P, EXPERTS, FC])
        b2_sb = sb(whole, "b2_sb", [EXPERTS, D])
        with ExitStack() as ctx:
            rden = sb(ctx, "rden", [P, NT, HEADS])
            xn = sb(ctx, "xnc", [P, 4, D])
            gate = sb(ctx, "gate", [P, KD, EXPERTS])
            xnT = sb(ctx, "xnTc", [P, 2, D])
            logits = sb(ctx, "logits", [P, NT, EXPERTS])
            work = sb(ctx, "work", [P, NT, EXPERTS])
            hot = sb(ctx, "hot", [P, TOP, NT, EXPERTS])
            taken = sb(ctx, "taken", [P, NT, EXPERTS])
            top = sb(ctx, "top", [P, TOP, NT])
            best = sb(ctx, "best", [P, NT])
            gap = sb(ctx, "gap", [P, 2, NT])
            strict = sb(ctx, "strict", [P, P])
            total = sb(ctx, "total", [P, EXPERTS, NT])
            upto = sb(ctx, "upto", [P, EXPERTS, NT])
            resets = sb(ctx, "resets", [P, EXPERTS, NT])
            reverse_i = sb(ctx, "reverse_i", [P, EXPERTS], I32)
            reverse = sb(ctx, "reverse", [P, EXPERTS])
            tiles_i = sb(ctx, "tiles_i", [P, 2, EXPERTS], I32)
            tiles_f = sb(ctx, "tiles_f", [P, 4, EXPERTS])
            past = sb(ctx, "past", [1, TILES, EXPERTS])
            past_sum = sb(ctx, "past_sum", [1, TILES])
            slot_f = sb(ctx, "slot_f", [P, NT])
            slot_i = sb(ctx, "slot_i", [P, 3, NT], I32)
            slot_h = sb(ctx, "slot_h", [P, 2, NT], BF16)
            iota_h = sb(ctx, "iota_h", [P, P], BF16)
            tile_h = sb(ctx, "tile_h", [P, NT], BF16)
            low = sb(ctx, "low", [P, NT, P], BF16)
            high = sb(ctx, "high", [P, NT, 2, TILES], BF16)
            listed = sb(ctx, "listed", [P, 6, TILES])
            valid = sb(ctx, "valid", [P, NT])
            b1_sb = sb(ctx, "b1_sb", [EXPERTS * FC, P])
            psT = [ps(ctx, f"psTc{i}") for i in range(2)]
            psL = [ps(ctx, f"psLc{i}") for i in range(2)]
            HALF = (NT + 1) // 2
            psR = [ps(ctx, f"psRc{i}") for i in range(2)]
            psN = [ps(ctx, f"psNc{i}") for i in range(2)]
            block = ctx.enter_context(nc.Block())

            @block.sync
            def _(sp):
                for c in range(KD):
                    sp.dma_start(gate[:, c, :], gate_w[c * P:(c + 1) * P, :]).then_inc(c_gate, 16)
                sp.dma_start(b1_sb[:, :], b1.rearrange("e (c f) -> (e c) f", f=P)).then_inc(c_b1, 16)
                sp.dma_start(b2_sb[:, :], b2).then_inc(c_b2, 16)

                def save(t, s, r):
                    sp.wait_ge(c_xn, t + 1)
                    sp.dma_start(norm_rows[bass.ds(t * P, P), :], xn[:, s, :]).then_inc(c_saved[s], 16)
                pipeline(sp, NT, 4, 0, [(save, 0)])
                sp.wait_ge(c_b2, 16)
                for s in range(4):
                    sp.wait_ge(c_saved[s], 16 * len(range(s, NT, 4)))

            @block.gpsimd
            def _(pool):
                nc.gpsimd.iota(reverse_i[:, :], [[-1, EXPERTS]], base=EXPERTS, channel_multiplier=0).then_inc(c_iota, 1)
                nc.gpsimd.memset(valid[:, :], 1.0).then_inc(c_valid, 1)
                pool.wait_ge(c_valid, 1)
                nc.gpsimd.affine_select(out=valid[:, NT - 1:NT], in_=valid[:, NT - 1:NT], compare_op=ALU.is_ge, fill=0.0,
                                        base=REST - 1, pattern=[[0, 1]], channel_multiplier=-1).then_inc(c_iota, 1)
                nc.gpsimd.affine_select(out=strict[:, :], in_=ones[:, :], compare_op=ALU.is_gt, fill=0.0,
                                        base=0, pattern=[[1, P]], channel_multiplier=-1).then_inc(c_strict, 1)

            @block.scalar
            def _(act):
                act.wait_ge(c_var, 1)
                nc.scalar.activation(rstd[:, :], ln_tmp[:, 0, :], ACT.Sqrt, bias=eps_col[:, 0:1]).then_inc(c_root, 1)

                def copy_xT(t, s, r):
                    act.wait_ge(c_xT_ps, t + 1)
                    if not early(t, 2):
                        act.wait_ge(c_log_ps, t - 1)
                    nc.scalar.copy(xnT[:, s % 2, :], psT[s % 2][:, 0:D]).then_inc(c_xT, 1)

                def keep(t, s, r):
                    act.wait_ge(c_xn, t + 1)
                    nc.scalar.copy(acc[:, bass.ds(t, 1), 0:D].rearrange("p o c -> p (o c)"), xn[:, s, :]).then_inc(c_kept, 1)
                pipeline(act, NT, 4, 2, [(copy_xT, 0), (keep, 0)])
                act.wait_ge(c_gap, 1)
                nc.scalar.activation(gap[:, 1, :], gap[:, 0, :], ACT.Exp).then_inc(c_exp, 1)

            @block.tensor
            def _(pe):
                pe.wait_ge(c_gate, 16 * KD)

                def transpose(t, s, r):
                    pe.wait_ge(c_xn, t + 1)
                    if not early(t, 2):
                        pe.wait_ge(c_xT, t - 1)
                    for c in range(KD):
                        last = nc.tensor.transpose(psT[s % 2][:, c * P:(c + 1) * P], xn[:, s, c * P:(c + 1) * P], ident[:, :])
                    last.then_inc(c_xT_ps, 1)

                def logit(t, s, r):
                    pe.wait_ge(c_xT, t + 1)
                    if not early(t, 2):
                        pe.wait_ge(c_log, t - 1)
                    for c in range(KD):
                        last = nc.tensor.matmul(psL[s % 2][:, 0:EXPERTS], xnT[:, s % 2, c * P:(c + 1) * P], gate[:, c, :],
                                                start=c == 0, stop=c == KD - 1)
                    last.then_inc(c_log_ps, 1)
                pipeline(pe, NT, 4, 3, [(transpose, 0), (logit, 1)])
                pe.wait_ge(c_b1, 16)
                pe.wait_ge(c_xT, NT)
                nc.tensor.transpose(psT[0][:, 0:EXPERTS * FC], b1_sb[:, :], ident[0:EXPERTS * FC, 0:EXPERTS * FC]).then_inc(c_b1_ps, 1)
                pe.wait_ge(c_strict, 1)
                pe.wait_ge(c_taken, 1)
                for i, (lo, hi) in enumerate(((0, HALF), (HALF, NT))):
                    rhs = taken[:, lo:hi, :].rearrange("p t e -> p (t e)")
                    nc.tensor.matmul(psR[i][:, 0:(hi - lo) * EXPERTS], strict[:, :], rhs, start=True, stop=True).then_inc(c_rank, 1)
                    nc.tensor.matmul(psN[i][:, 0:(hi - lo) * EXPERTS], ones[:, :], rhs, start=True, stop=True).then_inc(c_rank, 1)
                for k in range(TOP):
                    pe.wait_ge(c_high, k + 1)

                    def place(t, start, stop):
                        return nc.tensor.matmul(psL[k][:, 0:2 * TILES], low[:, bass.ds(t, 1), :].rearrange("p o f -> p (o f)"),
                                                high[:, bass.ds(t, 1), :, :].rearrange("p o a j -> p (o a j)"),
                                                start=start, stop=stop)
                    place(0, True, False)
                    with pe.Fori(0, (NT - 2) // 4) as r:
                        for u in range(4):
                            place(r * 4 + 1 + u, False, False)
                    for t in range(1 + (NT - 2) // 4 * 4, NT - 1):
                        place(t, False, False)
                    place(NT - 1, False, True).then_inc(c_listed, 1)

            @block.vector
            def _(dve):
                step = stepper(dve, c_vstep)
                step(nc.vector.tensor_scalar(rden[:, :, :], acc[:, :, D:ROW], TINY, None, ALU.max))
                step(nc.vector.reciprocal(rden[:, :, :], rden[:, :, :]))
                sums = acc[:, :, 0:D].rearrange("p t (h d) -> p t h d", h=HEADS)
                step(nc.vector.tensor_tensor(sums, sums, over(rden[:, :, :].unsqueeze(3), [P, NT, HEADS, DH]), ALU.mult))
                step(nc.vector.tensor_tensor(xs[:, :, :], xs[:, :, :], acc[:, :, 0:D], ALU.add))

                def tile_stats(t, s, r):
                    nc.vector.bn_stats(stats[:, bass.ds(t, 1), :].rearrange("p o s -> p (o s)"),
                                       xs[:, bass.ds(t, 1), :].rearrange("p o c -> p (o c)")).then_inc(c_stats, 1)
                pipeline(dve, NT, 8, 1, [(tile_stats, 0)])
                dve.wait_ge(c_stats, NT)
                bulk_rstd(step, c_var)
                dve.wait_ge(c_root, 1)
                step(nc.vector.reciprocal(rstd[:, :], rstd[:, :]))

                def norm(t, s, r):
                    if not early(t, 4):
                        dve.wait_ge(c_xT_ps, t - 3)
                        dve.wait_ge(c_kept, t - 3)
                        dve.wait_ge(c_saved[s], 16 * r)
                    nc.vector.tensor_scalar(xn[:, s, :], xs[:, bass.ds(t, 1), :].rearrange("p o c -> p (o c)"),
                                            mean[:, bass.ds(t, 1)], rstd[:, bass.ds(t, 1)],
                                            ALU.subtract, ALU.mult).then_inc(c_xn, 1)

                def keep_logit(t, s, r):
                    dve.wait_ge(c_log_ps, t + 1)
                    nc.vector.tensor_tensor(logits[:, bass.ds(t, 1), :].rearrange("p o e -> p (o e)"), psL[s % 2][:, 0:EXPERTS],
                                            rows_bc[:, 4 * D:], ALU.add).then_inc(c_log, 1)
                pipeline(dve, NT, 4, 6, [(norm, 0), (keep_logit, 2)])
                dve.wait_ge(c_log, NT)

                dve.wait_ge(c_iota, 2)
                step(nc.vector.tensor_copy(reverse[:, :], reverse_i[:, :]))
                step(nc.vector.tensor_copy(iota_h[:, :], iota_f[:, 0:P]))
                step(nc.vector.tensor_scalar(tile_h[:, :], iota_f[:, 0:NT], 1.0, None, ALU.add))
                rev = over(reverse[:, :].unsqueeze(1), [P, NT, EXPERTS])
                wide = [P, NT, EXPERTS]
                for k in range(TOP):
                    step(nc.vector.tensor_reduce(top[:, k, :], logits[:, :, :], AX.X, ALU.max))
                    step(nc.vector.tensor_tensor(work[:, :, :], logits[:, :, :], over(top[:, k, :].unsqueeze(2), wide), ALU.is_equal))
                    step(nc.vector.tensor_tensor(work[:, :, :], work[:, :, :], rev, ALU.mult))
                    step(nc.vector.tensor_reduce(best[:, :], work[:, :, :], AX.X, ALU.max))
                    step(nc.vector.tensor_tensor(hot[:, k, :, :], rev, over(best[:, :].unsqueeze(2), wide), ALU.is_equal))
                    if k < TOP - 1:
                        step(nc.vector.scalar_tensor_tensor(out=logits[:, :, :], in0=hot[:, k, :, :], scalar=-FAR,
                                                            in1=logits[:, :, :], op0=ALU.mult, op1=ALU.add))
                nc.vector.tensor_tensor(gap[:, 0, :], top[:, 1, :], top[:, 0, :], ALU.subtract).then_inc(c_gap, 1)
                step(nc.vector.tensor_tensor(taken[:, :, :], hot[:, 0, :, :], hot[:, 1, :, :], ALU.add))
                nc.vector.tensor_tensor(taken[:, :, :], taken[:, :, :], over(valid[:, :].unsqueeze(2), wide), ALU.mult).then_inc(c_taken, 1)
                dve.wait_ge(c_exp, 1)
                step(nc.vector.tensor_scalar(gap[:, 0, :], gap[:, 1, :], 1.0, None, ALU.add))
                step(nc.vector.reciprocal(share[:, 0, :], gap[:, 0, :]))
                step(nc.vector.tensor_tensor(share[:, 1, :], gap[:, 1, :], share[:, 0, :], ALU.mult))
                step(nc.vector.tensor_tensor(work[:, :, :], hot[:, 0, :, :], over(share[:, 0, :].unsqueeze(2), wide), ALU.mult))
                step(nc.vector.tensor_tensor(dense[:, :, :], hot[:, 1, :, :], over(share[:, 1, :].unsqueeze(2), wide), ALU.mult))
                step(nc.vector.tensor_tensor(dense[:, :, :], dense[:, :, :], work[:, :, :], ALU.add))
                dve.wait_ge(c_b1_ps, 1)
                step(nc.vector.tensor_copy(b1T[:, :, :].rearrange("p e c -> p (e c)"), psT[0][:, 0:EXPERTS * FC]))

                step(nc.vector.memset(resets[:, :, :], 1.0))
                step(nc.vector.memset(resets[:, :, 0:1], 0.0))
                dve.wait_ge(c_rank, 4)
                for i, (lo, hi) in enumerate(((0, HALF), (HALF, NT))):
                    step(nc.vector.tensor_copy(total[:, :, lo:hi],
                                               psN[i][:, 0:(hi - lo) * EXPERTS].rearrange("p (t e) -> p e t", e=EXPERTS)))
                flat = "p e t -> p (e t)"
                step(nc.vector.tensor_tensor_scan(upto[:, :, :].rearrange(flat), resets[:, :, :].rearrange(flat),
                                                  total[:, :, :].rearrange(flat), 0.0, ALU.mult, ALU.add))
                step(nc.vector.tensor_tensor(total[:, :, :], upto[:, :, :], total[:, :, :], ALU.subtract))
                shift = P.bit_length() - 1
                step(nc.vector.tensor_scalar(tiles_i[:, 0, :], upto[:, :, NT - 1], float(P - 1), None, ALU.add))
                step(nc.vector.tensor_scalar(tiles_i[:, 1, :], tiles_i[:, 0, :], shift, None, ALU.arith_shift_right))
                step(nc.vector.tensor_copy(tiles_f[:, 0, :], tiles_i[:, 1, :]))
                step(nc.vector.tensor_tensor_scan(tiles_f[:, 1, :], ones[:, 0:EXPERTS], tiles_f[:, 0, :], 0.0, ALU.mult, ALU.add))
                step(nc.vector.tensor_tensor(tiles_f[:, 2, :], tiles_f[:, 1, :], tiles_f[:, 0, :], ALU.subtract))
                step(nc.vector.tensor_scalar(tiles_f[:, 3, :], tiles_f[:, 2, :], float(P), None, ALU.mult))
                step(nc.vector.tensor_tensor(total[:, :, :], total[:, :, :], over(tiles_f[:, 3, :].unsqueeze(2), [P, EXPERTS, NT]), ALU.add))
                for i, (lo, hi) in enumerate(((0, HALF), (HALF, NT))):
                    step(nc.vector.tensor_tensor(work[:, lo:hi, :], total[:, :, lo:hi].rearrange("p e t -> p t e"),
                                                 psR[i][:, 0:(hi - lo) * EXPERTS].rearrange("p (t e) -> p t e", e=EXPERTS), ALU.add))
                step(nc.vector.tensor_scalar(valid[:, :], valid[:, :], -float(NOWHERE), float(NOWHERE), ALU.mult, ALU.add))
                for k in range(TOP):
                    step(nc.vector.tensor_tensor(logits[:, :, :], work[:, :, :], hot[:, k, :, :], ALU.mult))
                    step(nc.vector.tensor_reduce(slot_f[:, :], logits[:, :, :], AX.X, ALU.add))
                    step(nc.vector.tensor_tensor(slot_i[:, 0, :], slot_f[:, :], valid[:, :], ALU.add))
                    step(nc.vector.tensor_scalar(slot_i[:, 1, :], slot_i[:, 0, :], P - 1, None, ALU.bitwise_and))
                    step(nc.vector.tensor_scalar(slot_i[:, 2, :], slot_i[:, 0, :], shift, None, ALU.arith_shift_right))
                    step(nc.vector.tensor_copy(slot_h[:, :, :], slot_i[:, 1:3, :]))
                    if k:
                        dve.wait_ge(c_listed, k)
                    step(nc.vector.tensor_tensor(low[:, :, :], over(iota_h[:, :].unsqueeze(1), [P, NT, P]),
                                                 over(slot_h[:, 0, :].unsqueeze(2), [P, NT, P]), ALU.is_equal))
                    tall = [P, NT, TILES]
                    step(nc.vector.tensor_tensor(high[:, :, 1, :], over(iota_h[:, 0:TILES].unsqueeze(1), tall),
                                                 over(slot_h[:, 1, :].unsqueeze(2), tall), ALU.is_equal))
                    step(nc.vector.tensor_tensor(high[:, :, 0, :], high[:, :, 1, :], over(tile_h[:, :].unsqueeze(2), tall), ALU.mult))
                    nc.vector.tensor_scalar(high[:, :, 1, :], high[:, :, 1, :], iota_p[:, 0:1], None, ALU.mult).then_inc(c_high, 1)
                long = [1, TILES, EXPERTS]
                step(nc.vector.tensor_tensor(past[:, :, :], over(iota_f[0:1, 0:TILES].unsqueeze(2), long),
                                             over(tiles_f[0:1, 1, :].unsqueeze(1), long), ALU.is_ge))
                step(nc.vector.tensor_reduce(past_sum[:, :], past[:, :, :], AX.X, ALU.add))
                step(nc.vector.tensor_scalar(tile_expert[:, :], past_sum[:, :], float(EXPERTS - 1), None, ALU.min))
                dve.wait_ge(c_listed, TOP)
                for k in range(TOP):
                    step(nc.vector.tensor_copy(listed[:, 2 * k:2 * k + 2, :].rearrange("p a j -> p (a j)"), psL[k][:, 0:2 * TILES]))
                first_t, first_p, second_t, second_p = (listed[:, i, :] for i in range(4))
                token, target = listed[:, 4, :], listed[:, 5, :]
                step(nc.vector.tensor_tensor(token, first_t, second_t, ALU.add))
                step(nc.vector.tensor_scalar(target, token, 0.0, None, ALU.is_equal))
                step(nc.vector.tensor_scalar(token, token, float(P), -float(P), ALU.mult, ALU.add))
                step(nc.vector.tensor_tensor(token, token, first_p, ALU.add))
                step(nc.vector.tensor_tensor(token, token, second_p, ALU.add))
                step(nc.vector.tensor_scalar(token, token, 0.0, None, ALU.max))
                step(nc.vector.tensor_copy(slot_ends[:, :, 0], token))
                step(nc.vector.tensor_scalar(first_t, iota_f[:, 0:TILES], float(P), iota_p[:, 0:1], ALU.mult, ALU.add))
                step(nc.vector.tensor_scalar(first_t, first_t, float(TOP * NT * P), None, ALU.add))
                step(nc.vector.tensor_tensor(target, target, first_t, ALU.mult))
                step(nc.vector.tensor_scalar(second_t, second_t, 0.0, float(NT * P), ALU.is_gt, ALU.mult))
                step(nc.vector.tensor_tensor(target, target, second_t, ALU.add))
                step(nc.vector.tensor_tensor(slot_ends[:, :, 1], target, token, ALU.add))

        DR = 4
        d_w = [sem(f"d_w{i}") for i in range(DR)]; d_rows = [sem(f"d_rows{i}") for i in range(DR)]
        d_stored = [sem(f"d_stored{i}") for i in range(DR)]; d_src = sem("d_src"); d_dst = sem("d_dst")
        d_xT_ps = sem("d_xT_ps"); d_xT = sem("d_xT"); d_up = sem("d_up"); d_hid = sem("d_hid")
        d_down = sem("d_down"); d_y = sem("d_y"); d_apart = sem("d_apart")
        with ExitStack() as ctx:
            w1_sb = sb(ctx, "w1_sb", [P, DR, KD, F])
            w2_sb = sb(ctx, "w2_sb", [P, DR, FC, D])
            rows_sb = sb(ctx, "rows_sb", [P, DR, D])
            src_sb = sb(ctx, "src_sb", [P, DR, 1], I32)
            dst_sb = sb(ctx, "dst_sb", [P, DR, 1], I32)
            xT = sb(ctx, "xT", [P, DR, KD, P])
            hid = sb(ctx, "hid", [P, DR, FC, P])
            y_sb = sb(ctx, "y_sb", [P, DR, D])
            psX = [ps(ctx, f"psXd{i}") for i in range(2)]
            psH = [ps(ctx, f"psHd{i}") for i in range(2)]
            psY = [ps(ctx, f"psYd{i}") for i in range(2)]
            block = ctx.enter_context(nc.Block())
            w1_v = w1.rearrange("e (c p) f -> (e c p) f", p=P)
            w2_v = w2.rearrange("e (c p) f -> (e c p) f", p=P)

            @block.sync
            def _(sp):
                def load(j, s, r):
                    e = sp.value_load(tile_expert[0:1, bass.ds(j, 1)], min_val=0, max_val=EXPERTS - 1)
                    if not early(j, DR):
                        sp.wait_ge(d_down, j - DR + 1)
                    sp.dma_start(w1_sb[:, s, :, :], w1_v[bass.ds(e * D, D), :].rearrange("(c p) f -> p c f", p=P)).then_inc(d_w[s], 16)
                    sp.dma_start(w2_sb[:, s, :, :], w2_v[bass.ds(e * F, F), :].rearrange("(c p) f -> p c f", p=P)).then_inc(d_w[s], 16)
                pipeline(sp, TILES, DR, DR, [(load, 0)])

            @block.gpsimd
            def _(pool):
                def fetch(j, s, r):
                    if not early(j, DR):
                        pool.wait_ge(d_xT_ps, j - DR + 1)
                    pool.wait_ge(d_src, j + 1)
                    pool.sem_inc(d_apart, 1)
                    nc.gpsimd.indirect_dma_start(rows_sb[:, s, :], None, norm_rows,
                                                 bass.IndirectOffsetOnAxis(ap=src_sb[:, s, :], axis=0)).then_inc(d_rows[s], 16)

                def put(j, s, r):
                    pool.wait_ge(d_y, j + 1)
                    pool.wait_ge(d_dst, j + 1)
                    pool.sem_inc(d_apart, 1)
                    nc.gpsimd.indirect_dma_start(pair_rows, bass.IndirectOffsetOnAxis(ap=dst_sb[:, s, :], axis=0),
                                                 y_sb[:, s, :], None).then_inc(d_stored[s], 16)
                pipeline(pool, TILES, DR, DR, [(fetch, 0), (put, DR)])
                for s in range(DR):
                    pool.wait_ge(d_stored[s], 16 * len(range(s, TILES, DR)))

            @block.tensor
            def _(pe):
                def transpose(j, s, r):
                    pe.wait_ge(d_rows[s], 16 * (r + 1))
                    if not early(j, 2):
                        pe.wait_ge(d_xT, j - 1)
                    for c in range(KD):
                        last = nc.tensor.transpose(psX[s % 2][:, c * P:(c + 1) * P], rows_sb[:, s, c * P:(c + 1) * P], ident[:, :])
                    last.then_inc(d_xT_ps, 1)

                def up(j, s, r):
                    pe.wait_ge(d_w[s], 32 * (r + 1))
                    pe.wait_ge(d_xT, j + 1)
                    if not early(j, 2):
                        pe.wait_ge(d_hid, j - 1)
                    for f in range(FC):
                        for c in range(KD):
                            last = nc.tensor.matmul(psH[s % 2][:, f * P:(f + 1) * P], w1_sb[:, s, c, f * P:(f + 1) * P],
                                                    xT[:, s, c, :], start=c == 0, stop=c == KD - 1)
                    last.then_inc(d_up, 1)

                def down(j, s, r):
                    pe.wait_ge(d_hid, j + 1)
                    if not early(j, 2):
                        pe.wait_ge(d_y, j - 1)
                    for f in range(FC):
                        last = nc.tensor.matmul(psY[s % 2][:, 0:D], hid[:, s, f, :], w2_sb[:, s, f, :],
                                                start=f == 0, stop=f == FC - 1)
                    last.then_inc(d_down, 1)
                pipeline(pe, TILES, DR, 4, [(transpose, 0), (up, 1), (down, 2)])

            @block.scalar
            def _(act):
                def relu(j, s, r):
                    e = act.value_load(tile_expert[0:1, bass.ds(j, 1)], min_val=0, max_val=EXPERTS - 1)
                    act.wait_ge(d_up, j + 1)
                    if not early(j, DR):
                        act.wait_ge(d_down, j - DR + 1)
                    for f in range(FC):
                        last = nc.scalar.activation(hid[:, s, f, :], psH[s % 2][:, f * P:(f + 1) * P], ACT.Relu,
                                                    bias=b1T[:, bass.ds(e, 1), f:f + 1].rearrange("p o f -> p (o f)"))
                    last.then_inc(d_hid, 1)
                pipeline(act, TILES, DR, DR, [(relu, 0)])

            @block.vector
            def _(dve):
                def copy_src(j, s, r):
                    if not early(j, DR):
                        dve.wait_ge(d_rows[s], 16 * r)
                    nc.vector.tensor_copy(src_sb[:, s, :], slot_ends[:, bass.ds(j, 1), 0]).then_inc(d_src, 1)

                def copy_dst(j, s, r):
                    if not early(j, DR):
                        dve.wait_ge(d_stored[s], 16 * r)
                    nc.vector.tensor_copy(dst_sb[:, s, :], slot_ends[:, bass.ds(j, 1), 1]).then_inc(d_dst, 1)

                def copy_xT(j, s, r):
                    dve.wait_ge(d_xT_ps, j + 1)
                    if not early(j, DR):
                        dve.wait_ge(d_up, j - DR + 1)
                    nc.vector.tensor_copy(xT[:, s, :, :].rearrange("p c t -> p (c t)"), psX[s % 2][:, 0:D]).then_inc(d_xT, 1)

                def copy_y(j, s, r):
                    dve.wait_ge(d_down, j + 1)
                    nc.vector.tensor_copy(y_sb[:, s, :], psY[s % 2][:, 0:D]).then_inc(d_y, 1)
                pipeline(dve, TILES, DR, DR + 6, [(copy_src, 0), (copy_xT, 3), (copy_dst, 6), (copy_y, 6)])

        ER = 8
        e_got = [sem(f"e_got{i}") for i in range(ER)]
        e_dT_ps = sem("e_dT_ps"); e_dT = sem("e_dT"); e_base = sem("e_base"); e_sum = sem("e_sum"); e_fin = sem("e_fin")
        e_dv = sem("e_dv"); e_var = sem("e_var"); e_root = sem("e_root"); e_n = sem("e_n"); e_y = sem("e_y")
        e_tail = sem("e_tail"); e_gam = sem("e_gam"); e_apart = sem("e_apart"); e_out = [sem(f"e_out{i}") for i in range(ER)]
        with ExitStack() as ctx:
            got = sb(ctx, "got", [P, ER, TOP, D])
            denseT = sb(ctx, "denseT", [EXPERTS, 2, P])
            dcol = sb(ctx, "dcol", [P, 2, EXPERTS])
            y = sb(ctx, "y", [P, ER, D])
            mv = sb(ctx, "mv", [P, ER, 12])
            psD = [ps(ctx, f"psDe{i}") for i in range(2)]
            psB = [ps(ctx, f"psBe{i}") for i in range(2)]
            psX = [ps(ctx, f"psXe{i}") for i in range(2)]
            block = ctx.enter_context(nc.Block())

            @block.tensor
            def _(pe):
                def transpose(t, s, r):
                    pe.wait_ge(e_dv, t + 1)
                    if not early(t, 2):
                        pe.wait_ge(e_dT, t - 1)
                    nc.tensor.transpose(psD[s % 2][0:EXPERTS, 0:P], dcol[:, s % 2, :], ident[:, :]).then_inc(e_dT_ps, 1)

                def base(t, s, r):
                    pe.wait_ge(e_dT, t + 1)
                    if not early(t, 2):
                        pe.wait_ge(e_sum, 3 * t - 5)
                    nc.tensor.matmul(psB[s % 2][:, 0:D], denseT[:, s % 2, :], b2_sb[:, :], start=True, stop=False)
                    nc.tensor.matmul(psB[s % 2][:, 0:D], ident[:, :], acc[:, bass.ds(t, 1), 0:D].rearrange("p o c -> p (o c)"),
                                     start=False, stop=True).then_inc(e_base, 1)

                def tail(t, s, r):
                    if not early(t, 2):
                        pe.wait_ge(e_y, t - 1)
                    nc.tensor.matmul(psX[s % 2][:, 0:D], ones[0:1, :], rows_bc[0:1, 3 * D:4 * D], start=True, stop=False)
                    nc.tensor.matmul(psX[s % 2][:, 0:D], ident[:, :], xs[:, bass.ds(t, 1), :].rearrange("p o c -> p (o c)"),
                                     start=False, stop=True).then_inc(e_tail, 1)
                pipeline(pe, NT, ER, 8, [(transpose, 0), (base, 1), (tail, 2)])

            @block.scalar
            def _(act):
                def copy_dT(t, s, r):
                    act.wait_ge(e_dT_ps, t + 1)
                    if not early(t, 2):
                        act.wait_ge(e_base, t - 1)
                    nc.scalar.copy(denseT[:, s % 2, :], psD[s % 2][0:EXPERTS, 0:P]).then_inc(e_dT, 1)

                def root(t, s, r):
                    act.wait_ge(e_var, t + 1)
                    nc.scalar.activation(mv[:, s, 8:9], mv[:, s, 7:8], ACT.Sqrt, bias=eps_col[:, 0:1]).then_inc(e_root, 1)

                def normalize(t, s, r):
                    act.wait_ge(e_fin, 2 * t + 2)
                    nc.scalar.activation(y[:, s, :], y[:, s, :], ACT.Identity, bias=mv[:, s, 10:11], scale=mv[:, s, 9:10]).then_inc(e_n, 1)
                pipeline(act, NT, ER, 8, [(copy_dT, 0), (root, 2), (normalize, 3)])

            @block.vector
            def _(dve):
                def column(t, s, r):
                    if not early(t, 2):
                        dve.wait_ge(e_dT_ps, t - 1)
                    nc.vector.tensor_copy(dcol[:, s % 2, :], dense[:, bass.ds(t, 1), :].rearrange("p o e -> p (o e)")).then_inc(e_dv, 1)

                def combine(t, s, r):
                    dve.wait_ge(e_got[s], 16 * TOP * (r + 1))
                    dve.wait_ge(e_base, t + 1)
                    if not early(t, ER):
                        dve.wait_ge(e_out[s], 16 * r)
                    nc.vector.scalar_tensor_tensor(out=y[:, s, :], in0=got[:, s, 0, :], scalar=share[:, 0, bass.ds(t, 1)],
                                                   in1=psB[s % 2][:, 0:D], op0=ALU.mult, op1=ALU.add).then_inc(e_sum, 1)
                    dve.wait_ge(e_sum, 3 * t + 1)
                    nc.vector.scalar_tensor_tensor(out=y[:, s, :], in0=got[:, s, 1, :], scalar=share[:, 1, bass.ds(t, 1)],
                                                   in1=y[:, s, :], op0=ALU.mult, op1=ALU.add).then_inc(e_sum, 1)
                    dve.wait_ge(e_sum, 3 * t + 2)
                    nc.vector.bn_stats(mv[:, s, 0:6], y[:, s, :]).then_inc(e_sum, 1)
                    dve.wait_ge(e_sum, 3 * t + 3)
                    dve.sem_inc(e_apart, 1)
                    nc.vector.bn_aggr(mv[:, s, 6:8], mv[:, s, 0:6]).then_inc(e_var, 1)

                def scales(t, s, r):
                    dve.wait_ge(e_root, t + 1)
                    nc.vector.reciprocal(mv[:, s, 9:10], mv[:, s, 8:9]).then_inc(e_fin, 1)
                    dve.wait_ge(e_fin, 2 * t + 1)
                    nc.vector.scalar_tensor_tensor(out=mv[:, s, 10:11], in0=mv[:, s, 6:7], scalar=-1.0, in1=mv[:, s, 9:10],
                                                   op0=ALU.mult, op1=ALU.mult).then_inc(e_fin, 1)

                def finish(t, s, r):
                    dve.wait_ge(e_n, t + 1)
                    nc.vector.tensor_tensor(y[:, s, :], y[:, s, :], rows_bc[:, 2 * D:3 * D], ALU.mult).then_inc(e_gam, 1)
                    dve.wait_ge(e_gam, t + 1)
                    dve.wait_ge(e_tail, t + 1)
                    nc.vector.tensor_tensor(y[:, s, :], y[:, s, :], psX[s % 2][:, 0:D], ALU.add).then_inc(e_y, 1)
                pipeline(dve, NT, ER, ER + 1, [(column, 0), (combine, 1), (scales, 2), (finish, 3)])

            @block.sync
            def _(sp):
                def load(t, s, r):
                    if not early(t, ER):
                        sp.wait_ge(e_sum, 3 * (t - ER) + 2)
                    n = REST if isinstance(t, int) and t == NT - 1 else P
                    for k in range(TOP):
                        sp.dma_start(got[0:n, s, k, :], pair_rows[bass.ds(t * P + k * NT * P, n), :]).then_inc(e_got[s], 16)

                def store(t, s, r):
                    sp.wait_ge(e_y, t + 1)
                    if isinstance(t, int) and t == NT - 1:
                        sp.dma_start(out[(NT - 1) * P:N, :], y[0:REST, s, :]).then_inc(e_out[s], 16)
                    else:
                        sp.dma_start(out[bass.ds(t * P, P), :], y[:, s, :]).then_inc(e_out[s], 16)
                pipeline(sp, NT, ER, ER, [(load, 0), (store, 5)])
                for s in range(ER):
                    sp.wait_ge(e_out[s], 16 * len(range(s, NT, ER)))


_INS = ['x', 'src', 'dst', 'L0_gnn_W', 'L0_gnn_a_src', 'L0_gnn_a_dst', 'L0_ffn_gate_w', 'L0_ffn_gate_b',
        'L0_ffn_w1', 'L0_ffn_b1', 'L0_ffn_w2', 'L0_ffn_b2', 'L0_ffn_gamma', 'L0_ffn_beta']


def kernel(**inputs):
    import numpy as _np
    import concourse.bacc as _bacc
    from concourse import mybir as _mybir
    from concourse.bass_utils import run_bass_kernel_spmd as _run

    nc = _bacc.Bacc("TRN2", target_bir_lowering=False, num_devices=1)
    arrays, args = {}, []
    for name in _INS:
        a = _np.ascontiguousarray(inputs[name])
        arrays[f"in_{name}_dram"] = a
        args.append(nc.dram_tensor(f"in_{name}_dram", a.shape, _mybir.dt.from_np(a.dtype), kind="ExternalInput").ap())
    out = nc.dram_tensor("out_0_dram", inputs["x"].shape, _mybir.dt.float32, kind="ExternalOutput").ap()
    gnn_moe_kernel(nc, *args, out)
    r = _run(nc, [arrays], core_ids=[0])
    return r.results[0]["out_0_dram"]
```

```python
from contextlib import ExitStack

import concourse.bass as bass
from concourse import mybir

F32 = mybir.dt.float32
I32 = mybir.dt.int32
BF16 = mybir.dt.bfloat16
ALU = mybir.AluOpType
ACT = mybir.ActivationFunctionType
AX = mybir.AxisListType
RMAX = bass.bass_isa.ReduceOp.max

P = 128
G = 4
RING = 8
SLOPE = 0.01
EPS = 1e-5
LEVEL = 64.0
DECIDED = 1e-28
PASSES_MAX = 4096
FAR = 1e30
NOWHERE = 1 << 15
MSG_TO_ACC = 2
TINY = 1e-30
PAD_DST = 1 << 20


def pipeline(eng, count, unroll, head, stages, tail=0, rounds=None):
    last = max(lag for _, lag in stages)
    head = -(-head // unroll) * unroll
    counted = rounds is None
    if counted:
        rounds = (count - head - tail) // unroll

    def peeled(i):
        for stage, lag in stages:
            if 0 <= i - lag and (not counted or i - lag < count):
                stage(i - lag, (i - lag) % unroll, (i - lag) // unroll)

    for i in range(head):
        peeled(i)
    with eng.Fori(0, rounds) as r:
        for u in range(unroll):
            for stage, lag in stages:
                at = head + u - lag
                stage(r * unroll + at, at % unroll, r + at // unroll)
    if counted:
        for i in range(head + rounds * unroll, count + last):
            peeled(i)
        return
    for i in range(last):
        for stage, lag in stages:
            if i < lag:
                at = head + i - lag
                stage(rounds * unroll + at, at % unroll, rounds + at // unroll)


def early(item, depth):
    return isinstance(item, int) and item < depth


def gnn_moe_kernel(nc, x, src, dst, W, a_src, a_dst, gate_w, gate_b, w1, b1, w2, b2, gamma, beta, out):
    N, D = x.shape
    E = src.shape[0]
    HEADS, _, DH = W.shape
    EXPERTS, _, F = w1.shape
    TOP = 2
    NT = -(-N // P)
    REST = N - (NT - 1) * P
    KD = D // P
    FC = F // P
    ROW = D + HEADS
    CHUNKS = -(-E // P)
    GROUPS = -(-CHUNKS // G)
    assert GROUPS * G * P > E
    FULL = E // (G * P)
    VISITS = FULL + NT
    BLOCKS = -(-CHUNKS // P)
    FULL_CHUNKS = E // P
    DR, HEAD = 4, 12
    MOST = (N * TOP + EXPERTS * (P - 1)) // P
    TILES = HEAD + -(-(MOST - HEAD) // DR) * DR
    assert N * TOP // P > HEAD

    z_table = nc.dram_tensor("z_table", [NT * P, ROW], F32).ap()
    norm_rows = nc.dram_tensor("norm_rows", [NT * P, D], F32).ap()
    pair_rows = nc.dram_tensor("pair_rows", [(TOP * NT + TILES) * P, D], F32).ap()

    whole = ExitStack()

    def sem(name):
        return whole.enter_context(nc.semaphore(name))

    def sb(ctx, name, shape, dt=F32):
        return ctx.enter_context(nc.sbuf_tensor(name, shape, dt))

    def ps(ctx, name, shape=(P, 512)):
        return ctx.enter_context(nc.psum_tensor(name, list(shape), F32))

    def over(ap, shape):
        return ap.to_broadcast(shape)

    with whole:
        xs = sb(whole, "xs", [P, NT, D])
        ident = sb(whole, "ident", [P, P])
        affine = sb(whole, "affine", [P, 2 * D])
        eps_col = sb(whole, "eps_col", [P, 1])
        share = sb(whole, "share", [P, TOP, NT])
        slot_ends = sb(whole, "slot_ends", [P, TILES, 2], I32)
        tile_expert = sb(whole, "tile_expert", [1, TILES], I32)
        b1T = sb(whole, "b1T", [P, EXPERTS, FC])
        tile_rounds = sb(whole, "tile_rounds", [1, 1], I32)
        attention = whole.enter_context(ExitStack())
        ones = sb(attention, "ones", [P, P])
        iota_p = sb(attention, "iota_p", [P, 1])
        iota_f = sb(attention, "iota_f", [P, 512])
        rows_bc = sb(attention, "rows_bc", [P, 2 * D + EXPERTS])
        mean = sb(attention, "mean", [P, NT])
        rstd = sb(attention, "rstd", [P, NT])
        ln_tmp = sb(attention, "ln_tmp", [P, 2, NT])
        acc = sb(attention, "acc", [P, NT, ROW])
        esed = sb(attention, "esed", [P, NT, 2 * HEADS])
        graph = whole.enter_context(ExitStack())
        src_idx = sb(graph, "src_idx", [P, BLOCKS * P], I32)
        dst_col = sb(graph, "dst_col", [P, BLOCKS * P])
        visit_base = sb(graph, "visit_base", [P, VISITS])
        visit_tile = sb(graph, "visit_tile", [1, VISITS], I32)
        visit_group = sb(graph, "visit_group", [1, VISITS], I32)
        visit_slot = sb(graph, "visit_slot", [1, VISITS], I32)
        visit_word = sb(graph, "visit_word", [1, VISITS], I32)
        group_free = sb(graph, "group_free", [1, GROUPS], I32)

        BULK = 6

        def bulk_rstd(step, stats, at, ready):
            a, b, m = ln_tmp[:, 0, at], ln_tmp[:, 1, at], mean[:, at]
            step(nc.vector.tensor_tensor(m, stats[:, at, 1], stats[:, at, 4], ALU.add))
            step(nc.vector.tensor_scalar(m, m, 0.5, None, ALU.mult))
            step(nc.vector.tensor_tensor(a, stats[:, at, 1], m, ALU.subtract))
            step(nc.vector.tensor_tensor(a, a, a, ALU.mult))
            step(nc.vector.tensor_tensor(b, stats[:, at, 2], stats[:, at, 5], ALU.add))
            nc.vector.scalar_tensor_tensor(out=a, in0=b, scalar=1.0 / D, in1=a, op0=ALU.mult, op1=ALU.add).then_inc(ready, 1)

        def stepper(eng, semaphore, base=0):
            count = [0]

            def step(instruction):
                count[0] += 1
                instruction.then_inc(semaphore, 1)
                eng.wait_ge(semaphore, base + count[0])
            return step

        a_const = sem("a_const"); a_identz = sem("a_identz"); a_padded = sem("a_padded")
        XC = 4
        PART = (NT - 1) // XC
        assert PART % 4 == 0
        a_x = [sem(f"a_x{i}") for i in range(XC + 1)]
        a_edges = sem("a_edges"); a_w = sem("a_w"); a_rows = sem("a_rows"); a_late = sem("a_late"); a_last = sem("a_last")
        a_vstep = sem("a_vstep"); a_bulk = sem("a_bulk"); a_arrived = sem("a_arrived"); a_apart = sem("a_apart")
        a_zeroed = sem("a_zeroed"); a_es = sem("a_es")
        a_edge_f = sem("a_edge_f"); a_edge_ps = sem("a_edge_ps"); a_edge_sb = sem("a_edge_sb")
        a_last_f = sem("a_last_f"); a_last_ps = sem("a_last_ps"); a_ge = sem("a_ge"); a_cnt = sem("a_cnt")
        a_stats = sem("a_stats"); a_var = sem("a_var"); a_root = sem("a_root"); a_waug = sem("a_waug")
        a_xn = sem("a_xn"); a_xT_ps = sem("a_xT_ps"); a_xT = sem("a_xT"); a_z_ps = sem("a_z_ps")
        a_z = sem("a_z"); a_store = [sem(f"a_store{i}") for i in range(4)]
        with ExitStack() as ctx:
            stats = sb(ctx, "stats_a", [P, NT, 6])
            src_raw = sb(ctx, "src_raw", [P, BLOCKS, P], I32)
            dst_raw = sb(ctx, "dst_raw", [P, BLOCKS, P], I32)
            edge_f = sb(ctx, "edge_f", [P, 2, BLOCKS, P])
            wcat = sb(ctx, "wcat", [P, KD, D + 2 * HEADS])
            wprod = sb(ctx, "wprod", [P, D])
            last_i = sb(ctx, "last_i", [1, FULL], I32)
            last_f = sb(ctx, "last_f", [1, FULL])
            iota_i = sb(ctx, "iota_i", [P, 512], I32)
            iota_pi = sb(ctx, "iota_pi", [P, 1], I32)
            below = sb(ctx, "below", [P, 3, 512])
            thr = sb(ctx, "thr", [P, 4])
            xn = sb(ctx, "xn", [P, 4, D])
            xnT = sb(ctx, "xnT", [P, 2, D])
            z_out = sb(ctx, "z_out", [P, 4, D + 2 * HEADS])
            psA = [ps(ctx, f"psA{i}") for i in range(4)]
            psT = [ps(ctx, f"psTa{i}") for i in range(2)]
            psZ = [ps(ctx, f"psZa{i}") for i in range(2)]
            block = ctx.enter_context(nc.Block())
            TABLES, COLUMNS = 1, NT - PART
            EB = [(k, b) for k in range(2) for b in range(0, BLOCKS, 4)]
            assert len(EB) + 2 <= PART

            @block.sync
            def _(sp):
                for c in range(KD):
                    sp.dma_start(wcat[:, c, 0:D].rearrange("p (h d) -> p h d", h=HEADS),
                                 W[:, c * P:(c + 1) * P, :].rearrange("h p d -> p h d")).then_inc(a_w, 16)
                for i in range(XC):
                    sp.dma_start(xs[:, i * PART:(i + 1) * PART, :],
                                 x[i * PART * P:(i + 1) * PART * P].rearrange("(t p) c -> p t c", p=P)).then_inc(a_x[i], 16)
                sp.wait_ge(a_padded, 1)
                sp.dma_start(xs[0:REST, NT - 1, :], x[(NT - 1) * P:N]).then_inc(a_x[XC], 16)
                for i in range(XC + 1):
                    sp.wait_ge(a_x[i], 16)
                    sp.nop().then_inc(a_arrived, 1)

                def store(t, s, r):
                    sp.wait_ge(a_z, t + 1)
                    sp.dma_start(z_table[bass.ds(t * P, P), :], z_out[:, s, 0:ROW]).then_inc(a_store[s], 16)
                pipeline(sp, NT, 4, 0, [(store, 0)])
                for s in range(4):
                    sp.wait_ge(a_store[s], 16 * len(range(s, NT, 4)))

            @block.scalar
            def _(act):
                for i, r in enumerate((a_src, a_dst)):
                    act.dma_start(rows_bc[:, i * D:(i + 1) * D], over(r.rearrange("h d -> (h d)").unsqueeze(0), [P, D])).then_inc(a_rows, 16)
                with nc.allow_non_contiguous_dma("the last destination of each group"):
                    act.dma_start(last_i[:, :], dst[0:FULL * G * P].rearrange("(g f) -> g f", f=G * P)[:, G * P - 1:G * P]
                                  .rearrange("g o -> o g")).then_inc(a_last, 16)
                act.wait_ge(a_padded, 3)
                tail = BLOCKS - 1
                for raw, e in ((src_raw, src), (dst_raw, dst)):
                    act.dma_start(raw[:, 0:tail, :], e[0:tail * P * P].rearrange("(b p f) -> p b f", p=P, f=P)).then_inc(a_edges, 16)
                    n = FULL_CHUNKS - tail * P
                    act.dma_start(raw[0:n, tail, :], e[tail * P * P:FULL_CHUNKS * P].rearrange("(p f) -> p f", f=P)).then_inc(a_edges, 16)
                    if E > FULL_CHUNKS * P:
                        act.dma_start(raw[n:n + 1, tail, 0:E - FULL_CHUNKS * P],
                                      e[FULL_CHUNKS * P:E].unsqueeze(0)).then_inc(a_edges, 16)
                for to, r in ((rows_bc[:, 2 * D:], gate_b), (affine[:, 0:D], gamma), (affine[:, D:2 * D], beta)):
                    act.dma_start(to, over(r.unsqueeze(0), [P, to.shape[-1]])).then_inc(a_late, 16)

                def root(part, at):
                    act.wait_ge(a_var, part + 1)
                    nc.scalar.activation(rstd[:, at], ln_tmp[:, 0, at], ACT.Sqrt, bias=eps_col[:, 0:1]).then_inc(a_root, 1)
                root(0, slice(0, PART))

                def next_root(t, s, r):
                    if s == 8 and not (isinstance(r, int) and r >= XC):
                        part = r + 1
                        root(part, slice(XC * PART, NT) if isinstance(r, int) and r == XC - 1 else bass.ds(part * PART, PART))

                def copy_xT(t, s, r):
                    act.wait_ge(a_xT_ps, t + 1)
                    if not early(t, 2):
                        act.wait_ge(a_z_ps, t - 1)
                    nc.scalar.copy(xnT[:, s % 2, :], psT[s % 2][:, 0:D]).then_inc(a_xT, 1)

                def copy_z(t, s, r):
                    act.wait_ge(a_z_ps, t + 1)
                    if not early(t, 4):
                        at, use = s % 4, r * (PART // 4) + s // 4
                        act.wait_ge(a_store[at], 16 * use)
                        act.wait_ge(a_es, t - 3)
                    nc.scalar.copy(z_out[:, s % 4, :], psZ[s % 2][:, 0:D + 2 * HEADS]).then_inc(a_z, 1)
                pipeline(act, NT, PART, PART, [(next_root, 0), (copy_xT, 0), (copy_z, 1)], tail=PART + 1)

            @block.gpsimd
            def _(pool):
                nc.gpsimd.memset(xs[:, NT - 1, :], 0.0).then_inc(a_padded, 1)
                nc.gpsimd.memset(src_raw[:, BLOCKS - 1, :], 0).then_inc(a_padded, 1)
                nc.gpsimd.memset(dst_raw[:, BLOCKS - 1, :], PAD_DST).then_inc(a_padded, 1)
                nc.gpsimd.memset(ident[:, :], 0.0).then_inc(a_identz, 1)
                nc.gpsimd.memset(ones[:, :], 1.0).then_inc(a_const, 1)
                nc.gpsimd.memset(eps_col[:, :], EPS).then_inc(a_const, 1)
                nc.gpsimd.iota(iota_i[:, :], [[1, 512]], base=0, channel_multiplier=0).then_inc(a_const, 1)
                nc.gpsimd.iota(iota_pi[:, :], [[1, 1]], base=0, channel_multiplier=1).then_inc(a_const, 1)
                pool.wait_ge(a_identz, 1)
                nc.gpsimd.affine_select(out=ident[:, :], in_=ident[:, :], compare_op=ALU.not_equal, fill=1.0,
                                        base=0, pattern=[[-1, P]], channel_multiplier=1).then_inc(a_const, 1)
                pool.wait_ge(a_edges, 16 * (6 if E > FULL_CHUNKS * P else 4))
                for k, raw in enumerate((src_raw, dst_raw)):
                    nc.gpsimd.tensor_copy(edge_f[:, k, :, :], raw[:, :, :]).then_inc(a_edge_f, 1)
                nc.gpsimd.memset(acc[:, :, :], 0.0).then_inc(a_zeroed, 1)
                pool.wait_ge(a_zeroed, 1)

            @block.vector
            def _(dve):
                step = stepper(dve, a_vstep)
                dve.wait_ge(a_const, 5)
                step(nc.vector.tensor_copy(iota_f[:, :], iota_i[:, :]))
                step(nc.vector.tensor_copy(iota_p[:, :], iota_pi[:, :]))
                dve.wait_ge(a_w, 16 * KD)
                dve.wait_ge(a_rows, 16 * 2)
                for c in range(KD):
                    for k in range(2):
                        step(nc.vector.tensor_tensor(wprod[:, :], wcat[:, c, 0:D], rows_bc[:, k * D:(k + 1) * D], ALU.mult))
                        step(nc.vector.tensor_reduce(wcat[:, c, D + k * HEADS:D + (k + 1) * HEADS],
                                                     wprod[:, :].rearrange("p (h d) -> p h d", h=HEADS), AX.X, ALU.add))
                dve.sem_inc(a_waug, 1)

                def tile_stats(t, s, r):
                    nc.vector.bn_stats(stats[:, bass.ds(t, 1), :].rearrange("p o s -> p (o s)"),
                                       xs[:, bass.ds(t, 1), :].rearrange("p o c -> p (o c)")).then_inc(a_stats, 1)

                def invert(part, at, part_step):
                    dve.wait_ge(a_root, part + 1)
                    part_step(nc.vector.reciprocal(rstd[:, at], rstd[:, at]))
                dve.wait_ge(a_arrived, 1)
                for t in range(PART):
                    tile_stats(t, 0, 0)
                dve.wait_ge(a_stats, PART)
                first = slice(0, PART)
                part_step = stepper(dve, a_bulk)
                bulk_rstd(part_step, stats, first, a_var)
                invert(0, first, part_step)

                def norm(t, s, r):
                    if not early(t, 4):
                        dve.wait_ge(a_xT_ps, t - 3)
                    nc.vector.tensor_scalar(xn[:, s % 4, :], xs[:, bass.ds(t, 1), :].rearrange("p o c -> p (o c)"),
                                            mean[:, bass.ds(t, 1)], rstd[:, bass.ds(t, 1)],
                                            ALU.subtract, ALU.mult).then_inc(a_xn, 1)

                def next_part(t, s, r):
                    static = isinstance(r, int)
                    if static and r >= XC:
                        return
                    n = 1 if static and r == XC - 1 else PART
                    at = slice(XC * PART, NT) if n == 1 else bass.ds((r + 1) * PART, PART)
                    if s == 0:
                        dve.wait_ge(a_arrived, r + 2)
                        dve.sem_inc(a_apart, 1)
                    for u in range(s * n // 8, (s + 1) * n // 8) if s < 8 else ():
                        tile_stats((r + 1) * PART + u, 0, 0)
                    if s == 8:
                        dve.wait_ge(a_stats, (r + 1) * PART + n)
                        stepping[0] = stepper(dve, a_bulk, (r + 1) * BULK)
                        bulk_rstd(stepping[0], stats, at, a_var)
                    if s == PART - 1:
                        invert(r + 1, at, stepping[0])
                stepping = [None]

                def copy_es(t, s, r):
                    dve.wait_ge(a_z, t + 1)
                    nc.vector.tensor_copy(esed[:, bass.ds(t, 1), :].rearrange("p o c -> p (o c)"),
                                          z_out[:, s % 4, D:D + 2 * HEADS]).then_inc(a_es, 1)
                def aside(t, s, r):
                    if not isinstance(t, int):
                        return
                    if t == TABLES:
                        dve.wait_ge(a_last, 16)
                        nc.vector.tensor_copy(last_f[:, :], last_i[:, :]).then_inc(a_last_f, 1)
                        step(nc.vector.tensor_scalar(thr[:, 0:1], iota_p[:, :], float(P), float(P), ALU.mult, ALU.add))
                    if t == TABLES + 3:
                        dve.wait_ge(a_last_ps, 1)
                        step(nc.vector.tensor_scalar(below[:, 2, 0:FULL], psA[0][:, 0:FULL], thr[:, 0:1], None, ALU.is_lt))
                        step(nc.vector.tensor_reduce(thr[:, 1:2], below[:, 2, 0:FULL], AX.X, ALU.add))
                        step(nc.vector.scalar_tensor_tensor(out=thr[:, 2:3], in0=iota_p[:, :], scalar=1.0, in1=thr[:, 1:2], op0=ALU.add, op1=ALU.add))
                        nc.vector.tensor_scalar(below[:, 0, 0:VISITS], iota_f[:, 0:VISITS], thr[:, 2:3], None, ALU.is_ge).then_inc(a_ge, 1)
                        nc.vector.tensor_scalar(below[:, 1, 0:GROUPS], iota_f[:, 0:GROUPS], thr[:, 1:2], None, ALU.is_gt).then_inc(a_ge, 1)
                    if t == TABLES + 6:
                        dve.wait_ge(a_cnt, 2)
                        step(nc.vector.tensor_scalar(visit_base[:, :], psA[1][:, 0:VISITS], -float(P), None, ALU.mult))
                        step(nc.vector.tensor_copy(visit_tile[:, :], psA[1][0:1, 0:VISITS]))
                        step(nc.vector.scalar_tensor_tensor(out=visit_group[:, :], in0=psA[1][0:1, 0:VISITS], scalar=-1.0,
                                                            in1=iota_f[0:1, 0:VISITS], op0=ALU.mult, op1=ALU.add))
                        step(nc.vector.tensor_scalar(visit_slot[:, :], visit_group[:, :], RING - 1, None, ALU.bitwise_and))
                        step(nc.vector.tensor_copy(visit_word[:, :], visit_slot[:, :]))
                        step(nc.vector.scalar_tensor_tensor(out=visit_word[:, MSG_TO_ACC:VISITS], in0=visit_tile[:, 0:VISITS - MSG_TO_ACC],
                                                            scalar=float(RING), in1=visit_slot[:, MSG_TO_ACC:VISITS], op0=ALU.mult, op1=ALU.add))
                        step(nc.vector.memset(group_free[:, 0:RING], 0))
                        step(nc.vector.tensor_tensor(group_free[:, RING - 1:GROUPS], psA[2][0:1, 0:GROUPS - RING + 1],
                                                     iota_f[0:1, 0:GROUPS - RING + 1], ALU.add))
                    n = t - COLUMNS - 2
                    if 0 <= n < len(EB):
                        (k, b), to = EB[n], (src_idx, dst_col)[EB[n][0]]
                        m = min(4, BLOCKS - b)
                        dve.wait_ge(a_edge_ps, n + 1)
                        nc.vector.tensor_copy(to[:, b * P:(b + m) * P], psA[n % 4][:, 0:m * P]).then_inc(a_edge_sb, 1)
                pipeline(dve, NT, PART, PART, [(norm, 0), (next_part, 0), (aside, 0), (copy_es, 3)], tail=PART + 1)
                dve.wait_ge(a_late, 16 * 3)

            @block.tensor
            def _(pe):
                pe.wait_ge(a_const, 5)
                pe.wait_ge(a_waug, 1)

                def aside(t, s, r):
                    if not isinstance(t, int):
                        return
                    if t == TABLES + 1:
                        pe.wait_ge(a_last_f, 1)
                        nc.tensor.matmul(psA[0][:, 0:FULL], ones[0:1, :], last_f[0:1, :], start=True, stop=True).then_inc(a_last_ps, 1)
                    if t == TABLES + 4:
                        pe.wait_ge(a_ge, 2)
                        nc.tensor.matmul(psA[1][:, 0:VISITS], ones[0:NT, :], below[0:NT, 0, 0:VISITS], start=True, stop=True).then_inc(a_cnt, 1)
                        nc.tensor.matmul(psA[2][:, 0:GROUPS], ones[0:NT, :], below[0:NT, 1, 0:GROUPS], start=True, stop=True).then_inc(a_cnt, 1)
                    if t == COLUMNS:
                        pe.wait_ge(a_edge_f, 2)
                    n = t - COLUMNS
                    if 0 <= n < len(EB):
                        k, b = EB[n]
                        if n >= 4:
                            pe.wait_ge(a_edge_sb, n - 3)
                        for j in range(min(4, BLOCKS - b)):
                            last = nc.tensor.transpose(psA[n % 4][:, j * P:(j + 1) * P], edge_f[:, k, b + j, :], ident[:, :])
                        last.then_inc(a_edge_ps, 1)

                def transpose(t, s, r):
                    pe.wait_ge(a_xn, t + 1)
                    if not early(t, 2):
                        pe.wait_ge(a_xT, t - 1)
                    for c in range(KD):
                        last = nc.tensor.transpose(psT[s % 2][:, c * P:(c + 1) * P], xn[:, s, c * P:(c + 1) * P], ident[:, :])
                    last.then_inc(a_xT_ps, 1)

                def project(t, s, r):
                    pe.wait_ge(a_xT, t + 1)
                    if not early(t, 2):
                        pe.wait_ge(a_z, t - 1)
                    for c in range(KD):
                        last = nc.tensor.matmul(psZ[s % 2][:, 0:D + 2 * HEADS], xnT[:, s % 2, c * P:(c + 1) * P], wcat[:, c, :],
                                                start=c == 0, stop=c == KD - 1)
                    last.then_inc(a_z_ps, 1)
                pipeline(pe, NT, 4, PART, [(aside, 0), (transpose, 0), (project, 1)], tail=PART + 1)

        b_vstep = sem("b_vstep")
        b_spread = sem("b_spread"); b_all = sem("b_all"); b_passes = sem("b_passes")
        b_pstep = sem("b_pstep"); b_nodes = sem("b_nodes")
        b_idx = [sem(f"b_idx{i}") for i in range(RING)]; b_landed = [sem(f"b_landed{i}") for i in range(RING)]
        b_group = sem("b_group"); b_apart = sem("b_apart")
        b_loc = sem("b_loc"); b_S = sem("b_S"); b_ST_ps = sem("b_ST_ps"); b_ST = sem("b_ST")
        b_dest = sem("b_dest"); b_estep = sem("b_estep"); b_arg = sem("b_arg"); b_p = sem("b_p")
        b_msg = sem("b_msg"); b_sum = sem("b_sum"); b_acc = sem("b_acc"); b_es = sem("b_es")
        SH = 2 * HEADS
        SR = 8
        with ExitStack() as ctx:
            nodes = sb(ctx, "nodes", [P, NT, SH])
            level = sb(ctx, "level", [P, HEADS])
            spread = sb(ctx, "spread", [P, 2 * SH])
            spread_all = sb(ctx, "spread_all", [P, SH])
            npass_f = sb(ctx, "npass_f", [P, 2])
            npass_i = sb(ctx, "npass_i", [P, 1], I32)
            decided = sb(ctx, "decided", [P, NT, HEADS])
            pass_tmp = sb(ctx, "pass_tmp", [P, NT, HEADS])
            idx_ring = sb(ctx, "idx_ring", [P, RING, G], I32)
            ring = sb(ctx, "ring", [P, RING, G, ROW])
            es_edge = sb(ctx, "es_edge", [P, 4, G, HEADS])
            loc = sb(ctx, "loc", [P, SR, G])
            S = sb(ctx, "S", [P, SR, G, P])
            ST = sb(ctx, "ST", [P, 2, G * P])
            earg = sb(ctx, "earg", [P, 4, 3, G * HEADS])
            msg = sb(ctx, "msg", [P, 4, G, ROW])
            psT = [ps(ctx, f"psTb{i}") for i in range(2)]
            psE = [ps(ctx, f"psEb{i}") for i in range(2)]
            psM = [ps(ctx, f"psMb{i}") for i in range(2)]
            block = ctx.enter_context(nc.Block())

            @block.sync
            def _(sp):
                sp.wait_ge(b_passes, 1)
                npass = sp.value_load(npass_i[0:1, 0:1], min_val=1, max_val=PASSES_MAX)
                with sp.Fori(0, npass) as k:
                    def uses(s):
                        return len(range(s, GROUPS, RING))

                    def fetch_idx(g, s, r):
                        sp.dma_start(idx_ring[:, s, :], src_idx[:, bass.ds(g * G, G)]).then_inc(b_idx[s], 16)

                    def relay(g, s, r):
                        sp.wait_ge(b_landed[s], 16 * G * (k * uses(s) + r + 1))
                        sp.nop().then_inc(b_group, 1)

                    for g in range(RING):
                        fetch_idx(g, g, 0)
                    rounds = GROUPS // RING - 1
                    with sp.Fori(0, rounds) as r:
                        for s in range(RING):
                            relay(r * RING + s, s, r)
                            fetch_idx((r + 1) * RING + s, s, r + 1)
                    for g in range(rounds * RING, GROUPS):
                        relay(g, g % RING, g // RING)
                        if g + RING < GROUPS:
                            fetch_idx(g + RING, g % RING, g // RING + 1)


            @block.gpsimd
            def _(pool):
                pool.wait_ge(b_spread, 1)
                nc.gpsimd.partition_all_reduce(spread_all[:, :], spread[:, 0:SH], P, RMAX).then_inc(b_all, 1)
                pool.wait_ge(b_passes, 1)
                npass = pool.value_load(npass_i[0:1, 0:1], min_val=1, max_val=PASSES_MAX)
                with pool.Fori(0, npass) as k:
                    def gather(g, s, r):
                        done = pool.value_load(group_free[0:1, bass.ds(g, 1)], min_val=0, max_val=VISITS)
                        pool.wait_ge(b_msg, k * VISITS + done + 1)
                        pool.wait_ge(b_idx[s], 16 * (k * len(range(s, GROUPS, RING)) + r + 1))
                        pool.sem_inc(b_apart, 1)
                        for c in range(G):
                            nc.gpsimd.indirect_dma_start(ring[:, s, c, :], None, z_table,
                                                         bass.IndirectOffsetOnAxis(ap=idx_ring[:, s, c:c + 1], axis=0)
                                                         ).then_inc(b_landed[s], 16)
                    pipeline(pool, GROUPS, RING, 0, [(gather, 0)])

            @block.vector
            def _(dve):
                step = stepper(dve, b_vstep)
                step(nc.vector.tensor_reduce(spread[:, 0:HEADS], esed[:, :, 0:HEADS].rearrange("p t h -> p h t"), AX.X, ALU.max))
                step(nc.vector.tensor_reduce(spread[:, SH:SH + HEADS], esed[:, :, 0:HEADS].rearrange("p t h -> p h t"), AX.X, ALU.min))
                nc.vector.tensor_scalar(spread[:, HEADS:SH], spread[:, SH:SH + HEADS], -1.0, None, ALU.mult).then_inc(b_spread, 1)
                dve.sem_inc(b_msg, 1)
                step(nc.vector.tensor_copy(nodes[:, :, 0:HEADS], esed[:, :, HEADS:SH]))
                dve.wait_ge(b_all, 1)
                step(nc.vector.tensor_copy(level[:, :], spread_all[:, 0:HEADS]))
                step(nc.vector.tensor_tensor(spread[:, SH + HEADS:2 * SH], spread_all[:, 0:HEADS], spread_all[:, HEADS:SH], ALU.add))
                step(nc.vector.tensor_reduce(npass_f[:, 0:1], spread[:, SH + HEADS:2 * SH], AX.X, ALU.max))
                step(nc.vector.tensor_scalar(npass_f[:, 1:2], npass_f[:, 0:1], 1.0 / LEVEL, 1.0, ALU.mult, ALU.add))
                nc.vector.tensor_scalar(npass_i[:, :], npass_f[:, 1:2], float(PASSES_MAX), None, ALU.min).then_inc(b_passes, 1)
                dve.wait_ge(b_passes, 1)
                npass = dve.value_load(npass_i[0:1, 0:1], min_val=1, max_val=PASSES_MAX)
                with dve.Fori(0, npass) as k:
                    PASS_STEPS = 5
                    made = [0]

                    def pass_step(instruction):
                        made[0] += 1
                        instruction.then_inc(b_pstep, 1)
                        dve.wait_ge(b_pstep, k * PASS_STEPS + made[0])
                    den = acc[:, :, D:ROW]
                    pass_step(nc.vector.tensor_scalar(decided[:, :, :], den, DECIDED, None, ALU.is_ge))
                    pass_step(nc.vector.tensor_tensor(pass_tmp[:, :, :], esed[:, :, HEADS:SH],
                                                      over(level[:, :].unsqueeze(1), [P, NT, HEADS]), ALU.add))
                    pass_step(nc.vector.scalar_tensor_tensor(out=pass_tmp[:, :, :], in0=pass_tmp[:, :, :], scalar=SLOPE,
                                                             in1=pass_tmp[:, :, :], op0=ALU.mult, op1=ALU.max))
                    pass_step(nc.vector.scalar_tensor_tensor(out=nodes[:, :, HEADS:SH], in0=decided[:, :, :], scalar=FAR,
                                                             in1=pass_tmp[:, :, :], op0=ALU.mult, op1=ALU.add))
                    pass_step(nc.vector.tensor_scalar(level[:, :], level[:, :], LEVEL, None, ALU.subtract))
                    for h in range(HEADS):
                        nc.vector.tensor_tensor(acc[:, :, h * DH:(h + 1) * DH], acc[:, :, h * DH:(h + 1) * DH],
                                                       over(decided[:, :, h:h + 1], [P, NT, DH]), ALU.mult)
                    assert made[0] == PASS_STEPS
                    nc.vector.tensor_tensor(den, den, decided[:, :, :], ALU.mult).then_inc(b_nodes, 1)
                    dve.wait_ge(b_nodes, k + 1)
                    dve.sem_inc(b_apart, 1)
                    base = k * VISITS

                    def one_hot(v, s, r):
                        dve.wait_ge(b_loc, base + v + 1)
                        if not early(v, SR):
                            dve.wait_ge(b_sum, base + v - SR + 1)
                        nc.vector.tensor_tensor(S[:, s, :, :], over(iota_f[:, 0:P].unsqueeze(1), [P, G, P]),
                                                over(loc[:, s, :].unsqueeze(2), [P, G, P]), ALU.is_equal).then_inc(b_S, 1)

                    def e_add(v, s, r):
                        dve.wait_ge(b_es, base + v + 1)
                        dve.wait_ge(b_dest, base + v + 1)
                        dest = psE[s % 2][:, 0:G * SH].rearrange("p (g c) -> p g c", g=G)
                        nc.vector.tensor_tensor(earg[:, s % 4, 0, :].rearrange("p (g h) -> p g h", g=G),
                                                es_edge[:, s % 4, :, :], dest[:, :, 0:HEADS], ALU.add).then_inc(b_estep, 1)

                    def e_lrelu(v, s, r):
                        dve.wait_ge(b_estep, 3 * base + 3 * v + 1)
                        nc.vector.scalar_tensor_tensor(out=earg[:, s % 4, 1, :], in0=earg[:, s % 4, 0, :], scalar=SLOPE,
                                                       in1=earg[:, s % 4, 0, :], op0=ALU.mult, op1=ALU.max).then_inc(b_estep, 1)

                    def e_shift(v, s, r):
                        dve.wait_ge(b_estep, 3 * base + 3 * v + 2)
                        dest = psE[s % 2][:, 0:G * SH].rearrange("p (g c) -> p g c", g=G)
                        nc.vector.tensor_tensor(earg[:, s % 4, 2, :].rearrange("p (g h) -> p g h", g=G),
                                                earg[:, s % 4, 1, :].rearrange("p (g h) -> p g h", g=G),
                                                dest[:, :, HEADS:SH], ALU.subtract).then_inc(b_estep, 1)

                    def e_clamp(v, s, r):
                        dve.wait_ge(b_estep, 3 * base + 3 * v + 3)
                        nc.vector.tensor_scalar(earg[:, s % 4, 0, :], earg[:, s % 4, 2, :], 0.0, None, ALU.min).then_inc(b_arg, 1)

                    word = [None]

                    def look_up(v, s, r):
                        word[0] = dve.value_load(visit_word[0:1, bass.ds(v, 1)], min_val=0, max_val=RING * NT - 1)

                    def message(v, s, r):
                        slot = word[0] & (RING - 1)
                        dve.wait_ge(b_p, base + v + 1)
                        nc.vector.tensor_tensor(msg[:, s % 4, :, 0:D].rearrange("p g (h d) -> p g h d", h=HEADS),
                                                ring[:, bass.ds(slot, 1), :, 0:D].rearrange("p o g (h d) -> p (o g) h d", h=HEADS),
                                                over(msg[:, s % 4, :, D:ROW].unsqueeze(3), [P, G, HEADS, DH]), ALU.mult).then_inc(b_msg, 1)

                    def accumulate(v, s, r):
                        if isinstance(v, int) and v + MSG_TO_ACC >= VISITS:
                            tile = dve.value_load(visit_tile[0:1, bass.ds(v, 1)], min_val=0, max_val=NT - 1)
                        else:
                            tile = (word[0] >> (RING.bit_length() - 1)).with_bounds(min_val=0, max_val=NT - 1)
                        dve.wait_ge(b_sum, base + v + 1)
                        if not early(v, 1):
                            dve.wait_ge(b_acc, base + v)
                        at = acc[:, bass.ds(tile, 1), :].rearrange("p o c -> p (o c)")
                        nc.vector.tensor_tensor(at, at, psM[s % 2][:, 0:ROW], ALU.add).then_inc(b_acc, 1)
                    pipeline(dve, VISITS, SR, SR, [(look_up, 3), (e_add, 2), (one_hot, 0), (e_lrelu, 2), (accumulate, 3 + MSG_TO_ACC),
                                                   (e_shift, 2), (message, 3), (e_clamp, 2)])
                    dve.wait_ge(b_acc, base + VISITS)

            @block.scalar
            def _(act):
                act.wait_ge(b_passes, 1)
                npass = act.value_load(npass_i[0:1, 0:1], min_val=1, max_val=PASSES_MAX)
                with act.Fori(0, npass) as k:
                    base = k * VISITS

                    def locate(v, s, r):
                        group = act.value_load(visit_group[0:1, bass.ds(v, 1)], min_val=0, max_val=GROUPS - 1)
                        if not early(v, SR):
                            act.wait_ge(b_S, base + v - SR + 1)
                        nc.scalar.activation(loc[:, s, :], dst_col[:, bass.ds(group * G, G)], ACT.Identity,
                                             bias=visit_base[:, bass.ds(v, 1)]).then_inc(b_loc, 1)

                    def open_group(v, s, r):
                        group = act.value_load(visit_group[0:1, bass.ds(v, 1)], min_val=0, max_val=GROUPS - 1)
                        slot = group & (RING - 1)
                        act.wait_ge(b_group, k * GROUPS + group + 1)
                        if not early(v, 4):
                            act.wait_ge(b_arg, base + v - 3)
                        nc.scalar.copy(es_edge[:, s % 4, :, :],
                                       ring[:, bass.ds(slot, 1), :, D:ROW].rearrange("p o g h -> p (o g) h")).then_inc(b_es, 1)

                    def copy_ST(v, s, r):
                        act.wait_ge(b_ST_ps, base + v + 1)
                        if not early(v, 2):
                            act.wait_ge(b_dest, base + v - 1)
                        nc.scalar.copy(ST[:, s % 2, :], psT[s % 2][:, 0:G * P]).then_inc(b_ST, 1)

                    def exponent(v, s, r):
                        act.wait_ge(b_arg, base + v + 1)
                        if not early(v, 4):
                            act.wait_ge(b_sum, base + v - 3)
                        nc.scalar.activation(msg[:, s % 4, :, D:ROW], earg[:, s % 4, 0, :].rearrange("p (g h) -> p g h", g=G),
                                             ACT.Exp).then_inc(b_p, 1)
                    pipeline(act, VISITS, SR, 8, [(locate, 0), (copy_ST, 2), (open_group, 2), (exponent, 3)])

            @block.tensor
            def _(pe):
                pe.wait_ge(b_passes, 1)
                npass = pe.value_load(npass_i[0:1, 0:1], min_val=1, max_val=PASSES_MAX)
                with pe.Fori(0, npass) as k:
                    base = k * VISITS
                    pe.wait_ge(b_nodes, k + 1)

                    def transpose(v, s, r):
                        pe.wait_ge(b_S, base + v + 1)
                        if not early(v, 2):
                            pe.wait_ge(b_ST, base + v - 1)
                        for c in range(G):
                            last = nc.tensor.transpose(psT[s % 2][:, c * P:(c + 1) * P], S[:, s, c, :], ident[:, :])
                        last.then_inc(b_ST_ps, 1)

                    def destination(v, s, r):
                        tile = pe.value_load(visit_tile[0:1, bass.ds(v, 1)], min_val=0, max_val=NT - 1)
                        pe.wait_ge(b_ST, base + v + 1)
                        if not early(v, 2):
                            pe.wait_ge(b_arg, base + v - 1)
                        for c in range(G):
                            last = nc.tensor.matmul(psE[s % 2][:, c * SH:(c + 1) * SH], ST[:, s % 2, c * P:(c + 1) * P],
                                                    nodes[:, bass.ds(tile, 1), :].rearrange("p o c -> p (o c)"),
                                                    start=True, stop=True)
                        last.then_inc(b_dest, 1)

                    def weigh(v, s, r):
                        pe.wait_ge(b_msg, base + v + 2)
                        if not early(v, 2):
                            pe.wait_ge(b_acc, base + v - 1)
                        for c in range(G):
                            last = nc.tensor.matmul(psM[s % 2][:, 0:ROW], S[:, s, c, :], msg[:, s % 4, c, :],
                                                    start=c == 0, stop=c == G - 1)
                        last.then_inc(b_sum, 1)
                    pipeline(pe, VISITS, SR, 5, [(transpose, 0), (destination, 1), (weigh, 3)])

        graph.close()
        c_bulk = sem("c_bulk"); c_apart = sem("c_apart"); c_rden = sem("c_rden"); c_scaled = sem("c_scaled"); c_pool = sem("c_pool")
        c_pstep = sem("c_pstep"); c_vstep = sem("c_vstep"); c_stats = sem("c_stats"); c_var = sem("c_var")
        c_root = sem("c_root"); c_gate = sem("c_gate"); c_xn = sem("c_xn"); c_xT_ps = sem("c_xT_ps")
        c_xT = sem("c_xT"); c_log_ps = sem("c_log_ps"); c_log = sem("c_log"); c_gap = sem("c_gap")
        c_exp = sem("c_exp"); c_strict = sem("c_strict"); c_taken = sem("c_taken"); c_rank = sem("c_rank")
        c_b1 = sem("c_b1"); c_b1_ps = sem("c_b1_ps"); c_iota = sem("c_iota");
        c_valid = sem("c_valid"); c_saved = [sem(f"c_saved{i}") for i in range(4)]
        c_slot = sem("c_slot"); c_low = sem("c_low"); c_eq = sem("c_eq"); c_by_tile = sem("c_by_tile")
        c_by_part = sem("c_by_part"); c_listed = sem("c_listed")
        with ExitStack() as ctx:
            stats = sb(ctx, "stats_c", [P, NT, 6])
            rden = sb(ctx, "rden", [P, NT, HEADS])
            xn = sb(ctx, "xnc", [P, 4, D])
            gate = sb(ctx, "gate", [P, KD, EXPERTS])
            xnT = sb(ctx, "xnTc", [P, 2, D])
            logits = sb(ctx, "logits", [P, NT, EXPERTS])
            work = sb(ctx, "work", [P, NT, EXPERTS])
            hot = sb(ctx, "hot", [P, TOP, NT, EXPERTS])
            taken = sb(ctx, "taken", [P, NT, EXPERTS])
            top = sb(ctx, "top", [P, TOP, NT])
            best = sb(ctx, "best", [P, NT])
            gap = sb(ctx, "gap", [P, 2, NT])
            strict = sb(ctx, "strict", [P, P])
            total = sb(ctx, "total", [P, EXPERTS, NT])
            upto = sb(ctx, "upto", [P, EXPERTS, NT])
            resets = sb(ctx, "resets", [P, EXPERTS, NT])
            reverse_i = sb(ctx, "reverse_i", [P, EXPERTS], I32)
            reverse = sb(ctx, "reverse", [P, EXPERTS])
            tiles_i = sb(ctx, "tiles_i", [P, 2, EXPERTS], I32)
            tiles_f = sb(ctx, "tiles_f", [P, 4, EXPERTS])
            past = sb(ctx, "past", [1, TILES, EXPERTS], BF16)
            past_sum = sb(ctx, "past_sum", [1, TILES])
            slot_f = sb(ctx, "slot_f", [P, NT])
            slot_i = sb(ctx, "slot_i", [P, 3, NT], I32)
            slot_h = sb(ctx, "slot_h", [P, TOP, 2, NT], BF16)
            iota_h = sb(ctx, "iota_h", [P, P], BF16)
            tile_h = sb(ctx, "tile_h", [P, NT], BF16)
            HALF = (NT + 1) // 2
            LR = 3
            THIRD = -(-NT // 3)
            low = sb(ctx, "low", [P, LR, THIRD, P], BF16)
            high = sb(ctx, "high", [P, LR, THIRD, 3, TILES], BF16)
            LISTS = [(k, lo, min(lo + THIRD, NT)) for k in range(TOP) for lo in range(0, NT, THIRD)]
            listed = sb(ctx, "listed", [P, 6, TILES])
            valid = sb(ctx, "valid", [P, NT])
            b1_sb = sb(ctx, "b1_sb", [EXPERTS * FC, P])
            psT = [ps(ctx, f"psTc{i}") for i in range(2)]
            psL = [ps(ctx, f"psLc{i}") for i in range(2)]
            psR = [ps(ctx, f"psRc{i}") for i in range(2)]
            psN = [ps(ctx, f"psNc{i}") for i in range(2)]
            block = ctx.enter_context(nc.Block())

            @block.sync
            def _(sp):
                for c in range(KD):
                    sp.dma_start(gate[:, c, :], gate_w[c * P:(c + 1) * P, :]).then_inc(c_gate, 16)
                sp.dma_start(b1_sb[:, :], b1.rearrange("e (c f) -> (e c) f", f=P)).then_inc(c_b1, 16)

                def save(t, s, r):
                    sp.wait_ge(c_xn, t + 1)
                    sp.dma_start(norm_rows[bass.ds(t * P, P), :], xn[:, s, :]).then_inc(c_saved[s], 16)
                pipeline(sp, NT, 4, 0, [(save, 0)])
                for s in range(4):
                    sp.wait_ge(c_saved[s], 16 * len(range(s, NT, 4)))

            @block.gpsimd
            def _(pool):
                nc.gpsimd.iota(reverse_i[:, :], [[-1, EXPERTS]], base=EXPERTS, channel_multiplier=0).then_inc(c_iota, 1)
                nc.gpsimd.memset(valid[:, :], 1.0).then_inc(c_valid, 1)
                pool.wait_ge(c_valid, 1)
                nc.gpsimd.affine_select(out=valid[:, NT - 1:NT], in_=valid[:, NT - 1:NT], compare_op=ALU.is_ge, fill=0.0,
                                        base=REST - 1, pattern=[[0, 1]], channel_multiplier=-1).then_inc(c_iota, 1)
                nc.gpsimd.affine_select(out=strict[:, :], in_=ones[:, :], compare_op=ALU.is_gt, fill=0.0,
                                        base=0, pattern=[[1, P]], channel_multiplier=-1).then_inc(c_strict, 1)
                step = stepper(pool, c_pstep)
                pool.wait_ge(c_rden, 1)
                for i in range(1, XC + 1):
                    at = slice(i * PART, min((i + 1) * PART, NT))
                    part_sums = acc[:, at, 0:D].rearrange("p t (h d) -> p t h d", h=HEADS)
                    scaled = nc.gpsimd.tensor_tensor(part_sums, part_sums, over(rden[:, at, :].unsqueeze(3),
                                                                                [P, at.stop - at.start, HEADS, DH]), ALU.mult)
                    if i == 1:
                        scaled.then_inc(c_scaled, 1)
                        continue
                    step(scaled)
                    nc.gpsimd.tensor_tensor(xs[:, at, :], xs[:, at, :], acc[:, at, 0:D], ALU.add).then_inc(c_pool, 1)
                for n, (k, lo, hi) in enumerate(LISTS):
                    pool.wait_ge(c_eq, n + 1)
                    if n >= LR:
                        pool.wait_ge(c_listed, n - LR + 1)
                    nc.gpsimd.tensor_tensor(high[:, n % LR, 0:hi - lo, 0, :], high[:, n % LR, 0:hi - lo, 2, :],
                                            over(tile_h[:, lo:hi].unsqueeze(2), [P, hi - lo, TILES]), ALU.mult).then_inc(c_by_tile, 1)

            @block.scalar
            def _(act):
                def root(part, at):
                    act.wait_ge(c_var, part + 1)
                    nc.scalar.activation(rstd[:, at], ln_tmp[:, 0, at], ACT.Sqrt, bias=eps_col[:, 0:1]).then_inc(c_root, 1)
                root(0, slice(0, PART))

                def next_root(t, s, r):
                    if s == 8 and not (isinstance(r, int) and r >= XC):
                        part = r + 1
                        root(part, slice(XC * PART, NT) if isinstance(r, int) and r == XC - 1 else bass.ds(part * PART, PART))

                def copy_xT(t, s, r):
                    act.wait_ge(c_xT_ps, t + 1)
                    if not early(t, 2):
                        act.wait_ge(c_log_ps, t - 1)
                    nc.scalar.copy(xnT[:, s % 2, :], psT[s % 2][:, 0:D]).then_inc(c_xT, 1)

                pipeline(act, NT, PART, PART, [(next_root, 0), (copy_xT, 0)], tail=PART + 1)
                act.wait_ge(c_gap, 1)
                nc.scalar.activation(gap[:, 1, :], gap[:, 0, :], ACT.Exp).then_inc(c_exp, 1)
                for n, (k, lo, hi) in enumerate(LISTS):
                    act.wait_ge(c_eq, n + 1)
                    if n >= LR:
                        act.wait_ge(c_listed, n - LR + 1)
                    nc.scalar.activation(high[:, n % LR, 0:hi - lo, 1, :], high[:, n % LR, 0:hi - lo, 2, :], ACT.Copy,
                                         scale=iota_p[:, 0:1]).then_inc(c_by_part, 1)

            @block.tensor
            def _(pe):
                pe.wait_ge(c_gate, 16 * KD)

                def transpose(t, s, r):
                    pe.wait_ge(c_xn, t + 1)
                    if not early(t, 2):
                        pe.wait_ge(c_xT, t - 1)
                    for c in range(KD):
                        last = nc.tensor.transpose(psT[s % 2][:, c * P:(c + 1) * P], xn[:, s, c * P:(c + 1) * P], ident[:, :])
                    last.then_inc(c_xT_ps, 1)

                def logit(t, s, r):
                    pe.wait_ge(c_xT, t + 1)
                    if not early(t, 2):
                        pe.wait_ge(c_log, t - 1)
                    for c in range(KD):
                        last = nc.tensor.matmul(psL[s % 2][:, 0:EXPERTS], xnT[:, s % 2, c * P:(c + 1) * P], gate[:, c, :],
                                                start=c == 0, stop=c == KD - 1)
                    last.then_inc(c_log_ps, 1)
                pipeline(pe, NT, 4, 3, [(transpose, 0), (logit, 1)])
                pe.wait_ge(c_b1, 16)
                pe.wait_ge(c_xT, NT)
                nc.tensor.transpose(psT[0][:, 0:EXPERTS * FC], b1_sb[:, :], ident[0:EXPERTS * FC, 0:EXPERTS * FC]).then_inc(c_b1_ps, 1)
                pe.wait_ge(c_strict, 1)
                pe.wait_ge(c_taken, 1)
                for i, (lo, hi) in enumerate(((0, HALF), (HALF, NT))):
                    rhs = taken[:, lo:hi, :].rearrange("p t e -> p (t e)")
                    nc.tensor.matmul(psR[i][:, 0:(hi - lo) * EXPERTS], strict[:, :], rhs, start=True, stop=True).then_inc(c_rank, 1)
                    nc.tensor.matmul(psN[i][:, 0:(hi - lo) * EXPERTS], ones[:, :], rhs, start=True, stop=True).then_inc(c_rank, 1)
                for n, (k, lo, hi) in enumerate(LISTS):
                    pe.wait_ge(c_low, n + 1)
                    pe.wait_ge(c_by_tile, n + 1)
                    pe.wait_ge(c_by_part, n + 1)

                    def place(t):
                        return nc.tensor.matmul(psL[k][:, 0:2 * TILES], low[:, n % LR, bass.ds(t, 1), :].rearrange("p o f -> p (o f)"),
                                                high[:, n % LR, bass.ds(t, 1), 0:2, :].rearrange("p o a j -> p (o a j)"),
                                                start=lo == 0 and isinstance(t, int) and t == 0,
                                                stop=hi == NT and isinstance(t, int) and t == hi - lo - 1)
                    place(0)
                    rounds = (hi - lo - 2) // 4
                    with pe.Fori(0, rounds) as r:
                        for u in range(4):
                            place(r * 4 + (1 + u))
                    for t in range(1 + rounds * 4, hi - lo):
                        last = place(t)
                    last.then_inc(c_listed, 1)

            @block.vector
            def _(dve):
                step = stepper(dve, c_vstep)
                step(nc.vector.tensor_scalar(rden[:, :, :], acc[:, :, D:ROW], TINY, None, ALU.max))
                step(nc.vector.reciprocal(rden[:, :, :], rden[:, :, :]))
                dve.sem_inc(c_rden, 1)
                first = slice(0, PART)
                sums = acc[:, first, 0:D].rearrange("p t (h d) -> p t h d", h=HEADS)
                step(nc.vector.tensor_tensor(sums, sums, over(rden[:, first, :].unsqueeze(3), [P, PART, HEADS, DH]), ALU.mult))
                step(nc.vector.tensor_tensor(xs[:, first, :], xs[:, first, :], acc[:, first, 0:D], ALU.add))

                def tile_stats(t):
                    nc.vector.bn_stats(stats[:, bass.ds(t, 1), :].rearrange("p o s -> p (o s)"),
                                       xs[:, bass.ds(t, 1), :].rearrange("p o c -> p (o c)")).then_inc(c_stats, 1)

                def invert(part, at, part_step):
                    dve.wait_ge(c_root, part + 1)
                    part_step(nc.vector.reciprocal(rstd[:, at], rstd[:, at]))
                for t in range(PART):
                    tile_stats(t)
                dve.wait_ge(c_stats, PART)
                part_step = stepper(dve, c_bulk)
                bulk_rstd(part_step, stats, first, c_var)
                dve.wait_ge(c_iota, 2)
                step(nc.vector.tensor_copy(reverse[:, :], reverse_i[:, :]))
                step(nc.vector.tensor_copy(iota_h[:, :], iota_f[:, 0:P]))
                step(nc.vector.tensor_scalar(tile_h[:, :], iota_f[:, 0:NT], 1.0, None, ALU.add))
                step(nc.vector.memset(resets[:, :, :], 1.0))
                step(nc.vector.memset(resets[:, :, 0:1], 0.0))
                invert(0, first, part_step)
                stepping = [None]

                def next_part(t, s, r):
                    static = isinstance(r, int)
                    if static and r >= XC:
                        return
                    n = 1 if static and r == XC - 1 else PART
                    at = slice(XC * PART, NT) if n == 1 else bass.ds((r + 1) * PART, PART)
                    if s == 0:
                        if static and r == 0:
                            second = slice(PART, 2 * PART)
                            dve.wait_ge(c_scaled, 1)
                            step(nc.vector.tensor_tensor(xs[:, second, :], xs[:, second, :], acc[:, second, 0:D], ALU.add))
                        else:
                            dve.wait_ge(c_pool, r)
                            dve.sem_inc(c_apart, 1)
                    for u in range(s * n // 8, (s + 1) * n // 8) if s < 8 else ():
                        tile_stats((r + 1) * PART + u)
                    if s == 8:
                        dve.wait_ge(c_stats, (r + 1) * PART + n)
                        stepping[0] = stepper(dve, c_bulk, (r + 1) * BULK)
                        bulk_rstd(stepping[0], stats, at, c_var)
                    if s == PART - 1:
                        invert(r + 1, at, stepping[0])

                def norm(t, s, r):
                    if not early(t, 4):
                        dve.wait_ge(c_xT_ps, t - 3)
                        dve.wait_ge(c_saved[s % 4], 16 * (r * (PART // 4) + s // 4))
                    nc.vector.tensor_scalar(xn[:, s % 4, :], xs[:, bass.ds(t, 1), :].rearrange("p o c -> p (o c)"),
                                            mean[:, bass.ds(t, 1)], rstd[:, bass.ds(t, 1)],
                                            ALU.subtract, ALU.mult).then_inc(c_xn, 1)

                def keep_logit(t, s, r):
                    dve.wait_ge(c_log_ps, t + 1)
                    nc.vector.tensor_tensor(logits[:, bass.ds(t, 1), :].rearrange("p o e -> p (o e)"), psL[s % 2][:, 0:EXPERTS],
                                            rows_bc[:, 2 * D:], ALU.add).then_inc(c_log, 1)
                pipeline(dve, NT, PART, PART, [(norm, 0), (next_part, 0), (keep_logit, 3)], tail=PART + 1)
                dve.wait_ge(c_log, NT)

                rev = over(reverse[:, :].unsqueeze(1), [P, NT, EXPERTS])
                wide = [P, NT, EXPERTS]
                for k in range(TOP):
                    step(nc.vector.tensor_reduce(top[:, k, :], logits[:, :, :], AX.X, ALU.max))
                    step(nc.vector.tensor_tensor(work[:, :, :], logits[:, :, :], over(top[:, k, :].unsqueeze(2), wide), ALU.is_equal))
                    step(nc.vector.tensor_tensor(work[:, :, :], work[:, :, :], rev, ALU.mult))
                    step(nc.vector.tensor_reduce(best[:, :], work[:, :, :], AX.X, ALU.max))
                    step(nc.vector.tensor_tensor(hot[:, k, :, :], rev, over(best[:, :].unsqueeze(2), wide), ALU.is_equal))
                    if k < TOP - 1:
                        step(nc.vector.scalar_tensor_tensor(out=logits[:, :, :], in0=hot[:, k, :, :], scalar=-FAR,
                                                            in1=logits[:, :, :], op0=ALU.mult, op1=ALU.add))
                nc.vector.tensor_tensor(gap[:, 0, :], top[:, 1, :], top[:, 0, :], ALU.subtract).then_inc(c_gap, 1)
                step(nc.vector.tensor_tensor(taken[:, :, :], hot[:, 0, :, :], hot[:, 1, :, :], ALU.add))
                nc.vector.tensor_tensor(taken[:, :, :], taken[:, :, :], over(valid[:, :].unsqueeze(2), wide), ALU.mult).then_inc(c_taken, 1)
                dve.wait_ge(c_exp, 1)
                step(nc.vector.tensor_scalar(gap[:, 0, :], gap[:, 1, :], 1.0, None, ALU.add))
                step(nc.vector.reciprocal(share[:, 0, :], gap[:, 0, :]))
                step(nc.vector.tensor_tensor(share[:, 1, :], gap[:, 1, :], share[:, 0, :], ALU.mult))
                dve.wait_ge(c_b1_ps, 1)
                step(nc.vector.tensor_copy(b1T[:, :, :].rearrange("p e c -> p (e c)"), psT[0][:, 0:EXPERTS * FC]))

                dve.wait_ge(c_rank, 4)
                for i, (lo, hi) in enumerate(((0, HALF), (HALF, NT))):
                    step(nc.vector.tensor_copy(total[:, :, lo:hi],
                                               psN[i][:, 0:(hi - lo) * EXPERTS].rearrange("p (t e) -> p e t", e=EXPERTS)))
                flat = "p e t -> p (e t)"
                step(nc.vector.tensor_tensor_scan(upto[:, :, :].rearrange(flat), resets[:, :, :].rearrange(flat),
                                                  total[:, :, :].rearrange(flat), 0.0, ALU.mult, ALU.add))
                step(nc.vector.tensor_tensor(total[:, :, :], upto[:, :, :], total[:, :, :], ALU.subtract))
                shift = P.bit_length() - 1
                step(nc.vector.tensor_scalar(tiles_i[:, 0, :], upto[:, :, NT - 1], float(P - 1), None, ALU.add))
                step(nc.vector.tensor_scalar(tiles_i[:, 1, :], tiles_i[:, 0, :], shift, None, ALU.arith_shift_right))
                step(nc.vector.tensor_copy(tiles_f[:, 0, :], tiles_i[:, 1, :]))
                step(nc.vector.tensor_tensor_scan(tiles_f[:, 1, :], ones[:, 0:EXPERTS], tiles_f[:, 0, :], 0.0, ALU.mult, ALU.add))
                step(nc.vector.tensor_scalar(tile_rounds[:, :], tiles_f[0:1, 1, EXPERTS - 1:EXPERTS], float(DR - 1 - HEAD), None, ALU.add))
                step(nc.vector.tensor_scalar(tile_rounds[:, :], tile_rounds[:, :], DR.bit_length() - 1, None, ALU.arith_shift_right))
                step(nc.vector.tensor_tensor(tiles_f[:, 2, :], tiles_f[:, 1, :], tiles_f[:, 0, :], ALU.subtract))
                step(nc.vector.tensor_scalar(tiles_f[:, 3, :], tiles_f[:, 2, :], float(P), None, ALU.mult))
                step(nc.vector.tensor_tensor(total[:, :, :], total[:, :, :], over(tiles_f[:, 3, :].unsqueeze(2), [P, EXPERTS, NT]), ALU.add))
                for i, (lo, hi) in enumerate(((0, HALF), (HALF, NT))):
                    step(nc.vector.tensor_tensor(work[:, lo:hi, :], total[:, :, lo:hi].rearrange("p e t -> p t e"),
                                                 psR[i][:, 0:(hi - lo) * EXPERTS].rearrange("p (t e) -> p t e", e=EXPERTS), ALU.add))
                step(nc.vector.tensor_scalar(valid[:, :], valid[:, :], -float(NOWHERE), float(NOWHERE), ALU.mult, ALU.add))
                for k in range(TOP):
                    step(nc.vector.tensor_tensor(logits[:, :, :], work[:, :, :], hot[:, k, :, :], ALU.mult))
                    step(nc.vector.tensor_reduce(slot_f[:, :], logits[:, :, :], AX.X, ALU.add))
                    step(nc.vector.tensor_tensor(slot_i[:, 0, :], slot_f[:, :], valid[:, :], ALU.add))
                    step(nc.vector.tensor_scalar(slot_i[:, 1, :], slot_i[:, 0, :], P - 1, None, ALU.bitwise_and))
                    step(nc.vector.tensor_scalar(slot_i[:, 2, :], slot_i[:, 0, :], shift, None, ALU.arith_shift_right))
                    nc.vector.tensor_copy(slot_h[:, k, :, :], slot_i[:, 1:3, :]).then_inc(c_slot, 1)
                    dve.wait_ge(c_slot, k + 1)
                for n, (k, lo, hi) in enumerate(LISTS):
                    flat, tall = [P, hi - lo, P], [P, hi - lo, TILES]
                    if n >= LR:
                        dve.wait_ge(c_listed, n - LR + 1)
                        dve.wait_ge(c_by_part, n - LR + 1)
                        dve.wait_ge(c_by_tile, n - LR + 1)
                    nc.vector.tensor_tensor(high[:, n % LR, 0:hi - lo, 2, :], over(iota_h[:, 0:TILES].unsqueeze(1), tall),
                                            over(slot_h[:, k, 1, lo:hi].unsqueeze(2), tall), ALU.is_equal).then_inc(c_eq, 1)
                    nc.vector.tensor_tensor(low[:, n % LR, 0:hi - lo, :], over(iota_h[:, :].unsqueeze(1), flat),
                                            over(slot_h[:, k, 0, lo:hi].unsqueeze(2), flat), ALU.is_equal).then_inc(c_low, 1)
                long = [1, TILES, EXPERTS]
                step(nc.vector.tensor_tensor(past[:, :, :], over(iota_f[0:1, 0:TILES].unsqueeze(2), long),
                                             over(tiles_f[0:1, 1, :].unsqueeze(1), long), ALU.is_ge))
                step(nc.vector.tensor_reduce(past_sum[:, :], past[:, :, :], AX.X, ALU.add))
                step(nc.vector.tensor_scalar(tile_expert[:, :], past_sum[:, :], float(EXPERTS - 1), None, ALU.min))
                dve.wait_ge(c_listed, len(LISTS))
                for k in range(TOP):
                    step(nc.vector.tensor_copy(listed[:, 2 * k:2 * k + 2, :].rearrange("p a j -> p (a j)"), psL[k][:, 0:2 * TILES]))
                first_t, first_p, second_t, second_p = (listed[:, i, :] for i in range(4))
                token, target = listed[:, 4, :], listed[:, 5, :]
                step(nc.vector.tensor_tensor(token, first_t, second_t, ALU.add))
                step(nc.vector.tensor_scalar(target, token, 0.0, None, ALU.is_equal))
                step(nc.vector.tensor_scalar(token, token, float(P), -float(P), ALU.mult, ALU.add))
                step(nc.vector.tensor_tensor(token, token, first_p, ALU.add))
                step(nc.vector.tensor_tensor(token, token, second_p, ALU.add))
                step(nc.vector.tensor_scalar(token, token, 0.0, None, ALU.max))
                step(nc.vector.tensor_copy(slot_ends[:, :, 0], token))
                step(nc.vector.tensor_scalar(first_t, iota_f[:, 0:TILES], float(P), iota_p[:, 0:1], ALU.mult, ALU.add))
                step(nc.vector.tensor_scalar(first_t, first_t, float(TOP * NT * P), None, ALU.add))
                step(nc.vector.tensor_tensor(target, target, first_t, ALU.mult))
                step(nc.vector.tensor_scalar(second_t, second_t, 0.0, float(NT * P), ALU.is_gt, ALU.mult))
                step(nc.vector.tensor_tensor(target, target, second_t, ALU.add))
                step(nc.vector.tensor_tensor(slot_ends[:, :, 1], target, token, ALU.add))

        attention.close()

        def load_rounds(eng):
            return eng.value_load(tile_rounds[0:1, 0:1], min_val=1, max_val=(TILES - HEAD) // DR)
        d_w = sem("d_w"); d_w1 = sem("d_w1"); d_b2 = [sem(f"d_b2{i}") for i in range(DR)]
        d_rows = [sem(f"d_rows{i}") for i in range(DR)]
        d_stored = [sem(f"d_stored{i}") for i in range(DR)]; d_src = sem("d_src"); d_dst = sem("d_dst")
        d_xT_ps = sem("d_xT_ps"); d_xT = sem("d_xT"); d_up = sem("d_up"); d_hid = sem("d_hid")
        d_down = sem("d_down"); d_y = sem("d_y"); d_apart = sem("d_apart")
        with ExitStack() as ctx:
            w_all = sb(ctx, "w_all", [P, EXPERTS, KD * F + FC * D])
            w1_sb = sb(ctx, "w1_sb", [P, 2, KD, F])
            b2_sb = sb(ctx, "b2_sb", [P, DR, D])
            rows_sb = sb(ctx, "rows_sb", [P, DR, D])
            src_sb = sb(ctx, "src_sb", [P, DR, 1], I32)
            dst_sb = sb(ctx, "dst_sb", [P, DR, 1], I32)
            xT = sb(ctx, "xT", [P, 2, KD, P])
            hid = sb(ctx, "hid", [P, 2, FC, P])
            y_sb = sb(ctx, "y_sb", [P, DR, D])
            psX = [ps(ctx, f"psXd{i}") for i in range(2)]
            psH = [ps(ctx, f"psHd{i}") for i in range(2)]
            psY = [ps(ctx, f"psYd{i}") for i in range(2)]
            block = ctx.enter_context(nc.Block())

            @block.sync
            def _(sp):
                for e in range(EXPERTS):
                    if e:
                        sp.wait_ge(d_w, 32 * e)
                    sp.dma_start(w_all[:, e, 0:KD * F].rearrange("p (c f) -> p c f", f=F),
                                 w1[e].rearrange("(c p) f -> p c f", p=P)).then_inc(d_w, 16)
                    sp.dma_start(w_all[:, e, KD * F:].rearrange("p (c f) -> p c f", f=D),
                                 w2[e].rearrange("(c p) f -> p c f", p=P)).then_inc(d_w, 16)
                sp.wait_ge(d_w, 32 * EXPERTS)

            @block.gpsimd
            def _(pool):
                def fetch(j, s, r):
                    if not early(j, DR):
                        pool.wait_ge(d_xT_ps, j - DR + 1)
                    pool.wait_ge(d_src, j + 1)
                    pool.sem_inc(d_apart, 1)
                    nc.gpsimd.indirect_dma_start(rows_sb[:, s, :], None, norm_rows,
                                                 bass.IndirectOffsetOnAxis(ap=src_sb[:, s, :], axis=0)).then_inc(d_rows[s], 16)

                def put(j, s, r):
                    pool.wait_ge(d_y, j + 1)
                    pool.wait_ge(d_dst, j + 1)
                    pool.sem_inc(d_apart, 1)
                    nc.gpsimd.indirect_dma_start(pair_rows, bass.IndirectOffsetOnAxis(ap=dst_sb[:, s, :], axis=0),
                                                 y_sb[:, s, :], None).then_inc(d_stored[s], 16)
                rounds = load_rounds(pool)
                pipeline(pool, None, DR, HEAD, [(fetch, 0), (put, DR)], rounds=rounds)
                for s in range(DR):
                    pool.wait_ge(d_stored[s], rounds * 16 + 16 * (HEAD // DR))

            @block.tensor
            def _(pe):
                def transpose(j, s, r):
                    pe.wait_ge(d_rows[s], 16 * (r + 1))
                    if not early(j, 2):
                        pe.wait_ge(d_xT, j - 1)
                    for c in range(KD):
                        last = nc.tensor.transpose(psX[s % 2][:, c * P:(c + 1) * P], rows_sb[:, s, c * P:(c + 1) * P], ident[:, :])
                    last.then_inc(d_xT_ps, 1)

                def up(j, s, r):
                    pe.wait_ge(d_w1, j + 1)
                    pe.wait_ge(d_xT, j + 1)
                    if not early(j, 2):
                        pe.wait_ge(d_hid, j - 1)
                    for f in range(FC):
                        for c in range(KD):
                            last = nc.tensor.matmul(psH[s % 2][:, f * P:(f + 1) * P], w1_sb[:, s % 2, c, f * P:(f + 1) * P],
                                                    xT[:, s % 2, c, :], start=c == 0, stop=c == KD - 1)
                    last.then_inc(d_up, 1)

                def down(j, s, r):
                    e = pe.value_load(tile_expert[0:1, bass.ds(j, 1)], min_val=0, max_val=EXPERTS - 1)
                    pe.wait_ge(d_hid, j + 1)
                    if not early(j, 2):
                        pe.wait_ge(d_y, j - 1)
                    for f in range(FC):
                        w2_f = w_all[:, bass.ds(e, 1), KD * F + f * D:KD * F + (f + 1) * D].rearrange("p o f -> p (o f)")
                        last = nc.tensor.matmul(psY[s % 2][:, 0:D], hid[:, s % 2, f, :], w2_f, start=f == 0, stop=f == FC - 1)
                    last.then_inc(d_down, 1)
                pipeline(pe, None, DR, HEAD, [(transpose, 0), (up, 1), (down, 2)], rounds=load_rounds(pe))

            @block.scalar
            def _(act):
                def copy_w1(j, s, r):
                    e = act.value_load(tile_expert[0:1, bass.ds(j, 1)], min_val=0, max_val=EXPERTS - 1)
                    act.wait_ge(d_w, e * 32 + 32)
                    if not early(j, 2):
                        act.wait_ge(d_up, j - 1)
                    nc.scalar.copy(w1_sb[:, s % 2, :, :].rearrange("p c f -> p (c f)"),
                                   w_all[:, bass.ds(e, 1), 0:KD * F].rearrange("p o f -> p (o f)")).then_inc(d_w1, 1)
                    if not early(j, DR):
                        act.wait_ge(d_y, j - DR + 1)
                    act.dma_start(b2_sb[:, s, :], over(b2[bass.ds(e, 1), :], [P, D])).then_inc(d_b2[s], 16)

                def relu(j, s, r):
                    e = act.value_load(tile_expert[0:1, bass.ds(j, 1)], min_val=0, max_val=EXPERTS - 1)
                    act.wait_ge(d_up, j + 1)
                    if not early(j, 2):
                        act.wait_ge(d_down, j - 1)
                    for f in range(FC):
                        last = nc.scalar.activation(hid[:, s % 2, f, :], psH[s % 2][:, f * P:(f + 1) * P], ACT.Relu,
                                                    bias=b1T[:, bass.ds(e, 1), f:f + 1].rearrange("p o f -> p (o f)"))
                    last.then_inc(d_hid, 1)
                pipeline(act, None, DR, HEAD, [(copy_w1, 0), (relu, 2)], rounds=load_rounds(act))

            @block.vector
            def _(dve):
                def copy_src(j, s, r):
                    if not early(j, DR):
                        dve.wait_ge(d_rows[s], 16 * r)
                    nc.vector.tensor_copy(src_sb[:, s, :], slot_ends[:, bass.ds(j, 1), 0]).then_inc(d_src, 1)

                def copy_dst(j, s, r):
                    if not early(j, DR):
                        dve.wait_ge(d_stored[s], 16 * r)
                    nc.vector.tensor_copy(dst_sb[:, s, :], slot_ends[:, bass.ds(j, 1), 1]).then_inc(d_dst, 1)

                def copy_xT(j, s, r):
                    dve.wait_ge(d_xT_ps, j + 1)
                    if not early(j, 2):
                        dve.wait_ge(d_up, j - 1)
                    nc.vector.tensor_copy(xT[:, s % 2, :, :].rearrange("p c t -> p (c t)"), psX[s % 2][:, 0:D]).then_inc(d_xT, 1)

                def add_b2(j, s, r):
                    dve.wait_ge(d_b2[s], 16 * (r + 1))
                    dve.wait_ge(d_down, j + 1)
                    nc.vector.tensor_tensor(y_sb[:, s, :], psY[s % 2][:, 0:D], b2_sb[:, s, :], ALU.add).then_inc(d_y, 1)

                def add_beta(j, s, r):
                    if isinstance(j, int):
                        lo, hi = NT * j // HEAD, NT * (j + 1) // HEAD
                        nc.vector.tensor_tensor(xs[:, lo:hi, :], xs[:, lo:hi, :],
                                                over(affine[:, D:2 * D].unsqueeze(1), [P, hi - lo, D]), ALU.add)
                pipeline(dve, None, DR, HEAD, [(copy_src, 0), (copy_xT, 3), (copy_dst, 6), (add_b2, 6), (add_beta, 0)], rounds=load_rounds(dve))

        ER = 8
        e_got = [sem(f"e_got{i}") for i in range(ER)]
        e_sum = sem("e_sum"); e_fin = sem("e_fin"); e_var = sem("e_var"); e_root = sem("e_root")
        e_first = sem("e_first"); e_base = sem("e_base"); e_y = sem("e_y"); e_apart = sem("e_apart"); e_out = [sem(f"e_out{i}") for i in range(ER)]
        with ExitStack() as ctx:
            got = sb(ctx, "got", [P, ER, TOP + 1, D])
            y = sb(ctx, "y", [P, ER, D])
            mv = sb(ctx, "mv", [P, ER, 10])
            block = ctx.enter_context(nc.Block())

            @block.scalar
            def _(act):
                def root(t, s, r):
                    act.wait_ge(e_var, t + 1)
                    nc.scalar.activation(mv[:, s, 8:9], mv[:, s, 7:8], ACT.Sqrt, bias=eps_col[:, 0:1]).then_inc(e_root, 1)

                def scale_first(t, s, r):
                    act.wait_ge(e_got[s], 16 * 2 * (r + 1))
                    nc.scalar.activation(got[:, s, 0, :], got[:, s, 0, :], ACT.Copy, scale=share[:, 0, bass.ds(t, 1)]).then_inc(e_first, 1)
                pipeline(act, NT, ER, ER, [(scale_first, 0), (root, 3)])

            @block.gpsimd
            def _(pool):
                def base(t, s, r):
                    pool.wait_ge(e_first, t + 1)
                    nc.gpsimd.tensor_tensor(got[:, s, 0, :], got[:, s, 0, :], got[:, s, TOP, :], ALU.add).then_inc(e_base, 1)
                pipeline(pool, NT, ER, 0, [(base, 0)])

            @block.vector
            def _(dve):
                def add_second(t, s, r):
                    dve.wait_ge(e_base, t + 1)
                    if not early(t, ER):
                        dve.wait_ge(e_out[s], 16 * r)
                    nc.vector.scalar_tensor_tensor(out=y[:, s, :], in0=got[:, s, 1, :], scalar=share[:, 1, bass.ds(t, 1)],
                                                   in1=got[:, s, 0, :], op0=ALU.mult, op1=ALU.add).then_inc(e_sum, 1)

                def tile_stats(t, s, r):
                    dve.wait_ge(e_sum, 2 * t + 1)
                    nc.vector.bn_stats(mv[:, s, 0:6], y[:, s, :]).then_inc(e_sum, 1)

                def variance(t, s, r):
                    dve.wait_ge(e_sum, 2 * t + 2)
                    dve.sem_inc(e_apart, 1)
                    nc.vector.bn_aggr(mv[:, s, 6:8], mv[:, s, 0:6]).then_inc(e_var, 1)

                def invert(t, s, r):
                    dve.wait_ge(e_root, t + 1)
                    nc.vector.reciprocal(mv[:, s, 9:10], mv[:, s, 8:9]).then_inc(e_fin, 1)

                def scale(t, s, r):
                    nc.vector.scalar_tensor_tensor(out=y[:, s, :], in0=y[:, s, :], scalar=mv[:, s, 6:7], in1=affine[:, 0:D],
                                                   op0=ALU.subtract, op1=ALU.mult).then_inc(e_fin, 1)

                def finish(t, s, r):
                    dve.wait_ge(e_fin, 2 * t + 2)
                    nc.vector.scalar_tensor_tensor(out=y[:, s, :], in0=y[:, s, :], scalar=mv[:, s, 9:10],
                                                   in1=xs[:, bass.ds(t, 1), :].rearrange("p o c -> p (o c)"),
                                                   op0=ALU.mult, op1=ALU.add).then_inc(e_y, 1)
                pipeline(dve, NT, ER, ER, [(add_second, 0), (variance, 1), (invert, 2), (scale, 2), (tile_stats, 0), (finish, 2)])

            pairs = pair_rows[0:TOP * NT * P, :].rearrange("(k r) c -> r k c", k=TOP)

            @block.sync
            def _(sp):
                def load(t, s, r):
                    if not early(t, ER):
                        sp.wait_ge(e_sum, 2 * (t - ER) + 1)
                    n = REST if isinstance(t, int) and t == NT - 1 else P
                    sp.dma_start(got[0:n, s, 0:TOP, :], pairs[bass.ds(t * P, n), :, :]).then_inc(e_got[s], 16)
                    sp.dma_start(got[0:n, s, TOP, :], norm_rows[bass.ds(t * P, n), :]).then_inc(e_got[s], 16)

                def store(t, s, r):
                    sp.wait_ge(e_y, t + 1)
                    if isinstance(t, int) and t == NT - 1:
                        sp.dma_start(out[(NT - 1) * P:N, :], y[0:REST, s, :]).then_inc(e_out[s], 16)
                    else:
                        sp.dma_start(out[bass.ds(t * P, P), :], y[:, s, :]).then_inc(e_out[s], 16)
                pipeline(sp, NT, ER, ER, [(load, 0), (store, 7)])
                for s in range(ER):
                    sp.wait_ge(e_out[s], 16 * len(range(s, NT, ER)))


_INS = ['x', 'src', 'dst', 'L0_gnn_W', 'L0_gnn_a_src', 'L0_gnn_a_dst', 'L0_ffn_gate_w', 'L0_ffn_gate_b',
        'L0_ffn_w1', 'L0_ffn_b1', 'L0_ffn_w2', 'L0_ffn_b2', 'L0_ffn_gamma', 'L0_ffn_beta']


def kernel(**inputs):
    import numpy as _np
    import concourse.bacc as _bacc
    from concourse import mybir as _mybir
    from concourse.bass_utils import run_bass_kernel_spmd as _run

    nc = _bacc.Bacc("TRN2", target_bir_lowering=False, num_devices=1)
    arrays, args = {}, []
    for name in _INS:
        a = _np.ascontiguousarray(inputs[name])
        arrays[f"in_{name}_dram"] = a
        args.append(nc.dram_tensor(f"in_{name}_dram", a.shape, _mybir.dt.from_np(a.dtype), kind="ExternalInput").ap())
    out = nc.dram_tensor("out_0_dram", inputs["x"].shape, _mybir.dt.float32, kind="ExternalOutput").ap()
    gnn_moe_kernel(nc, *args, out)
    r = _run(nc, [arrays], core_ids=[0])
    return r.results[0]["out_0_dram"]
```
